# Optimizing a Trainium2 kernel written in Bass

```python
import numpy as np
import jax
import jax.numpy as jnp

def _softmax(x, axis=-1):
    return jax.nn.softmax(x, axis=axis)

def _gelu(x):
    return jax.nn.gelu(x, approximate=True)

def _silu(x):
    return jax.nn.silu(x)

def _sigmoid(x):
    return jax.nn.sigmoid(x)

def _layernorm(x, axis=-1, eps=1e-05):
    m = jnp.mean(x, axis=axis, keepdims=True)
    v = jnp.var(x, axis=axis, keepdims=True)
    return (x - m) / jnp.sqrt(v + eps)

def _scatter_add(tgt, idx, src, axis=0):
    return tgt.at[idx].add(src)

def _segment_sum(src, seg, n):
    return jax.ops.segment_sum(src, seg, n)
kernel_name = 'mk_adaln_d2_jaxref_r8_ec44b1'

def setup_inputs(seed: int=0):
    np.random.seed(seed)
    _w = jnp.asarray

    def _L0_attn_setup():
        import jax, jax.numpy as jnp
        import numpy as np
        B, T, C = (2, 256, 128)
        N_HEAD = 16
        WINDOW = 64
        ROPE_BASE = 10000.0

        def _apply_rotary(x, cos, sin):
            d = x.shape[-1] // 2
            x1, x2 = (x[..., :d], x[..., d:])
            return jnp.concatenate([x1 * cos + x2 * sin, -x1 * sin + x2 * cos], axis=-1)
        key = jax.random.key(seed)
        k1, k2, k3 = jax.random.split(key, 3)
        x = jax.random.normal(k1, (B, T, C), dtype=jnp.float32)
        w_attn = jax.random.normal(k2, (3 * C, C), dtype=jnp.float32) * 0.02
        w_proj = jax.random.normal(k3, (C, C), dtype=jnp.float32) * 0.02
        return {'x': x, 'w_attn': w_attn, 'w_proj': w_proj}
    _L0_attn_in = _L0_attn_setup()

    def _L0_ffn_setup():
        import jax, jax.numpy as jnp
        import numpy as np
        B, S, D = (2, 256, 128)
        M = 256
        E = 8
        TOP_K = 2
        key = jax.random.key(seed)
        ks = jax.random.split(key, 5)
        std = 0.02
        return {'residual': jax.random.normal(ks[0], (B, S, D), jnp.float32), 'W_router': jax.random.normal(ks[1], (D, E), jnp.float32) * std, 'W_gate': jax.random.normal(ks[2], (E, D, M), jnp.float32) * std, 'b_gate': jnp.zeros((E, M), jnp.float32), 'W_up': jax.random.normal(ks[3], (E, D, M), jnp.float32) * std, 'b_up': jnp.zeros((E, M), jnp.float32), 'W_out': jax.random.normal(ks[4], (E, M, D), jnp.float32) * std, 'b_out': jnp.zeros((E, D), jnp.float32)}
    _L0_ffn_in = _L0_ffn_setup()
    _L0_c = _w((lambda *s: np.random.randn(*s).astype(np.float32) * 0.05)(16, 128))
    _L0_wmod = _w((lambda *s: np.random.randn(*s).astype(np.float32) * 0.05)(128, 6 * 128) * 128 ** (-0.5))

    def _L1_attn_setup():
        import jax, jax.numpy as jnp
        import numpy as np
        T, B, E, H = (256, 2, 128, 16)
        D = E // H
        MAX_REL = 16

        def _rel_idx(lq, lk):
            d = jnp.arange(lk)[None, :] - jnp.arange(lq)[:, None]
            return jnp.clip(d, -MAX_REL, MAX_REL) + MAX_REL
        key = jax.random.key(seed)
        ks = jax.random.split(key, 11)
        s = 1.0 / np.sqrt(E)
        inp = {'query': jax.random.normal(ks[0], (T, B, E), dtype=jnp.float32), 'Wq': jax.random.normal(ks[1], (E, E), dtype=jnp.float32) * s, 'bq': jnp.zeros((E,), dtype=jnp.float32), 'Wk': jax.random.normal(ks[2], (E, E), dtype=jnp.float32) * s, 'bk': jnp.zeros((E,), dtype=jnp.float32), 'Wv': jax.random.normal(ks[3], (E, E), dtype=jnp.float32) * s, 'bv': jnp.zeros((E,), dtype=jnp.float32), 'Wo': jax.random.normal(ks[4], (E, E), dtype=jnp.float32) * s, 'bo': jnp.zeros((E,), dtype=jnp.float32), 'rk_table': jax.random.normal(ks[5], (2 * MAX_REL + 1, D), dtype=jnp.float32) * 0.05, 'rv_table': jax.random.normal(ks[6], (2 * MAX_REL + 1, D), dtype=jnp.float32) * 0.05}
        return inp
    _L1_attn_in = _L1_attn_setup()

    def _L1_ffn_setup():
        import jax, jax.numpy as jnp
        import numpy as np
        E = 8
        D = 128
        DO = 128
        R = 64
        H = 32
        B, T = (8, 256)
        key = jax.random.key(seed)
        ks = jax.random.split(key, 12)
        s = lambda k, shape, fan: jax.random.normal(k, shape, jnp.float32) / np.sqrt(fan)
        return {'x': jax.random.normal(ks[0], (B, T, D), jnp.float32), 'W_base': s(ks[1], (D, DO), D), 'b_base': jnp.zeros((DO,), jnp.float32), 'Wd1': s(ks[2], (E, D, H), D), 'bd1': jnp.zeros((E, H), jnp.float32), 'Wd2': s(ks[3], (E, H, D), H), 'bd2': jnp.zeros((E, D), jnp.float32), 'Wa_down': s(ks[4], (E, D, R), D), 'ba_down': jnp.zeros((E, R), jnp.float32), 'Wa_up': s(ks[5], (E, R, DO), R), 'ba_up': jnp.zeros((E, DO), jnp.float32)}
    _L1_ffn_in = _L1_ffn_setup()
    _L1_c = _w((lambda *s: np.random.randn(*s).astype(np.float32) * 0.05)(16, 128))
    _L1_wmod = _w((lambda *s: np.random.randn(*s).astype(np.float32) * 0.05)(128, 6 * 128) * 128 ** (-0.5))
    _d = {'L0_attn_x': _L0_attn_in['x'], 'L0_attn_w_attn': _L0_attn_in['w_attn'], 'L0_attn_w_proj': _L0_attn_in['w_proj'], 'L0_ffn_W_router': _L0_ffn_in['W_router'], 'L0_ffn_W_gate': _L0_ffn_in['W_gate'], 'L0_ffn_b_gate': _L0_ffn_in['b_gate'], 'L0_ffn_W_up': _L0_ffn_in['W_up'], 'L0_ffn_b_up': _L0_ffn_in['b_up'], 'L0_ffn_W_out': _L0_ffn_in['W_out'], 'L0_ffn_b_out': _L0_ffn_in['b_out'], 'L0_c': _L0_c, 'L0_wmod': _L0_wmod, 'L1_attn_Wq': _L1_attn_in['Wq'], 'L1_attn_bq': _L1_attn_in['bq'], 'L1_attn_Wk': _L1_attn_in['Wk'], 'L1_attn_bk': _L1_attn_in['bk'], 'L1_attn_Wv': _L1_attn_in['Wv'], 'L1_attn_bv': _L1_attn_in['bv'], 'L1_attn_Wo': _L1_attn_in['Wo'], 'L1_attn_bo': _L1_attn_in['bo'], 'L1_attn_rk_table': _L1_attn_in['rk_table'], 'L1_attn_rv_table': _L1_attn_in['rv_table'], 'L1_ffn_W_base': _L1_ffn_in['W_base'], 'L1_ffn_b_base': _L1_ffn_in['b_base'], 'L1_ffn_Wd1': _L1_ffn_in['Wd1'], 'L1_ffn_bd1': _L1_ffn_in['bd1'], 'L1_ffn_Wd2': _L1_ffn_in['Wd2'], 'L1_ffn_bd2': _L1_ffn_in['bd2'], 'L1_ffn_Wa_down': _L1_ffn_in['Wa_down'], 'L1_ffn_ba_down': _L1_ffn_in['ba_down'], 'L1_ffn_Wa_up': _L1_ffn_in['Wa_up'], 'L1_ffn_ba_up': _L1_ffn_in['ba_up'], 'L1_c': _L1_c, 'L1_wmod': _L1_wmod}
    _x0 = _d['L0_attn_x']
    _d['L0_attn_x'] = jax.random.normal(jax.random.fold_in(jax.random.key(seed), 1), (16, 256, 128), dtype=_x0.dtype)
    del _x0
    return _d

def reference(L0_attn_x, L0_attn_w_attn, L0_attn_w_proj, L0_ffn_W_router, L0_ffn_W_gate, L0_ffn_b_gate, L0_ffn_W_up, L0_ffn_b_up, L0_ffn_W_out, L0_ffn_b_out, L0_c, L0_wmod, L1_attn_Wq, L1_attn_bq, L1_attn_Wk, L1_attn_bk, L1_attn_Wv, L1_attn_bv, L1_attn_Wo, L1_attn_bo, L1_attn_rk_table, L1_attn_rv_table, L1_ffn_W_base, L1_ffn_b_base, L1_ffn_Wd1, L1_ffn_bd1, L1_ffn_Wd2, L1_ffn_bd2, L1_ffn_Wa_down, L1_ffn_ba_down, L1_ffn_Wa_up, L1_ffn_ba_up, L1_c, L1_wmod):

    def _L0_attn_ref(x, w_attn, w_proj):
        import jax, jax.numpy as jnp
        import numpy as np
        B, T, C = (2, 256, 128)
        N_HEAD = 16
        WINDOW = 64
        ROPE_BASE = 10000.0

        def _apply_rotary(x, cos, sin):
            d = x.shape[-1] // 2
            x1, x2 = (x[..., :d], x[..., d:])
            return jnp.concatenate([x1 * cos + x2 * sin, -x1 * sin + x2 * cos], axis=-1)
        Bb, Tt, Cc = x.shape
        H = N_HEAD
        D = Cc // H
        qkv = x @ w_attn.T
        q, k, v = jnp.split(qkv, 3, axis=2)
        q = q.reshape(Bb, Tt, H, D)
        k = k.reshape(Bb, Tt, H, D)
        v = v.reshape(Bb, Tt, H, D)
        inv_freq = 1.0 / ROPE_BASE ** (jnp.arange(0, D, 2, dtype=jnp.float32) / D)
        freqs = jnp.outer(jnp.arange(Tt, dtype=jnp.float32), inv_freq)
        cos = jnp.cos(freqs)[None, :, None, :]
        sin = jnp.sin(freqs)[None, :, None, :]
        q = _apply_rotary(q, cos, sin)
        k = _apply_rotary(k, cos, sin)
        pos = jnp.arange(Tt)
        diff = pos[:, None] - pos[None, :]
        mask = (diff >= 0) & (diff <= WINDOW)
        scale = 1.0 / jnp.sqrt(jnp.asarray(D, dtype=q.dtype))
        scores = jnp.einsum('bqhd,bkhd->bhqk', q, k) * scale
        scores = jnp.where(mask[None, None, :, :], scores, jnp.asarray(-1e+30, scores.dtype))
        attn = jax.nn.softmax(scores, axis=-1)
        y = jnp.einsum('bhqk,bkhd->bqhd', attn, v).reshape(Bb, Tt, Cc)
        return y @ w_proj.T

    def _L0_ffn_ref(residual, W_router, W_gate, b_gate, W_up, b_up, W_out, b_out):
        import jax, jax.numpy as jnp
        import numpy as np
        B, S, D = (2, 256, 128)
        M = 256
        E = 8
        TOP_K = 2
        router_logits = jnp.einsum('bsd,de->bse', residual, W_router)
        router_probs = jax.nn.softmax(router_logits, axis=-1)
        top_k_probs, top_k_idx = jax.lax.top_k(router_probs, TOP_K)
        top_k_probs = top_k_probs / (jnp.sum(top_k_probs, -1, keepdims=True) + 1e-08)
        one_hot = jax.nn.one_hot(top_k_idx, E, dtype=residual.dtype)
        expert_weights = jnp.einsum('bsk,bske->bse', top_k_probs, one_hot)
        gate = jax.nn.silu(jnp.einsum('bsd,edm->ebsm', residual, W_gate) + b_gate[:, None, None, :])
        up = jnp.einsum('bsd,edm->ebsm', residual, W_up) + b_up[:, None, None, :]
        hidden = gate * up
        expert_out = jnp.einsum('ebsm,emd->ebsd', hidden, W_out) + b_out[:, None, None, :]
        output = jnp.einsum('bse,ebsd->bsd', expert_weights, expert_out)
        return output

    def _L1_attn_ref(query, Wq, bq, Wk, bk, Wv, bv, Wo, bo, rk_table, rv_table):
        import jax, jax.numpy as jnp
        import numpy as np
        T, B, E, H = (256, 2, 128, 16)
        D = E // H
        MAX_REL = 16

        def _rel_idx(lq, lk):
            d = jnp.arange(lk)[None, :] - jnp.arange(lq)[:, None]
            return jnp.clip(d, -MAX_REL, MAX_REL) + MAX_REL
        t, b, e = query.shape
        scale = D ** (-0.5)
        q = (query @ Wq.T + bq) * scale
        k = query @ Wk.T + bk
        v = query @ Wv.T + bv
        q = q.reshape(t, b * H, D).transpose(1, 0, 2)
        k = k.reshape(t, b * H, D).transpose(1, 0, 2)
        v = v.reshape(t, b * H, D).transpose(1, 0, 2)
        scores = jnp.einsum('ntd,nsd->nts', q, k)
        rk = rk_table[_rel_idx(t, t)]
        scores = scores + jnp.einsum('ntd,tsd->nts', q, rk)
        probs = jax.nn.softmax(scores, axis=-1)
        rv = rv_table[_rel_idx(t, t)]
        attn = jnp.einsum('nts,nsd->ntd', probs, v) + jnp.einsum('nts,tsd->ntd', probs, rv)
        attn = attn.transpose(1, 0, 2).reshape(t, b, e)
        return attn @ Wo.T + bo

    def _L1_ffn_ref(x, W_base, b_base, Wd1, bd1, Wd2, bd2, Wa_down, ba_down, Wa_up, ba_up):
        import jax, jax.numpy as jnp
        import numpy as np
        E = 8
        D = 128
        DO = 128
        R = 64
        H = 32
        B, T = (8, 256)
        base = jnp.einsum('btd,do->bto', x, W_base) + b_base
        h = jax.nn.relu(jnp.einsum('btd,edh->ebth', x, Wd1) + bd1[:, None, None, :])
        recon = jnp.einsum('ebth,ehd->ebtd', h, Wd2) + bd2[:, None, None, :]
        losses = jnp.mean((recon - x[None]) ** 2, axis=(2, 3))
        idx = jnp.argmin(losses, axis=0)
        a = jax.nn.relu(jnp.einsum('btd,bdr->btr', x, Wa_down[idx]) + ba_down[idx][:, None, :])
        adapter_out = jnp.einsum('btr,bro->bto', a, Wa_up[idx]) + ba_up[idx][:, None, :]
        return base + adapter_out
    x = L0_attn_x
    mod = (_silu(L0_c) @ L0_wmod).reshape(L0_c.shape[0], 6, 1, -1)
    sa, ca, ga, sb, cb, gb = (mod[:, 0], mod[:, 1], mod[:, 2], mod[:, 3], mod[:, 4], mod[:, 5])
    ga = (2 * (ga >= 0) - 1) * jnp.maximum(jnp.abs(ga), 0.25)
    gb = (2 * (gb >= 0) - 1) * jnp.maximum(jnp.abs(gb), 0.25)
    h = _layernorm(x, axis=-1) * (1 + ca) + sa
    x = x + ga * _L0_attn_ref(h, L0_attn_w_attn, L0_attn_w_proj)
    h = _layernorm(x, axis=-1) * (1 + cb) + sb
    x = x + gb * _L0_ffn_ref(h, L0_ffn_W_router, L0_ffn_W_gate, L0_ffn_b_gate, L0_ffn_W_up, L0_ffn_b_up, L0_ffn_W_out, L0_ffn_b_out)
    mod = (_silu(L1_c) @ L1_wmod).reshape(L1_c.shape[0], 6, 1, -1)
    sa, ca, ga, sb, cb, gb = (mod[:, 0], mod[:, 1], mod[:, 2], mod[:, 3], mod[:, 4], mod[:, 5])
    ga = (2 * (ga >= 0) - 1) * jnp.maximum(jnp.abs(ga), 0.25)
    gb = (2 * (gb >= 0) - 1) * jnp.maximum(jnp.abs(gb), 0.25)
    h = _layernorm(x, axis=-1) * (1 + ca) + sa
    x = x + ga * _L1_attn_ref(h, L1_attn_Wq, L1_attn_bq, L1_attn_Wk, L1_attn_bk, L1_attn_Wv, L1_attn_bv, L1_attn_Wo, L1_attn_bo, L1_attn_rk_table, L1_attn_rv_table)
    h = _layernorm(x, axis=-1) * (1 + cb) + sb
    x = x + gb * _L1_ffn_ref(h, L1_ffn_W_base, L1_ffn_b_base, L1_ffn_Wd1, L1_ffn_bd1, L1_ffn_Wd2, L1_ffn_bd2, L1_ffn_Wa_down, L1_ffn_ba_down, L1_ffn_Wa_up, L1_ffn_ba_up)
    return x

_drawn_inputs = setup_inputs


def setup_inputs(seed=0):
    import zlib

    import numpy as np

    out = dict(_drawn_inputs(seed))
    spreads = {'L0_ffn_b_gate': (0.0, 0.8),
     'L0_ffn_b_up': (0.0, 0.8),
     'L0_ffn_b_out': (0.0, 0.725),
     'L1_attn_bq': (0.0, 0.8),
     'L1_attn_bk': (0.0, 2.0),
     'L1_attn_bv': (0.0, 0.1),
     'L1_attn_bo': (0.0, 0.567),
     'L1_ffn_b_base': (0.0, 0.352),
     'L1_ffn_bd1': (0.0, 0.1),
     'L1_ffn_bd2': (0.0, 0.1),
     'L1_ffn_ba_down': (0.0, 0.436),
     'L1_ffn_ba_up': (0.0, 0.336)}
    factors = {'L0_attn_w_attn': 8.0,
     'L0_attn_w_proj': 8.0,
     'L0_ffn_W_router': 3.567,
     'L0_ffn_W_gate': 8.0,
     'L0_ffn_W_up': 8.0,
     'L0_ffn_W_out': 8.0,
     'L1_attn_rk_table': 8.0,
     'L1_attn_rv_table': 8.0}
    for name, (base, spread) in spreads.items():
        noise = np.random.default_rng([zlib.crc32(name.encode()), seed]).standard_normal(out[name].shape)
        drawn = base * np.exp(spread * noise) if base else spread * noise
        out[name] = jnp.asarray(drawn.astype(out[name].dtype))
    for name, factor in factors.items():
        out[name] = (out[name] * factor).astype(out[name].dtype)
    return out
```

```python
from contextlib import ExitStack

import numpy as np

import concourse.bass as bass
from concourse import mybir

F32 = mybir.dt.float32
BF16 = mybir.dt.bfloat16
ALU = mybir.AluOpType
ACT = mybir.ActivationFunctionType
AX = mybir.AxisListType

NB, T, C = 16, 256, 128
P = 128
NHALF = T // P
H, D = 16, 8
WINDOW = 64
QB = 32
NQB = T // QB
WIN = WINDOW + QB
HG = 4
HPG = H // HG
E0, M = 8, 256
MT = M // P
MAXREL = 16
E1, HD1, R = 8, 32, 64
EPS = 1e-5
NEG = -1e30


def shape_constants():
    f = np.float32
    half = D // 2
    inv = (1.0 / (f(10000.0) ** (np.arange(0, D, 2, dtype=f) / f(D)))).astype(f)
    ang = np.outer(np.arange(T, dtype=f), inv).astype(f)
    cos, sin = np.cos(ang).astype(f), np.sin(ang).astype(f)
    ch = np.arange(C)
    rc = cos[:, ch % half].T
    rs = sin[:, ch % half].T * np.where(ch % D < half, 1, -1)[:, None]
    scale = 1.0 / np.sqrt(f(D))
    rope = np.stack([rc * scale, rc, rs * scale, rs], 1).astype(f)
    masks = np.zeros((P, 2 * HG), f)
    masks[ch, (ch // D) % HPG] = 1
    masks[ch, HG + ch // (C // HG)] = 1
    key, q = np.arange(P)[:, None], np.arange(QB)[None, :]
    win = np.zeros((P, 3, HPG, QB), f)
    for v, first in enumerate((WINDOW, WINDOW - QB, 0)):
        ok = (key >= q) & (key <= q + WINDOW) & (key >= first)
        win[:, v] = np.where(ok | (key >= WIN), 0.0, NEG)[:, None, :]
    eye = np.eye(P, dtype=f)
    pick = np.zeros((P, HG, WIN), f)
    pick[np.arange(WIN), :, np.arange(WIN)] = 1
    return {
        "const_rope": rope, "const_masks": masks, "const_window": win.reshape(P, -1),
        "const_eye": eye, "const_pick": pick.reshape(P, -1),
        "const_order": np.tile((E0 - np.arange(E0, dtype=f))[None], (P, 1)),
    }


def build(nc, a, out):
    with ExitStack() as ctx:
        def sb(name, shape, dt=F32, until=ctx):
            return until.enter_context(nc.sbuf_tensor(name, shape, dt))

        def sem(name):
            return ctx.enter_context(nc.semaphore(name))

        x = sb("x", [P, NB, NHALF, C])
        eye = sb("eye", [P, P])
        rope = sb("rope", [P, 4, T])
        masks = sb("masks", [P, 2 * HG])
        window_f = sb("window_f", [P, 3 * P])
        window_bf = sb("window_bf", [P, 3, P], BF16)
        pick_f = sb("pick_f", [P, HG * WIN])
        pick_bf = sb("pick_bf", [P, HG * WIN], BF16)
        order = sb("order", [P, E0])
        w_qkv0 = sb("w_qkv0", [P, 5, C])
        w_proj0 = sb("w_proj0", [P, C])
        c_t = sb("c_t", [P, 2, NB])
        silu_c = sb("silu_c", [P, 2, NB])
        w_mod = sb("w_mod", [P, 2, 6, C])
        mod = sb("mod", [P, 2, 4, NB])
        gates = sb("gates", [P, NB, 2, C])
        gate_sign = sb("gate_sign", [P, 512])
        gate_size = sb("gate_size", [P, 2, 512])
        stats = sb("stats", [P, NB, NHALF, 6])
        ln_sum = sb("ln_sum", [P, NB, NHALF])
        ln_dif = sb("ln_dif", [P, NB, NHALF])
        ln_dev = sb("ln_dev", [P, NB, NHALF])
        var_eps = sb("var_eps", [P, NB, NHALF])
        mean = sb("mean", [P, NB, NHALF])
        minus_half = sb("minus_half", [P, NB, NHALF])
        rstd = sb("rstd", [P, NB, NHALF])
        xn = sb("xn", [P, NHALF, C])

        po = ctx.enter_context(nc.psum_tensor("po", [P, 1024], F32))
        ps = [ctx.enter_context(nc.psum_tensor(f"ps{i}", [P, 512], F32)) for i in range(6)]

        ones_row = [P, 1]

        x_in = sem("x_in")
        small_in = sem("small_in")
        l0_in = sem("l0_in")
        all_in = sem("all_in")
        silu_done = sem("silu_done")
        mod_psum = sem("mod_psum")
        mod_done = sem("mod_done")
        gate_psum = sem("gate_psum")
        gate_steps = sem("gate_steps")
        gate_abs = sem("gate_abs")
        const_done = sem("const_done")
        st_done = sem("st_done")
        ln_steps = sem("ln_steps")
        ln_var = sem("ln_var")
        ln_rstd = sem("ln_rstd")

        def token_variances(dve, n):
            nc.vector.tensor_tensor(ln_sum[:], stats[:, :, :, 1], stats[:, :, :, 4], ALU.add)
            nc.vector.tensor_tensor(ln_dif[:], stats[:, :, :, 1], stats[:, :, :, 4], ALU.subtract)
            nc.vector.tensor_tensor(ln_dev[:], stats[:, :, :, 2], stats[:, :, :, 5], ALU.add).then_inc(ln_steps, 1)
            dve.wait_ge(ln_steps, 3 * n + 1)
            nc.vector.tensor_scalar(mean[:], ln_sum[:], 0.5, None, ALU.mult)
            nc.vector.tensor_tensor(ln_dif[:], ln_dif[:], ln_dif[:], ALU.mult).then_inc(ln_steps, 1)
            dve.wait_ge(ln_steps, 3 * n + 2)
            nc.vector.tensor_scalar(ln_dif[:], ln_dif[:], 0.25, EPS, ALU.mult, ALU.add).then_inc(ln_steps, 1)
            dve.wait_ge(ln_steps, 3 * n + 3)
            nc.vector.scalar_tensor_tensor(out=var_eps[:], in0=ln_dev[:], scalar=1.0 / C, in1=ln_dif[:], op0=ALU.mult,
                                           op1=ALU.add).then_inc(ln_var, 1)

        def token_scales(pool, n):
            pool.wait_ge(ln_var, n + 1)
            nc.gpsimd.tensor_tensor(rstd[:], var_eps[:], minus_half[:], ALU.pow).then_inc(ln_rstd, 1)

        w_gate = sb("w_gate", [P, E0, M])
        w_up = sb("w_up", [P, E0, M])
        w_out = sb("w_out", [P, E0, MT, C])
        b_gu = sb("b_gu", [P, 2, E0 * MT])
        b_out = sb("b_out", [P, 4, C])
        w_router = sb("w_router", [P, E0])

        l1 = {}
        for name, shape in (("w_qkv1", [P, 3 * C]), ("b_qkv1", [P, 3 * C]), ("b_q1", [P, 1]), ("rk", [P, H, 2 * MAXREL + 1]),
                            ("rv", [P, 16, 8, D]), ("w_o1", [P, C]), ("b_o1", [P, C]),
                            ("w_base", [P, C]), ("b_base", [P, C]), ("w_d1", [P, 2 * P]), ("b_d1", [P, 2]),
                            ("w_d2", [P, E1, C]), ("b_d2", [P, E1]), ("w_ad", [P, R, E1]), ("b_ad", [R, E1]),
                            ("w_au", [P, C, E1])):
            l1[name] = sb(name, shape)

        def gate_program(dve, layer):
            for pair in range(NB // 2):
                n = layer * (NB // 2) + pair
                src = ps[pair % 2]
                dve.wait_ge(gate_abs, n + 1)
                nc.vector.tensor_scalar(gate_sign[:], src[:], 0.0, 0.5, ALU.is_ge, ALU.subtract).then_inc(gate_steps, 1)
                dve.wait_ge(gate_steps, 2 * n + 1)
                nc.vector.scalar_tensor_tensor(
                    out=gates[:, 2 * pair:2 * pair + 2, :, :].rearrange("p b g c -> p (b g c)"), in0=gate_size[:, pair % 2, :],
                    scalar=0.5, in1=gate_sign[:], op0=ALU.max, op1=ALU.mult).then_inc(gate_steps, 1)
                dve.wait_ge(gate_steps, 2 * n + 2)

        def gate_sizes(act, layer):
            for pair in range(NB // 2):
                n = layer * (NB // 2) + pair
                act.wait_ge(gate_psum, n + 1)
                if pair >= 2:
                    act.wait_ge(gate_steps, 2 * n - 2)
                nc.scalar.activation(gate_size[:, pair % 2, :], ps[pair % 2][:], ACT.Abs, scale=2.0).then_inc(gate_abs, 1)

        def gate_matmuls(pe, layer):
            for pair in range(NB // 2):
                n = layer * (NB // 2) + pair
                if pair >= 2:
                    pe.wait_ge(gate_steps, 2 * n - 2)
                for j in range(2):
                    b = 2 * pair + j
                    last = nc.tensor.matmul(ps[pair % 2][:, j * 2 * C:(j + 1) * 2 * C],
                                            silu_c[:, layer, b:b + 1].to_broadcast([P, P]),
                                            w_mod[:, layer, 4:6, :].rearrange("p j c -> p (j c)"),
                                            start=True, stop=True)
                last.then_inc(gate_psum, 1)

        with nc.Block() as block:
            @block.sync
            def _(sp):
                for name, t in (("cT", c_t), ("wmod", w_mod)):
                    sp.dma_start(t[:], a[name]).then_inc(small_in, 16)
                xv = a["x"].rearrange("b (h p) c -> p b h c", p=P)
                for q in range(4):
                    sp.dma_start(x[:, 4 * q:4 * q + 4], xv[:, 4 * q:4 * q + 4]).then_inc(x_in, 16)
                sp.wait_ge(x_in, 64)
                sp.wait_ge(l0_in, 16 * 8)

            @block.gpsimd
            def _(pool):
                for name, t in (("const_eye", eye), ("const_rope", rope), ("const_masks", masks),
                                ("const_window", window_f), ("const_pick", pick_f), ("const_order", order),
                                ("wqkv0", w_qkv0), ("wproj0", w_proj0)):
                    pool.dma_start(t[:], a[name]).then_inc(l0_in, 16)
                token_scales(pool, 0)

            @block.scalar
            def _(act):
                act.wait_ge(small_in, 32)
                nc.scalar.activation(silu_c[:], c_t[:], ACT.Silu).then_inc(silu_done, 1)
                gate_sizes(act, 0)
                for name, t in (("wgate", w_gate), ("wup", w_up), ("wout", w_out), ("bgu", b_gu), ("bout", b_out),
                                ("wrouter", w_router)) + tuple(l1.items()):
                    act.dma_start(t[:], a[name]).then_inc(all_in, 16)

            @block.tensor
            def _(pe):
                pe.wait_ge(silu_done, 1)
                for layer in range(2):
                    for j in range(4):
                        last = nc.tensor.matmul(ps[2][:, (layer * 4 + j) * NB:(layer * 4 + j + 1) * NB],
                                                w_mod[:, layer, j, :], silu_c[:, layer, :], start=True, stop=True)
                last.then_inc(mod_psum, 1)
                gate_matmuls(pe, 0)

            @block.vector
            def _(dve):
                nc.vector.memset(minus_half[:], -0.5)
                dve.wait_ge(mod_psum, 1)
                pm = ps[2][:, 0:8 * NB].rearrange("p (l j b) -> p l j b", l=2, j=4)
                nc.vector.tensor_copy(mod[:, :, 0, :], pm[:, :, 0, :])
                nc.vector.tensor_scalar(mod[:, :, 1, :], pm[:, :, 1, :], 1.0, None, ALU.add)
                nc.vector.tensor_copy(mod[:, :, 2, :], pm[:, :, 2, :])
                nc.vector.tensor_scalar(mod[:, :, 3, :], pm[:, :, 3, :], 1.0, None, ALU.add).then_inc(mod_done, 1)
                gate_program(dve, 0)
                dve.wait_ge(l0_in, 16 * 8)
                nc.vector.tensor_copy(window_bf[:].rearrange("p v q -> p (v q)"), window_f[:])
                nc.vector.tensor_copy(pick_bf[:], pick_f[:]).then_inc(const_done, 1)
                dve.wait_ge(x_in, 64)
                with dve.Fori(0, NB) as b:
                    for h in range(NHALF):
                        last = nc.vector.bn_stats(stats[:, b, h, :], x[:, b, h, :])
                    last.then_inc(st_done, 1)
                dve.wait_ge(st_done, NB)
                token_variances(dve, 0)

        phase = ExitStack()
        h_t = sb("h_t", [P, WINDOW + T], until=phase)
        rope_c = sb("rope_c", [P, 512], until=phase)
        rope_s = sb("rope_s", [P, 512], until=phase)
        qk = sb("qk", [P, 512], until=phase)
        q_m = sb("q_m", [P, NQB, HPG, QB], until=phase)
        k_m = sb("k_m", [P, HG, WINDOW + T], until=phase)
        v_win = sb("v_win", [WIN, NQB, C], until=phase)
        negmax = sb("negmax", [P, NQB, HG], until=phase)
        esum = sb("esum", [P, NQB, HG], until=phase)
        rsum = sb("rsum", [P, NQB, HG], until=phase)
        p_exp = sb("p_exp", [P, 2, HG, WIN], until=phase)
        p_nrm = sb("p_nrm", [P, 2, HG, WIN], until=phase)
        p_t = sb("p_t", [WIN, 2, HG * P], until=phase)
        y_t = sb("y_t", [P, T], until=phase)
        upd = sb("upd", [P, NHALF, C], until=phase)

        s0 = {n: sem("a0_" + n) for n in (
            "pads", "xn", "x_t", "h_t", "qk_psum", "v_psum", "v_sb", "rope_mul", "rope", "masked", "scores", "y_part", "negmax",
            "exp", "rsum", "p_nrm", "p_t_psum", "p_t", "pv", "y", "proj", "upd", "x1", "st")}

        with nc.Block() as block:
            @block.tensor
            def _(pe):
                pe.wait_ge(s0["pads"], 1)
                with pe.Fori(0, NB) as b:
                    pe.wait_ge(s0["xn"], b + 1)
                    for h in range(NHALF):
                        last = nc.tensor.transpose(ps[0][:, h * P:(h + 1) * P], xn[:, h, :], eye[:])
                    last.then_inc(s0["x_t"], 1)
                    pe.wait_ge(s0["h_t"], b + 1)
                    for j in range(4):
                        last = nc.tensor.matmul(ps[j // 2][:, (j % 2) * T:(j % 2 + 1) * T], w_qkv0[:, j, :],
                                                h_t[:, WINDOW:], start=True, stop=True)
                    last.then_inc(s0["qk_psum"], 1)
                    for qb in range(NQB):
                        last = nc.tensor.matmul(po[0:WIN, qb * P:(qb + 1) * P], h_t[:, qb * QB:qb * QB + WIN],
                                                w_qkv0[:, 4, :], start=True, stop=True)
                    last.then_inc(s0["v_psum"], 1)

                    def scores(qb):
                        if qb >= 2:
                            pe.wait_ge(s0["exp"], NQB * b + qb - 1)
                        pst = ps[2 + qb % 2][:, 0:HG * WIN]
                        nc.tensor.matmul(pst, window_bf[:, min(qb, 2), :], pick_bf[:], start=True, stop=False)
                        nc.tensor.matmul(pst, q_m[:, qb, :, :].rearrange("p h q -> p (h q)"),
                                         k_m[:, :, qb * QB:qb * QB + WIN], start=False, stop=True).then_inc(s0["scores"], 1)

                    def attend(qb):
                        pe.wait_ge(s0["p_t"], NQB * b + qb + 1)
                        for g in range(HG):
                            last = nc.tensor.matmul(po[g * 32:(g + 1) * 32, qb * P:(qb + 1) * P],
                                                    v_win[:, qb, g * 32:(g + 1) * 32],
                                                    p_t[:, qb % 2, g * P:(g + 1) * P], start=True, stop=True)
                        last.then_inc(s0["pv"], 1)

                    pe.wait_ge(s0["masked"], b + 1)
                    scores(0)
                    scores(1)
                    pe.wait_ge(s0["v_sb"], 2 * b + 2)
                    for qb in range(NQB):
                        pe.wait_ge(s0["p_nrm"], NQB * b + qb + 1)
                        for g in range(HG):
                            last = nc.tensor.transpose(ps[4 + qb % 2][0:WIN, g * P:(g + 1) * P], p_nrm[:, qb % 2, g, :],
                                                       eye[:])
                        last.then_inc(s0["p_t_psum"], 1)
                        if qb + 2 < NQB:
                            scores(qb + 2)
                        if qb >= 1:
                            attend(qb - 1)
                    attend(NQB - 1)
                    pe.wait_ge(s0["y"], b + 1)
                    for h in range(NHALF):
                        last = nc.tensor.matmul(ps[1][:, h * P:(h + 1) * P], y_t[:, h * P:(h + 1) * P], w_proj0[:],
                                                start=True, stop=True)
                    last.then_inc(s0["proj"], 1)

            @block.scalar
            def _(act):
                with act.Fori(0, NB) as b:
                    act.wait_ge(s0["x_t"], b + 1)
                    nc.scalar.activation(h_t[:, WINDOW:], ps[0][:, 0:T], ACT.Identity, scale=mod[:, 0, 1, bass.ds(b, 1)],
                                         bias=mod[:, 0, 0, bass.ds(b, 1)]).then_inc(s0["h_t"], 1)
                    act.wait_ge(s0["v_psum"], b + 1)
                    for i in range(2):
                        nc.scalar.copy(v_win[:, 4 * i:4 * i + 4, :].rearrange("p q c -> p (q c)"),
                                       po[0:WIN, 512 * i:512 * (i + 1)]).then_inc(s0["v_sb"], 1)
                    for qb in range(NQB):
                        act.wait_ge(s0["negmax"], NQB * b + qb + 1)
                        if qb >= 2:
                            act.wait_ge(s0["p_nrm"], NQB * b + qb - 1)
                        for g in range(HG):
                            last = nc.scalar.activation(p_exp[:, qb % 2, g, :], ps[2 + qb % 2][:, g * WIN:(g + 1) * WIN],
                                                        ACT.Exp, bias=negmax[:, qb, g:g + 1],
                                                        accum_out=esum[:, qb, g:g + 1])
                        last.then_inc(s0["exp"], 1)

            @block.gpsimd
            def _(pool):
                with pool.Fori(0, NB) as b:
                    for qb in range(NQB):
                        pool.wait_ge(s0["rsum"], NQB * b + qb + 1)
                        if qb >= 2:
                            pool.wait_ge(s0["p_t_psum"], NQB * b + qb - 1)
                        nc.gpsimd.tensor_tensor(p_nrm[:, qb % 2], p_exp[:, qb % 2],
                                                rsum[:, qb, :].unsqueeze(2).to_broadcast([P, HG, WIN]),
                                                ALU.mult).then_inc(s0["p_nrm"], 1)
                token_scales(pool, 1)

            @block.vector
            def _(dve):
                nc.vector.memset(h_t[:, 0:WINDOW], 0.0)
                nc.vector.memset(k_m[:, :, 0:WINDOW], 0.0).then_inc(s0["pads"], 1)
                with dve.Fori(0, NB) as b:
                    for h in range(NHALF):
                        last = nc.vector.tensor_scalar(xn[:, h, :], x[:, b, h, :], mean[:, b, h:h + 1],
                                                       rstd[:, b, h:h + 1], ALU.subtract, ALU.mult)
                    last.then_inc(s0["xn"], 1)
                    dve.wait_ge(s0["qk_psum"], b + 1)
                    nc.vector.tensor_tensor(rope_c[:], ps[0][:], rope[:, 0:2, :].rearrange("p j t -> p (j t)"), ALU.mult)
                    nc.vector.tensor_tensor(rope_s[:], ps[1][:], rope[:, 2:4, :].rearrange("p j t -> p (j t)"),
                                            ALU.mult).then_inc(s0["rope_mul"], 1)
                    dve.wait_ge(s0["rope_mul"], b + 1)
                    nc.vector.tensor_tensor(qk[:], rope_c[:], rope_s[:], ALU.add).then_inc(s0["rope"], 1)
                    dve.wait_ge(s0["rope"], b + 1)
                    for i in range(HPG):
                        nc.vector.tensor_scalar(q_m[:, :, i, :], qk[:, 0:T].rearrange("p (n q) -> p n q", q=QB),
                                                masks[:, i:i + 1], None, ALU.mult)
                    for g in range(HG):
                        last = nc.vector.tensor_scalar(k_m[:, g, WINDOW:], qk[:, T:], masks[:, HG + g:HG + g + 1], None,
                                                       ALU.mult)
                    last.then_inc(s0["masked"], 1)

                    def maximum(qb):
                        dve.wait_ge(s0["scores"], NQB * b + qb + 1)
                        nc.vector.tensor_reduce(negmax[:, qb, :],
                                                ps[2 + qb % 2][:, 0:HG * WIN].rearrange("p (g k) -> p g k", g=HG),
                                                AX.X, ALU.max, negate=True).then_inc(s0["negmax"], 1)

                    def inverse(qb):
                        dve.wait_ge(s0["exp"], NQB * b + qb + 1)
                        nc.vector.reciprocal(rsum[:, qb, :], esum[:, qb, :]).then_inc(s0["rsum"], 1)

                    maximum(0)
                    maximum(1)
                    inverse(0)
                    for qb in range(NQB):
                        if qb + 1 < NQB:
                            inverse(qb + 1)
                        dve.wait_ge(s0["p_t_psum"], NQB * b + qb + 1)
                        if qb >= 2:
                            dve.wait_ge(s0["pv"], NQB * b + qb - 1)
                        nc.vector.tensor_copy(p_t[:, qb % 2, :], ps[4 + qb % 2][0:WIN, :]).then_inc(s0["p_t"], 1)
                        if qb + 2 < NQB:
                            maximum(qb + 2)
                    dve.wait_ge(s0["pv"], NQB * (b + 1))
                    o4 = po[:].rearrange("p (n h q) -> p h n q", h=HPG, q=QB)
                    yv = y_t[:].rearrange("p (n q) -> p n q", q=QB)
                    nc.vector.tensor_scalar(yv, o4[:, 0], masks[:, 0:1], None, ALU.mult).then_inc(s0["y_part"], 1)
                    for i in range(1, HPG):
                        dve.wait_ge(s0["y_part"], (HPG - 1) * b + i)
                        last = nc.vector.scalar_tensor_tensor(out=yv, in0=o4[:, i], scalar=masks[:, i:i + 1], in1=yv,
                                                              op0=ALU.mult, op1=ALU.add)
                        last.then_inc(s0["y_part" if i < HPG - 1 else "y"], 1)
                    dve.wait_ge(s0["proj"], b + 1)
                    nc.vector.tensor_tensor(upd[:], ps[1][:, 0:T].rearrange("p (h c) -> p h c", h=NHALF),
                                            gates[:, bass.ds(b, 1), 0, :].to_broadcast([P, NHALF, C]),
                                            ALU.mult).then_inc(s0["upd"], 1)
                    dve.wait_ge(s0["upd"], b + 1)
                    nc.vector.tensor_tensor(x[:, b], x[:, b], upd[:], ALU.add).then_inc(s0["x1"], 1)
                    dve.wait_ge(s0["x1"], b + 1)
                    dve.wait_ge(const_done, 1)
                    for h in range(NHALF):
                        last = nc.vector.bn_stats(stats[:, b, h, :], x[:, b, h, :])
                    last.then_inc(s0["st"], 1)
                dve.wait_ge(s0["st"], NB)
                token_variances(dve, 1)
        phase.close()

        phase = ExitStack()
        CH = 4
        NCH = NB * NHALF // CH
        xn4 = sb("xn4", [P, CH, C], until=phase)
        h4 = sb("h4", [P, CH * P], until=phase)
        logit_max = sb("logit_max", [P, CH], until=phase)
        prob = sb("prob", [P, CH, E0], until=phase)
        prob_sum = sb("prob_sum", [P, CH], until=phase)
        hit = sb("hit", [P, CH, E0], until=phase)
        rank = sb("rank", [P, CH, E0], until=phase)
        rank_max = sb("rank_max", [P, CH], until=phase)
        first = sb("first", [P, CH, E0], until=phase)
        second = sb("second", [P, CH, E0], until=phase)
        left = sb("left", [P, CH, E0], until=phase)
        top = sb("top", [P, 2, CH], until=phase)
        top_sum = sb("top_sum", [P, CH], until=phase)
        w_exp = sb("w_exp", [P, P], until=phase)
        w_exp_t = sb("w_exp_t", [P, P], until=phase)
        act_g = sb("act_g", [P, 2, CH * P], until=phase)
        hid = sb("hid", [P, 2, MT, CH * P], until=phase)
        acc = sb("acc", [P, CH, C], until=phase)

        ROUTE_STEPS = 4 + 5 + 6 + 7
        s1 = {n: sem("e0_" + n) for n in (
            "zero", "chain", "xn", "x_t", "h", "logits", "route", "prob", "w", "w_t_psum", "w_t", "bias", "acc0", "gate_up", "silu",
            "hid", "out", "acc", "upd", "x2", "st")}

        with nc.Block() as block:
            @block.sync
            def _(sp):
                sp.wait_ge(all_in, 16 * (6 + len(l1)))

            @block.tensor
            def _(pe):
                pe.wait_ge(all_in, 16 * (6 + len(l1)))
                with pe.Fori(0, NCH) as c:
                    pe.wait_ge(s1["xn"], c + 1)
                    for t in range(CH):
                        last = nc.tensor.transpose(ps[0][:, t * P:(t + 1) * P], xn4[:, t, :], eye[:])
                    last.then_inc(s1["x_t"], 1)
                    pe.wait_ge(s1["h"], 2 * c + 2)
                    for t in range(CH):
                        last = nc.tensor.matmul(ps[1][:, t * E0:(t + 1) * E0], h4[:, t * P:(t + 1) * P], w_router[:],
                                                start=True, stop=True)
                    last.then_inc(s1["logits"], 1)

                    def gate_up(k):
                        if k >= 2:
                            pe.wait_ge(s1["hid"], E0 * MT * c + k - 1)
                        for j, w in enumerate((w_gate, w_up)):
                            last = nc.tensor.matmul(ps[2 + 2 * j + k % 2][:], w[:, k // MT, (k % MT) * P:(k % MT + 1) * P],
                                                    h4[:], start=True, stop=True)
                        last.then_inc(s1["gate_up"], 1)

                    def down(e):
                        pe.wait_ge(s1["hid"], E0 * MT * c + MT * (e + 1))
                        if e >= 2:
                            pe.wait_ge(s1["acc"], E0 * c + e - 1)
                        for t in range(CH):
                            for m in range(MT):
                                last = nc.tensor.matmul(po[:, (e % 2) * 512 + t * C:(e % 2) * 512 + (t + 1) * C],
                                                        hid[:, e % 2, m, t * P:(t + 1) * P], w_out[:, e, m, :],
                                                        start=(m == 0), stop=(m == MT - 1))
                        last.then_inc(s1["out"], 1)

                    for e in range(E0):
                        for m in range(MT):
                            gate_up(MT * e + m)
                        if e == 1:
                            pe.wait_ge(s1["w"], c + 1)
                            nc.tensor.transpose(ps[1][:, 0:P], w_exp[:], eye[:]).then_inc(s1["w_t_psum"], 1)
                            pe.wait_ge(s1["w_t"], c + 1)
                            for t in range(CH):
                                last = nc.tensor.matmul(ps[0][:, t * C:(t + 1) * C], w_exp_t[:], b_out[:, t, :],
                                                        start=True, stop=True)
                            last.then_inc(s1["bias"], 1)
                        if e >= 1:
                            down(e - 1)
                    down(E0 - 1)

            @block.scalar
            def _(act):
                with act.Fori(0, NCH) as c:
                    act.wait_ge(s1["x_t"], c + 1)
                    for j in range(2):
                        b = 2 * c + j
                        nc.scalar.activation(h4[:, j * T:(j + 1) * T], ps[0][:, j * T:(j + 1) * T], ACT.Identity,
                                             scale=mod[:, 0, 3, bass.ds(b, 1)],
                                             bias=mod[:, 0, 2, bass.ds(b, 1)]).then_inc(s1["h"], 1)
                    act.wait_ge(s1["route"], c + 1)
                    nc.scalar.activation(prob[:], hit[:], ACT.Exp).then_inc(s1["prob"], 1)
                    for k in range(E0 * MT):
                        act.wait_ge(s1["gate_up"], E0 * MT * c + k + 1)
                        nc.scalar.activation(act_g[:, k % 2, :], ps[2 + k % 2][:], ACT.Silu,
                                             bias=b_gu[:, 0, k:k + 1]).then_inc(s1["silu"], 1)
                        if k == 3:
                            act.wait_ge(s1["bias"], c + 1)
                            nc.scalar.copy(acc[:].rearrange("p t c -> p (t c)"), ps[0][:]).then_inc(s1["acc0"], 1)

            @block.vector
            def _(dve):
                nc.vector.memset(w_exp[:], 0.0).then_inc(s1["zero"], 1)
                dve.wait_ge(s1["zero"], 1)
                with dve.Fori(0, NCH) as c:
                    for t in range(CH):
                        b = 2 * c + t // 2
                        last = nc.vector.tensor_scalar(xn4[:, t, :], x[:, b, t % 2, :], mean[:, b, t % 2:t % 2 + 1],
                                                       rstd[:, b, t % 2:t % 2 + 1], ALU.subtract, ALU.mult)
                    last.then_inc(s1["xn"], 1)
                    dve.wait_ge(s1["logits"], c + 1)
                    lg = ps[1][:, 0:CH * E0].rearrange("p (t e) -> p t e", e=E0)
                    wide = lambda v: v.unsqueeze(2).to_broadcast([P, CH, E0])
                    steps = [0]

                    def chain(ins):
                        steps[0] += 1
                        ins.then_inc(s1["chain"], 1)
                        dve.wait_ge(s1["chain"], ROUTE_STEPS * c + steps[0])

                    chain(nc.vector.tensor_reduce(logit_max[:], lg, AX.X, ALU.max))
                    nc.vector.tensor_tensor(hit[:], lg, wide(logit_max[:]), ALU.subtract).then_inc(s1["route"], 1)
                    dve.wait_ge(s1["prob"], c + 1)
                    chain(nc.vector.tensor_reduce(prob_sum[:], prob[:], AX.X, ALU.add))
                    chain(nc.vector.reciprocal(prob_sum[:], prob_sum[:]))
                    chain(nc.vector.tensor_tensor(prob[:], prob[:], wide(prob_sum[:]), ALU.mult))
                    src = prob
                    for j, mark in enumerate((first, second)):
                        chain(nc.vector.tensor_reduce(top[:, j, :], src[:], AX.X, ALU.max))
                        chain(nc.vector.tensor_tensor(hit[:], src[:], wide(top[:, j, :]), ALU.is_equal))
                        chain(nc.vector.tensor_tensor(rank[:], hit[:], order[:].unsqueeze(1).to_broadcast([P, CH, E0]),
                                                      ALU.mult))
                        chain(nc.vector.tensor_reduce(rank_max[:], rank[:], AX.X, ALU.max))
                        chain(nc.vector.tensor_tensor(mark[:], rank[:], wide(rank_max[:]), ALU.is_equal))
                        if j == 0:
                            chain(nc.vector.scalar_tensor_tensor(out=left[:], in0=mark[:], scalar=-2.0, in1=src[:],
                                                                 op0=ALU.mult, op1=ALU.add))
                            src = left
                    chain(nc.vector.tensor_tensor(top_sum[:], top[:, 0, :], top[:, 1, :], ALU.add))
                    chain(nc.vector.tensor_scalar(top_sum[:], top_sum[:], 1e-8, None, ALU.add))
                    chain(nc.vector.reciprocal(top_sum[:], top_sum[:]))
                    for j in range(2):
                        chain(nc.vector.tensor_tensor(top[:, j, :], top[:, j, :], top_sum[:], ALU.mult))
                    chain(nc.vector.tensor_tensor(first[:], first[:], wide(top[:, 0, :]), ALU.mult))
                    chain(nc.vector.tensor_tensor(second[:], second[:], wide(top[:, 1, :]), ALU.mult))
                    assert steps[0] == ROUTE_STEPS
                    nc.vector.tensor_tensor(w_exp[:, 0:CH * E0].rearrange("p (t e) -> p t e", e=E0), first[:], second[:],
                                            ALU.add).then_inc(s1["w"], 1)

                    def hidden(k):
                        dve.wait_ge(s1["silu"], E0 * MT * c + k + 1)
                        if k // MT >= 2:
                            dve.wait_ge(s1["out"], E0 * c + k // MT - 1)
                        nc.vector.scalar_tensor_tensor(out=hid[:, k // MT % 2, k % MT, :], in0=ps[4 + k % 2][:],
                                                       scalar=b_gu[:, 1, k:k + 1], in1=act_g[:, k % 2, :],
                                                       op0=ALU.add, op1=ALU.mult).then_inc(s1["hid"], 1)

                    def accumulate(e):
                        dve.wait_ge(s1["out"], E0 * c + e + 1)
                        for t in range(CH):
                            last = nc.vector.scalar_tensor_tensor(
                                out=acc[:, t, :], in0=po[:, (e % 2) * 512 + t * C:(e % 2) * 512 + (t + 1) * C],
                                scalar=w_exp[:, t * E0 + e:t * E0 + e + 1], in1=acc[:, t, :], op0=ALU.mult, op1=ALU.add)
                        last.then_inc(s1["acc"], 1)

                    for k in range(E0 * MT):
                        if k == 3:
                            dve.wait_ge(s1["w_t_psum"], c + 1)
                            nc.vector.tensor_copy(w_exp_t[:], ps[1][:, 0:P]).then_inc(s1["w_t"], 1)
                        hidden(k)
                        if k % MT == 0 and k >= 2 * MT:
                            if k == 2 * MT:
                                dve.wait_ge(s1["acc0"], c + 1)
                            else:
                                dve.wait_ge(s1["acc"], E0 * c + k // MT - 2)
                            accumulate(k // MT - 2)
                    for e in (E0 - 2, E0 - 1):
                        dve.wait_ge(s1["acc"], E0 * c + e)
                        accumulate(e)
                    dve.wait_ge(s1["acc"], E0 * (c + 1))
                    for j in range(2):
                        last = nc.vector.tensor_tensor(acc[:, 2 * j:2 * j + 2, :], acc[:, 2 * j:2 * j + 2, :],
                                                       gates[:, bass.ds(2 * c + j, 1), 1, :].to_broadcast([P, 2, C]),
                                                       ALU.mult)
                    last.then_inc(s1["upd"], 1)
                    dve.wait_ge(s1["upd"], c + 1)
                    xc = x[:, bass.ds(2 * c, 2), :, :].rearrange("p b h c -> p (b h) c")
                    nc.vector.tensor_tensor(xc, xc, acc[:], ALU.add).then_inc(s1["x2"], 1)
                    dve.wait_ge(s1["x2"], c + 1)
                    dve.wait_ge(const_done, 1)
                    for t in range(CH):
                        last = nc.vector.bn_stats(stats[:, 2 * c + t // 2, t % 2, :], x[:, 2 * c + t // 2, t % 2, :])
                    last.then_inc(s1["st"], 1)
                dve.wait_ge(s1["st"], NCH)
                token_variances(dve, 2)

            @block.gpsimd
            def _(pool):
                token_scales(pool, 2)
        phase.close()

        phase = ExitStack()
        h1t = sb("h1t", [P, P], until=phase)
        qkv = sb("qkv", [P, NB, 3, C], until=phase)
        q1_t = sb("q1_t", [P, P], until=phase)
        rel = sb("rel", [P, NB, H, NB], until=phase)
        prod_s = sb("prod_s", [P, H, NB, D], until=phase)
        score = sb("score", [P, 2, H, NB], until=phase)
        smax = sb("smax", [P, H], until=phase)
        ssum = sb("ssum", [P, H], until=phase)
        prob1 = sb("prob1", [P, 2, H, NB], until=phase)
        prob1_t = sb("prob1_t", [P, 2, P], until=phase)
        prod_v = sb("prod_v", [P, H, D, NB], until=phase)
        att = sb("att", [P, C], until=phase)
        att_t = sb("att_t", [P, P], until=phase)
        upd1 = sb("upd1", [P, C], until=phase)
        SCALE1 = float(D) ** -0.5

        s2 = {n: sem("a1_" + n) for n in (
            "xn", "x_t", "h", "qkv_psum", "q_psum", "qkv", "q_t", "rel_psum", "rel", "prod_s", "dots", "raw", "max", "score",
            "exp", "sum", "inv", "prob", "p_t_psum", "p_t", "rv", "prod_v", "mix", "att", "att_t_psum", "att_t", "proj",
            "upd", "gated", "x3", "st")}
        rk = l1["rk"]

        with nc.Block() as block:
            @block.tensor
            def _(pe):
                gate_matmuls(pe, 1)
                pe.wait_ge(gate_steps, 2 * NB)
                with pe.Fori(0, NHALF) as half:
                    with pe.Fori(0, NB) as t:
                        n = half * NB + t
                        pe.wait_ge(s2["xn"], n + 1)
                        nc.tensor.transpose(ps[0][:, 0:P], xn[:, 0, :], eye[:]).then_inc(s2["x_t"], 1)
                        pe.wait_ge(s2["h"], n + 1)
                        nc.tensor.matmul(ps[2][:, 0:P], l1["w_qkv1"][:, 0:C], h1t[:], start=True,
                                         stop=True).then_inc(s2["q_psum"], 1)
                        pe.wait_ge(s2["q_t"], n + 1)
                        nc.tensor.matmul(ps[1][:, 0:3 * C], h1t[:], l1["w_qkv1"][:], start=True,
                                         stop=True).then_inc(s2["qkv_psum"], 1)
                        nc.tensor.matmul(ps[3][:, 0:H * NB], q1_t[:], rk[:, :, bass.ds(MAXREL - t, NB)], start=True,
                                         stop=True).then_inc(s2["rel_psum"], 1)
                    with pe.Fori(0, NB) as t:
                        n = half * NB + t
                        pe.wait_ge(s2["prob"], n + 1)
                        for j in range(2):
                            last = nc.tensor.transpose(ps[4][:, j * P:(j + 1) * P],
                                                       prob1[:, 0, 8 * j:8 * j + 8, :].rearrange("p h s -> p (h s)"), eye[:])
                        last.then_inc(s2["p_t_psum"], 1)
                        pe.wait_ge(s2["p_t"], n + 1)
                        for j in range(2):
                            last = nc.tensor.matmul(ps[5][:, j * 64:(j + 1) * 64], prob1_t[:, j, :],
                                                    l1["rv"][:, bass.ds(t, 1), :, :], start=True, stop=True)
                        last.then_inc(s2["rv"], 1)
                        pe.wait_ge(s2["att"], n + 1)
                        nc.tensor.transpose(ps[0][:, 0:P], att[:], eye[:]).then_inc(s2["att_t_psum"], 1)
                        pe.wait_ge(s2["att_t"], n + 1)
                        nc.tensor.matmul(ps[1][:, 0:C], att_t[:], l1["w_o1"][:], start=True,
                                         stop=True).then_inc(s2["proj"], 1)

            @block.scalar
            def _(act):
                gate_sizes(act, 1)
                with act.Fori(0, NHALF) as half:
                    with act.Fori(0, NB) as t:
                        n = half * NB + t
                        act.wait_ge(s2["x_t"], n + 1)
                        nc.scalar.activation(h1t[:], ps[0][:, 0:P], ACT.Identity, scale=mod[:, 1, 1, bass.ds(t, 1)],
                                             bias=mod[:, 1, 0, bass.ds(t, 1)]).then_inc(s2["h"], 1)
                        act.wait_ge(s2["q_psum"], n + 1)
                        nc.scalar.activation(q1_t[:], ps[2][:, 0:P], ACT.Identity,
                                             bias=l1["b_q1"][:]).then_inc(s2["q_t"], 1)
                        act.wait_ge(s2["rel_psum"], n + 1)
                        nc.scalar.copy(rel[:, bass.ds(t, 1), :, :].rearrange("p t h s -> p (t h s)"),
                                       ps[3][:, 0:H * NB]).then_inc(s2["rel"], 1)
                    with act.Fori(0, NB) as t:
                        n = half * NB + t
                        act.wait_ge(s2["score"], n + 1)
                        nc.scalar.activation(score[:, 1], score[:, 0], ACT.Exp, scale=SCALE1).then_inc(s2["exp"], 1)
                        act.wait_ge(s2["p_t_psum"], n + 1)
                        nc.scalar.copy(prob1_t[:].rearrange("p j q -> p (j q)"), ps[4][:, 0:2 * P]).then_inc(s2["p_t"], 1)
                        act.wait_ge(s2["att_t_psum"], n + 1)
                        nc.scalar.copy(att_t[:], ps[0][:, 0:P]).then_inc(s2["att_t"], 1)

            @block.gpsimd
            def _(pool):
                with pool.Fori(0, NHALF) as half:
                    with pool.Fori(0, NB) as t:
                        n = half * NB + t
                        pool.wait_ge(s2["qkv"], NB * half + NB)
                        pool.wait_ge(s2["dots"], n + 1)
                        qv = qkv[:, bass.ds(t, 1), 0, :].rearrange("p o (h d) -> p (o h) d", d=D)
                        kv = qkv[:, :, 1, :].rearrange("p s (h d) -> p h s d", d=D)
                        nc.gpsimd.tensor_tensor(prod_s[:], qv.unsqueeze(2).to_broadcast([P, H, NB, D]), kv,
                                                ALU.mult).then_inc(s2["prod_s"], 1)
                token_scales(pool, 3)

            @block.vector
            def _(dve):
                gate_program(dve, 1)
                nc.vector.memset(prod_v[:], 0.0).then_inc(s2["dots"], 1)
                with dve.Fori(0, NHALF) as half:
                    with dve.Fori(0, NB) as t:
                        n = half * NB + t
                        nc.vector.tensor_scalar(xn[:, 0, :], x[:, t, half, :], mean[:, t, bass.ds(half, 1)],
                                                rstd[:, t, bass.ds(half, 1)], ALU.subtract, ALU.mult).then_inc(s2["xn"], 1)
                        dve.wait_ge(s2["qkv_psum"], n + 1)
                        nc.vector.tensor_tensor(qkv[:, bass.ds(t, 1), :, :].rearrange("p o j c -> p (o j c)"),
                                                ps[1][:, 0:3 * C], l1["b_qkv1"][:], ALU.add).then_inc(s2["qkv"], 1)
                        dve.wait_ge(s2["x_t"], n + 1)
                    with dve.Fori(0, NB) as t:
                        n = half * NB + t
                        dve.wait_ge(s2["rel"], NB * half + NB)
                        dve.wait_ge(s2["prod_s"], n + 1)
                        nc.vector.tensor_reduce(score[:, 0], prod_s[:], AX.X, ALU.add).then_inc(s2["dots"], 1)
                        dve.wait_ge(s2["dots"], n + 2)
                        nc.vector.tensor_tensor(score[:, 0], score[:, 0], rel[:, t, :, :], ALU.add).then_inc(s2["raw"], 1)
                        dve.wait_ge(s2["raw"], n + 1)
                        nc.vector.tensor_reduce(smax[:], score[:, 0], AX.X, ALU.max).then_inc(s2["max"], 1)
                        dve.wait_ge(s2["max"], n + 1)
                        nc.vector.tensor_tensor(score[:, 0], score[:, 0], smax[:].unsqueeze(2).to_broadcast([P, H, NB]),
                                                ALU.subtract).then_inc(s2["score"], 1)
                        dve.wait_ge(s2["exp"], n + 1)
                        nc.vector.tensor_reduce(ssum[:], score[:, 1], AX.X, ALU.add).then_inc(s2["sum"], 1)
                        dve.wait_ge(s2["sum"], n + 1)
                        nc.vector.reciprocal(ssum[:], ssum[:]).then_inc(s2["inv"], 1)
                        dve.wait_ge(s2["inv"], n + 1)
                        nc.vector.tensor_tensor(prob1[:, 0], score[:, 1], ssum[:].unsqueeze(2).to_broadcast([P, H, NB]),
                                                ALU.mult).then_inc(s2["prob"], 1)
                        dve.wait_ge(s2["prob"], n + 1)
                        nc.vector.tensor_tensor(prod_v[:], prob1[:, 0].unsqueeze(2).to_broadcast([P, H, D, NB]),
                                                qkv[:, :, 2, :].rearrange("p s (h d) -> p h d s", d=D),
                                                ALU.mult).then_inc(s2["prod_v"], 1)
                        dve.wait_ge(s2["prod_v"], n + 1)
                        nc.vector.tensor_reduce(att[:], prod_v[:].rearrange("p h d s -> p (h d) s"), AX.X,
                                                ALU.add).then_inc(s2["mix"], 1)
                        dve.wait_ge(s2["mix"], n + 1)
                        dve.wait_ge(s2["rv"], n + 1)
                        nc.vector.tensor_tensor(att[:], ps[5][:, 0:C], att[:], ALU.add).then_inc(s2["att"], 1)
                        dve.wait_ge(s2["proj"], n + 1)
                        nc.vector.tensor_tensor(upd1[:], ps[1][:, 0:C], l1["b_o1"][:], ALU.add).then_inc(s2["upd"], 1)
                        dve.wait_ge(s2["upd"], n + 1)
                        nc.vector.tensor_tensor(upd1[:], upd1[:], gates[:, t, 0, :], ALU.mult).then_inc(s2["gated"], 1)
                        dve.wait_ge(s2["gated"], n + 1)
                        nc.vector.tensor_tensor(x[:, t, half, :], x[:, t, half, :], upd1[:], ALU.add).then_inc(s2["x3"], 1)
                        dve.wait_ge(s2["x3"], n + 1)
                        dve.wait_ge(const_done, 1)
                        nc.vector.bn_stats(stats[:, t, half, :], x[:, t, half, :]).then_inc(s2["st"], 1)
                dve.wait_ge(s2["st"], NHALF * NB)
                token_variances(dve, 3)
        phase.close()

        phase = ExitStack()
        h_b = sb("h_b", [P, T], until=phase)
        h_all = sb("h_all", [P, NB, T], until=phase)
        enc = sb("enc", [P, 2, T], until=phase)
        diff = sb("diff", [P, 2, 2, T], until=phase)
        losses = sb("losses", [P, NB, E1], until=phase)
        ones = sb("ones", [P, P], until=phase)
        least = sb("least", [P, NB], until=phase)
        is_least = sb("is_least", [P, NB, E1], until=phase)
        chosen = sb("chosen", [P, NB, E1], until=phase)
        base_u = sb("base_u", [P, NHALF, C], until=phase)
        down_m = sb("down_m", [P, R, E1], until=phase)
        down_w = sb("down_w", [P, R], until=phase)
        down_bm = sb("down_bm", [R, E1], until=phase)
        down_b = sb("down_b", [R, 1], until=phase)
        up_m = sb("up_m", [P, C, E1], until=phase)
        up_w = sb("up_w", [P, C], until=phase)
        a_t = sb("a_t", [P, T], until=phase)
        upd2 = sb("upd2", [P, NHALF, C], until=phase)
        s3 = {n: sem("e1_" + n) for n in (
            "init", "argmin", "sq", "xn", "x_t", "h", "kept", "base", "base1", "base2", "x4", "enc_psum", "enc", "rec", "diff", "loss",
            "loss_psum", "route", "down_m", "down_w", "up_m", "up_w", "code", "a_t", "up", "upd", "x5")}
        out_done = sem("out_done")
        NP = E1 // 2

        with nc.Block() as block:
            @block.tensor
            def _(pe):
                with pe.Fori(0, NB) as b:
                    pe.wait_ge(s3["xn"], b + 1)
                    for h in range(NHALF):
                        last = nc.tensor.transpose(ps[0][:, h * P:(h + 1) * P], xn[:, h, :], eye[:])
                    last.then_inc(s3["x_t"], 1)
                    pe.wait_ge(s3["h"], b + 1)
                    for j in range(2):
                        last = nc.tensor.matmul(ps[1][:, j * T:(j + 1) * T], l1["w_d1"][:, j * P:(j + 1) * P], h_b[:],
                                                start=True, stop=True)
                    last.then_inc(s3["enc_psum"], 1)
                    for h in range(NHALF):
                        last = nc.tensor.matmul(ps[0][:, h * C:(h + 1) * C], h_b[:, h * P:(h + 1) * P], l1["w_base"][:],
                                                start=True, stop=True)
                    last.then_inc(s3["base"], 1)
                    pe.wait_ge(s3["enc"], 2 * b + 2)
                    for p in range(NP):
                        if p >= 2:
                            pe.wait_ge(s3["diff"], NP * b + p - 1)
                        for j in range(2):
                            last = nc.tensor.matmul(ps[2 + p % 2][:, j * T:(j + 1) * T], l1["w_d2"][:, 2 * p + j, :],
                                                    enc[:, p // 2, :], start=True, stop=True)
                        last.then_inc(s3["rec"], 1)
                pe.wait_ge(s3["loss"], NB)
                nc.tensor.matmul(ps[4][:, 0:NB * E1], ones[:], losses[:].rearrange("p b e -> p (b e)"), start=True,
                                 stop=True).then_inc(s3["loss_psum"], 1)
                with pe.Fori(0, NB) as b:
                    pe.wait_ge(s3["down_w"], b + 1)
                    nc.tensor.matmul(ps[0][0:R, 0:T], down_w[:], h_all[:, b, :], start=True, stop=True)\
                        .then_inc(s3["code"], 1)
                    pe.wait_ge(s3["a_t"], b + 1)
                    pe.wait_ge(s3["up_w"], b + 2)
                    for h in range(NHALF):
                        last = nc.tensor.matmul(ps[1][:, h * C:(h + 1) * C], a_t[:, h * P:(h + 1) * P], up_w[:],
                                                start=True, stop=True)
                    last.then_inc(s3["up"], 1)

            @block.scalar
            def _(act):
                with act.Fori(0, NB) as b:
                    act.wait_ge(s3["x_t"], b + 1)
                    nc.scalar.activation(h_b[:], ps[0][:, 0:T], ACT.Identity, scale=mod[:, 1, 3, bass.ds(b, 1)],
                                         bias=mod[:, 1, 2, bass.ds(b, 1)]).then_inc(s3["h"], 1)
                    act.wait_ge(s3["enc_psum"], b + 1)
                    for j in range(2):
                        nc.scalar.activation(enc[:, j, :], ps[1][:, j * T:(j + 1) * T], ACT.Relu,
                                             bias=l1["b_d1"][:, j:j + 1]).then_inc(s3["enc"], 1)
                    for p in range(NP):
                        act.wait_ge(s3["diff"], NP * b + p + 1)
                        for j in range(2):
                            last = nc.scalar.activation(diff[:, p % 2, j, :], diff[:, p % 2, j, :], ACT.Square,
                                                        bias=l1["b_d2"][:, 2 * p + j:2 * p + j + 1],
                                                        accum_out=losses[:, b, 2 * p + j:2 * p + j + 1])
                        if p < NP - 1:
                            last.then_inc(s3["sq"], 1)
                        else:
                            last.then_inc(s3["loss"], 1)
                with act.Fori(0, NB) as b:
                    act.wait_ge(s3["code"], b + 1)
                    act.wait_ge(s3["down_w"], b + 1)
                    nc.scalar.activation(a_t[0:R, :], ps[0][0:R, 0:T], ACT.Relu, bias=down_b[:]).then_inc(s3["a_t"], 1)

            @block.gpsimd
            def _(pool):
                with pool.Fori(0, NB) as b:
                    pool.wait_ge(s3["h"], b + 1)
                    nc.gpsimd.tensor_copy(h_all[:, b, :], h_b[:]).then_inc(s3["kept"], 1)
                pool.wait_ge(s3["route"], 4)
                with pool.Fori(0, NB) as b:
                    pool.wait_ge(s3["up_w"], b + 1)
                    nc.gpsimd.tensor_tensor(up_m[:], l1["w_au"][:], chosen[:, b, :].unsqueeze(1).to_broadcast([P, C, E1]),
                                            ALU.mult).then_inc(s3["up_m"], 1)

            @block.vector
            def _(dve):
                nc.vector.memset(ones[:], 1.0)
                nc.vector.memset(a_t[R:P, :], 0.0).then_inc(s3["init"], 1)
                dve.wait_ge(s3["init"], 1)
                nc.vector.memset(a_t[R:R + 1, :], 1.0)
                with dve.Fori(0, NB) as b:
                    for h in range(NHALF):
                        last = nc.vector.tensor_scalar(xn[:, h, :], x[:, b, h, :], mean[:, b, h:h + 1],
                                                       rstd[:, b, h:h + 1], ALU.subtract, ALU.mult)
                    last.then_inc(s3["xn"], 1)
                    for p in range(NP):
                        dve.wait_ge(s3["rec"], NP * b + p + 1)
                        if p >= 2:
                            dve.wait_ge(s3["sq"], (NP - 1) * b + p - 1)
                        nc.vector.tensor_tensor(diff[:, p % 2], ps[2 + p % 2][:].rearrange("p (j t) -> p j t", j=2),
                                                h_b[:].unsqueeze(1).to_broadcast([P, 2, T]),
                                                ALU.subtract).then_inc(s3["diff"], 1)
                    dve.wait_ge(s3["base"], b + 1)
                    nc.vector.tensor_tensor(base_u[:], ps[0][:, 0:T].rearrange("p (h c) -> p h c", h=NHALF),
                                            l1["b_base"][:].unsqueeze(1).to_broadcast([P, NHALF, C]),
                                            ALU.add).then_inc(s3["base1"], 1)
                    dve.wait_ge(s3["base1"], b + 1)
                    nc.vector.tensor_tensor(base_u[:], base_u[:], gates[:, bass.ds(b, 1), 1, :].to_broadcast([P, NHALF, C]),
                                            ALU.mult).then_inc(s3["base2"], 1)
                    dve.wait_ge(s3["base2"], b + 1)
                    nc.vector.tensor_tensor(x[:, b], x[:, b], base_u[:], ALU.add).then_inc(s3["x4"], 1)
                    dve.wait_ge(s3["kept"], b + 1)
                    dve.wait_ge(s3["loss"], b + 1)
                dve.wait_ge(s3["loss_psum"], 1)
                ls = ps[4][:, 0:NB * E1].rearrange("p (b e) -> p b e", e=E1)
                wide = lambda v: v.unsqueeze(2).to_broadcast([P, NB, E1])
                nc.vector.tensor_reduce(least[:], ls, AX.X, ALU.min).then_inc(s3["argmin"], 1)
                dve.wait_ge(s3["argmin"], 1)
                nc.vector.tensor_tensor(is_least[:], ls, wide(least[:]), ALU.is_equal).then_inc(s3["argmin"], 1)
                dve.wait_ge(s3["argmin"], 2)
                nc.vector.tensor_tensor(is_least[:], is_least[:], order[:].unsqueeze(1).to_broadcast([P, NB, E1]),
                                        ALU.mult).then_inc(s3["argmin"], 1)
                dve.wait_ge(s3["argmin"], 3)
                nc.vector.tensor_reduce(least[:], is_least[:], AX.X, ALU.max).then_inc(s3["argmin"], 1)
                dve.wait_ge(s3["argmin"], 4)
                nc.vector.tensor_tensor(chosen[:], is_least[:], wide(least[:]), ALU.is_equal).then_inc(s3["route"], 4)
                dve.wait_ge(s3["route"], 4)
                nc.vector.memset(up_w[:], 0.0).then_inc(s3["up_w"], 1)
                dve.wait_ge(s3["up_w"], 1)
                with dve.Fori(0, NB) as b:
                    pick = lambda rows, n: chosen[0:rows, b, :].unsqueeze(1).to_broadcast([rows, n, E1])
                    nc.vector.tensor_tensor(down_m[:], l1["w_ad"][:], pick(P, R), ALU.mult)
                    nc.vector.tensor_tensor(down_bm[:], l1["b_ad"][:], chosen[0:R, b, :], ALU.mult).then_inc(s3["down_m"], 1)
                    dve.wait_ge(s3["down_m"], b + 1)
                    nc.vector.tensor_reduce(down_b[:], down_bm[:], AX.X, ALU.add)
                    nc.vector.tensor_reduce(down_w[:], down_m[:], AX.X, ALU.add).then_inc(s3["down_w"], 1)
                    dve.wait_ge(s3["up_m"], b + 1)
                    nc.vector.tensor_reduce(up_w[:], up_m[:], AX.X, ALU.add).then_inc(s3["up_w"], 1)
                    dve.wait_ge(s3["up"], b + 1)
                    nc.vector.tensor_tensor(upd2[:], ps[1][:, 0:T].rearrange("p (h c) -> p h c", h=NHALF),
                                            gates[:, bass.ds(b, 1), 1, :].to_broadcast([P, NHALF, C]),
                                            ALU.mult).then_inc(s3["upd"], 1)
                    dve.wait_ge(s3["upd"], b + 1)
                    nc.vector.tensor_tensor(x[:, b], x[:, b], upd2[:], ALU.add).then_inc(s3["x5"], 1)

            @block.sync
            def _(sp):
                ov = out.rearrange("b (h p) c -> b p h c", p=P)
                with sp.Fori(0, NB) as b:
                    sp.wait_ge(s3["x5"], b + 1)
                    sp.dma_start(ov[b], x[:, b]).then_inc(out_done, 16)
                sp.wait_ge(out_done, 16 * NB)
        phase.close()


def lay_out(d):
    g = {k: np.asarray(v) for k, v in d.items()}
    half = D // 2
    ch = np.arange(C)
    partner = (ch // D) * D + (ch % D + half) % D
    wa = g["L0_attn_w_attn"]
    q, k, v = wa[:C], wa[C:2 * C], wa[2 * C:]
    r = {"x": g["L0_attn_x"]}
    r["wqkv0"] = np.stack([q.T, k.T, q[partner].T, k[partner].T, v.T], 1)
    r["wproj0"] = g["L0_attn_w_proj"].T
    r["cT"] = np.stack([g["L0_c"].T, g["L1_c"].T], 1)
    r["wmod"] = np.stack([g[n].reshape(C, 6, C)[:, [0, 1, 3, 4, 2, 5]] for n in ("L0_wmod", "L1_wmod")], 1)
    r["wgate"] = g["L0_ffn_W_gate"].transpose(1, 0, 2)
    r["wup"] = g["L0_ffn_W_up"].transpose(1, 0, 2)
    r["wout"] = g["L0_ffn_W_out"].reshape(E0, MT, P, C).transpose(2, 0, 1, 3)
    r["bgu"] = np.stack([g["L0_ffn_b_gate"].reshape(E0 * MT, P).T, g["L0_ffn_b_up"].reshape(E0 * MT, P).T], 1)
    bo = np.zeros((P, 4, C), np.float32)
    for i in range(4):
        bo[i * E0:(i + 1) * E0, i] = g["L0_ffn_b_out"]
    r["bout"] = bo
    r["wrouter"] = g["L0_ffn_W_router"]
    row = lambda n: np.broadcast_to(g[n].reshape(1, -1), (P, g[n].size))
    r["w_qkv1"] = np.concatenate([g["L1_attn_W" + n].T for n in "qkv"], 1)
    r["b_qkv1"] = np.concatenate([row("L1_attn_b" + n) for n in "qkv"], 1)
    r["b_q1"] = g["L1_attn_bq"].reshape(C, 1)
    rk = np.zeros((C, H, 2 * MAXREL + 1), np.float32)
    rv = np.zeros((P, 16, 8, D), np.float32)
    for h in range(H):
        rk[h * D:(h + 1) * D, h] = g["L1_attn_rk_table"].T
    for h in range(8):
        for t in range(16):
            rv[h * 16:(h + 1) * 16, t, h] = g["L1_attn_rv_table"][MAXREL - t:2 * MAXREL - t]
    r["rk"], r["rv"] = rk, rv
    r["w_o1"] = g["L1_attn_Wo"].T
    r["b_o1"] = row("L1_attn_bo")
    r["w_base"] = g["L1_ffn_W_base"]
    r["b_base"] = row("L1_ffn_b_base")
    r["w_d1"] = g["L1_ffn_Wd1"].transpose(1, 0, 2).reshape(C, E1 * HD1)
    r["b_d1"] = g["L1_ffn_bd1"].reshape(2, P).T
    wd2 = np.zeros((P, E1, C), np.float32)
    for e in range(E1):
        wd2[(e % 4) * HD1:(e % 4 + 1) * HD1, e] = g["L1_ffn_Wd2"][e]
    r["w_d2"] = wd2
    r["b_d2"] = g["L1_ffn_bd2"].T
    r["w_ad"] = g["L1_ffn_Wa_down"].transpose(1, 2, 0)
    r["b_ad"] = g["L1_ffn_ba_down"].T
    au = np.zeros((P, C, E1), np.float32)
    au[:R] = g["L1_ffn_Wa_up"].transpose(1, 2, 0)
    au[R] = g["L1_ffn_ba_up"].T
    r["w_au"] = au
    return r


def kernel(**inputs):
    import concourse.bacc as bacc
    from concourse.bass_utils import run_bass_kernel_spmd

    arrays = {**lay_out(inputs), **shape_constants()}
    arrays = {"in_" + k: np.ascontiguousarray(v) for k, v in arrays.items()}
    nc = bacc.Bacc("TRN2", target_bir_lowering=False, num_devices=1)
    aps = {k[3:]: nc.dram_tensor(k, v.shape, mybir.dt.from_np(v.dtype), kind="ExternalInput").ap() for k, v in arrays.items()}
    out = nc.dram_tensor("x_out", (NB, T, C), F32, kind="ExternalOutput").ap()
    build(nc, aps, out)
    r = run_bass_kernel_spmd(nc, [arrays], core_ids=[0])
    return r.results[0]["x_out"]
```

```python
from contextlib import ExitStack

import numpy as np

import concourse.bass as bass
from concourse import mybir

F32 = mybir.dt.float32
BF16 = mybir.dt.bfloat16
ALU = mybir.AluOpType
ACT = mybir.ActivationFunctionType
AX = mybir.AxisListType

NB, T, C = 16, 256, 128
P = 128
NHALF = T // P
H, D = 16, 8
WINDOW = 64
QB = 32
NQB = T // QB
WIN = WINDOW + QB
HG = 4
HPG = H // HG
E0, M = 8, 256
MT = M // P
MAXREL = 16
E1, HD1, R = 8, 32, 64
EPS = 1e-5
NEG = -1e30


def shape_constants():
    f = np.float32
    half = D // 2
    inv = (1.0 / (f(10000.0) ** (np.arange(0, D, 2, dtype=f) / f(D)))).astype(f)
    ang = np.outer(np.arange(T, dtype=f), inv).astype(f)
    cos, sin = np.cos(ang).astype(f), np.sin(ang).astype(f)
    ch = np.arange(C)
    rc = cos[:, ch % half].T
    rs = sin[:, ch % half].T * np.where(ch % D < half, 1, -1)[:, None]
    scale = 1.0 / np.sqrt(f(D))
    rope = np.stack([rc * scale, rc, rs * scale, rs], 1).astype(f)
    masks = np.zeros((P, 2 * HG), f)
    masks[ch, (ch // D) % HPG] = 1
    masks[ch, HG + ch // (C // HG)] = 1
    key, q = np.arange(P)[:, None], np.arange(QB)[None, :]
    win = np.zeros((P, 3, HPG, QB), f)
    for v, first in enumerate((WINDOW, WINDOW - QB, 0)):
        ok = (key >= q) & (key <= q + WINDOW) & (key >= first)
        win[:, v] = np.where(ok | (key >= WIN), 0.0, NEG)[:, None, :]
    eye = np.eye(P, dtype=f)
    pick = np.zeros((P, HG, WIN), f)
    pick[np.arange(WIN), :, np.arange(WIN)] = 1
    return {
        "const_rope": rope, "const_masks": masks, "const_window": win.reshape(P, -1),
        "const_eye": eye, "const_pick": pick.reshape(P, -1),
        "const_order": np.tile((E0 - np.arange(E0, dtype=f))[None], (P, 1)),
    }


def build(nc, a, out):
    with ExitStack() as ctx:
        def sb(name, shape, dt=F32, until=ctx):
            return until.enter_context(nc.sbuf_tensor(name, shape, dt))

        def sem(name):
            return ctx.enter_context(nc.semaphore(name))

        x = sb("x", [P, NB, NHALF, C])
        eye = sb("eye", [P, P])
        masks = sb("masks", [P, 2 * HG])
        order = sb("order", [P, E0])
        c_t = sb("c_t", [P, 2, NB])
        silu_c = sb("silu_c", [P, 2, NB])
        w_mod = sb("w_mod", [P, 2, 6, C])
        mod = sb("mod", [P, 2, 4, NB])
        gates = sb("gates", [P, NB, 2, C])
        gate_sign = sb("gate_sign", [P, 512])
        gate_size = sb("gate_size", [P, 2, 512])
        stats = sb("stats", [P, NB, NHALF, 6])
        ln_sum = sb("ln_sum", [P, NB, NHALF])
        ln_dif = sb("ln_dif", [P, NB, NHALF])
        ln_dev = sb("ln_dev", [P, NB, NHALF])
        var_eps = sb("var_eps", [P, NB, NHALF])
        mean = sb("mean", [P, NB, NHALF])
        minus_half = sb("minus_half", [P, NB, NHALF])
        rstd = sb("rstd", [P, NB, NHALF])
        xn = sb("xn", [P, NHALF, C])

        po = ctx.enter_context(nc.psum_tensor("po", [P, 1024], F32))
        ps = [ctx.enter_context(nc.psum_tensor(f"ps{i}", [P, 512], F32)) for i in range(6)]

        ones_row = [P, 1]

        x_in = sem("x_in")
        small_in = sem("small_in")
        l0_in = sem("l0_in")
        all_in = sem("all_in")
        silu_done = sem("silu_done")
        mod_psum = sem("mod_psum")
        mod_done = sem("mod_done")
        gate_psum = sem("gate_psum")
        gate_steps = sem("gate_steps")
        gate_abs = sem("gate_abs")
        const_done = sem("const_done")
        st_done = sem("st_done")
        ln_steps = sem("ln_steps")
        ln_var = sem("ln_var")
        ln_rstd = sem("ln_rstd")

        def token_variances(dve, n):
            nc.vector.tensor_tensor(ln_sum[:], stats[:, :, :, 1], stats[:, :, :, 4], ALU.add)
            nc.vector.tensor_tensor(ln_dif[:], stats[:, :, :, 1], stats[:, :, :, 4], ALU.subtract)
            nc.vector.tensor_tensor(ln_dev[:], stats[:, :, :, 2], stats[:, :, :, 5], ALU.add).then_inc(ln_steps, 1)
            dve.wait_ge(ln_steps, 3 * n + 1)
            nc.vector.tensor_scalar(mean[:], ln_sum[:], 0.5, None, ALU.mult)
            nc.vector.tensor_tensor(ln_dif[:], ln_dif[:], ln_dif[:], ALU.mult).then_inc(ln_steps, 1)
            dve.wait_ge(ln_steps, 3 * n + 2)
            nc.vector.tensor_scalar(ln_dif[:], ln_dif[:], 0.25, EPS, ALU.mult, ALU.add).then_inc(ln_steps, 1)
            dve.wait_ge(ln_steps, 3 * n + 3)
            nc.vector.scalar_tensor_tensor(out=var_eps[:], in0=ln_dev[:], scalar=1.0 / C, in1=ln_dif[:], op0=ALU.mult,
                                           op1=ALU.add).then_inc(ln_var, 1)

        def token_scales(pool, n):
            pool.wait_ge(ln_var, n + 1)
            nc.gpsimd.tensor_tensor(rstd[:], var_eps[:], minus_half[:], ALU.pow).then_inc(ln_rstd, 1)


        l1 = {}
        for name, shape in (("w_qkv1", [P, 3 * C]), ("b_qkv1", [P, 3 * C]), ("b_q1", [P, 1]), ("rk", [P, H, 2 * MAXREL + 1]),
                            ("rv", [P, 16, 8, D]), ("w_o1", [P, C]), ("b_o1", [P, C]),
                            ("w_base", [P, C]), ("b_base", [P, C]), ("w_d1", [P, 2 * P]), ("b_d1", [P, 2]),
                            ("w_d2", [P, E1, C]), ("b_d2", [P, E1]), ("w_ad", [P, R, E1]), ("b_ad", [R, E1]),
                            ("w_au", [P, C, E1])):
            l1[name] = sb(name, shape)

        layer0 = ExitStack()
        rope = sb("rope", [P, 4, T], until=layer0)
        window_f = sb("window_f", [P, 3 * P], until=layer0)
        window_bf = sb("window_bf", [P, 3, P], BF16, until=layer0)
        pick_f = sb("pick_f", [P, HG * WIN], until=layer0)
        pick_bf = sb("pick_bf", [P, HG * WIN], BF16, until=layer0)
        w_qkv0 = sb("w_qkv0", [P, 5, C], until=layer0)
        w_proj0 = sb("w_proj0", [P, C], until=layer0)
        w_gate = sb("w_gate", [P, E0, M], until=layer0)
        w_up = sb("w_up", [P, E0, M], until=layer0)
        w_out = sb("w_out", [P, E0, MT, C], until=layer0)
        b_gu = sb("b_gu", [P, 2, E0 * MT], until=layer0)
        b_out = sb("b_out", [P, 4, C], until=layer0)
        w_router = sb("w_router", [P, E0], until=layer0)

        def gate_program(dve, layer):
            for pair in range(NB // 2):
                n = layer * (NB // 2) + pair
                src = ps[pair % 2]
                dve.wait_ge(gate_abs, n + 1)
                nc.vector.tensor_scalar(gate_sign[:], src[:], 0.0, 0.5, ALU.is_ge, ALU.subtract).then_inc(gate_steps, 1)
                dve.wait_ge(gate_steps, 2 * n + 1)
                nc.vector.scalar_tensor_tensor(
                    out=gates[:, 2 * pair:2 * pair + 2, :, :].rearrange("p b g c -> p (b g c)"), in0=gate_size[:, pair % 2, :],
                    scalar=0.5, in1=gate_sign[:], op0=ALU.max, op1=ALU.mult).then_inc(gate_steps, 1)
                dve.wait_ge(gate_steps, 2 * n + 2)

        def gate_sizes(act, layer):
            for pair in range(NB // 2):
                n = layer * (NB // 2) + pair
                act.wait_ge(gate_psum, n + 1)
                if pair >= 2:
                    act.wait_ge(gate_steps, 2 * n - 2)
                nc.scalar.activation(gate_size[:, pair % 2, :], ps[pair % 2][:], ACT.Abs, scale=2.0).then_inc(gate_abs, 1)

        def gate_matmuls(pe, layer):
            for pair in range(NB // 2):
                n = layer * (NB // 2) + pair
                if pair >= 2:
                    pe.wait_ge(gate_steps, 2 * n - 2)
                for j in range(2):
                    b = 2 * pair + j
                    last = nc.tensor.matmul(ps[pair % 2][:, j * 2 * C:(j + 1) * 2 * C],
                                            silu_c[:, layer, b:b + 1].to_broadcast([P, P]),
                                            w_mod[:, layer, 4:6, :].rearrange("p j c -> p (j c)"),
                                            start=True, stop=True)
                last.then_inc(gate_psum, 1)

        with nc.Block() as block:
            @block.sync
            def _(sp):
                for name, t in (("cT", c_t), ("wmod", w_mod)):
                    sp.dma_start(t[:], a[name]).then_inc(small_in, 16)
                xv = a["x"].rearrange("b (h p) c -> p b h c", p=P)
                for q in range(4):
                    sp.dma_start(x[:, 4 * q:4 * q + 4], xv[:, 4 * q:4 * q + 4]).then_inc(x_in, 16)
                sp.wait_ge(x_in, 64)
                sp.wait_ge(l0_in, 16 * 8)

            @block.gpsimd
            def _(pool):
                for name, t in (("const_eye", eye), ("const_rope", rope), ("const_masks", masks),
                                ("const_window", window_f), ("const_pick", pick_f), ("const_order", order),
                                ("wqkv0", w_qkv0), ("wproj0", w_proj0)):
                    pool.dma_start(t[:], a[name]).then_inc(l0_in, 16)
                token_scales(pool, 0)

            @block.scalar
            def _(act):
                act.wait_ge(small_in, 32)
                nc.scalar.activation(silu_c[:], c_t[:], ACT.Silu).then_inc(silu_done, 1)
                gate_sizes(act, 0)
                for name, t in (("wgate", w_gate), ("wup", w_up), ("wout", w_out), ("bgu", b_gu), ("bout", b_out),
                                ("wrouter", w_router)) + tuple(l1.items()):
                    act.dma_start(t[:], a[name]).then_inc(all_in, 16)

            @block.tensor
            def _(pe):
                pe.wait_ge(silu_done, 1)
                for layer in range(2):
                    for j in range(4):
                        last = nc.tensor.matmul(ps[2][:, (layer * 4 + j) * NB:(layer * 4 + j + 1) * NB],
                                                w_mod[:, layer, j, :], silu_c[:, layer, :], start=True, stop=True)
                last.then_inc(mod_psum, 1)
                gate_matmuls(pe, 0)

            @block.vector
            def _(dve):
                nc.vector.memset(minus_half[:], -0.5)
                dve.wait_ge(mod_psum, 1)
                pm = ps[2][:, 0:8 * NB].rearrange("p (l j b) -> p l j b", l=2, j=4)
                nc.vector.tensor_copy(mod[:, :, 0, :], pm[:, :, 0, :])
                nc.vector.tensor_scalar(mod[:, :, 1, :], pm[:, :, 1, :], 1.0, None, ALU.add)
                nc.vector.tensor_copy(mod[:, :, 2, :], pm[:, :, 2, :])
                nc.vector.tensor_scalar(mod[:, :, 3, :], pm[:, :, 3, :], 1.0, None, ALU.add).then_inc(mod_done, 1)
                gate_program(dve, 0)
                dve.wait_ge(l0_in, 16 * 8)
                nc.vector.tensor_copy(window_bf[:].rearrange("p v q -> p (v q)"), window_f[:])
                nc.vector.tensor_copy(pick_bf[:], pick_f[:]).then_inc(const_done, 1)
                dve.wait_ge(x_in, 64)
                with dve.Fori(0, NB) as b:
                    for h in range(NHALF):
                        last = nc.vector.bn_stats(stats[:, b, h, :], x[:, b, h, :])
                    last.then_inc(st_done, 1)
                dve.wait_ge(st_done, NB)
                token_variances(dve, 0)

        phase = ExitStack()
        h_t = sb("h_t", [P, WINDOW + T], until=phase)
        rope_c = sb("rope_c", [P, 512], until=phase)
        rope_s = sb("rope_s", [P, 512], until=phase)
        qk = sb("qk", [P, 512], until=phase)
        q_m = sb("q_m", [P, 2, NQB, HPG, QB], until=phase)
        k_m = sb("k_m", [P, 2, HG, WINDOW + T], until=phase)
        v_win = sb("v_win", [WIN, 2, NQB, C], until=phase)
        negmax = sb("negmax", [P, NQB, HG], until=phase)
        esum = sb("esum", [P, NQB, HG], until=phase)
        rsum = sb("rsum", [P, NQB, HG], until=phase)
        p_exp = sb("p_exp", [P, 2, HG, WIN], until=phase)
        p_nrm = sb("p_nrm", [P, 2, HG, WIN], until=phase)
        p_t = sb("p_t", [WIN, 2, HG * P], until=phase)
        y_t = sb("y_t", [P, T], until=phase)
        upd = sb("upd", [P, NHALF, C], until=phase)
        ACT_QB = (3, 7)
        s0 = {n: sem("a0_" + n) for n in (
            "pads", "xn", "x_t", "h_t", "qk_psum", "v_psum", "v_sb", "rope_mul", "rope", "masked", "scores", "negmax",
            "exp", "rsum", "p_nrm", "p_t_psum", "p_t_dve", "p_t_act", "pv", "y_part", "y", "proj", "upd", "x1", "st")}

        def p_t_ready(eng, b, qb):
            if qb in ACT_QB:
                eng.wait_ge(s0["p_t_act"], len(ACT_QB) * b + ACT_QB.index(qb) + 1)
            else:
                before = sum(q in ACT_QB for q in range(qb))
                eng.wait_ge(s0["p_t_dve"], (NQB - len(ACT_QB)) * b + qb - before + 1)

        def entries(eng, entry):
            entry(0, 0, False, True)
            with eng.Fori(0, NB // 2 - 1) as pair:
                entry(2 * pair + 1, 1, True, True)
                entry(2 * pair + 2, 0, True, True)
            entry(NB - 1, 1, True, False)

        with nc.Block() as block:
            @block.tensor
            def _(pe):
                def to_channels(b):
                    pe.wait_ge(s0["xn"], b + 1)
                    for h in range(NHALF):
                        last = nc.tensor.transpose(ps[1][:, h * P:(h + 1) * P], xn[:, h, :], eye[:])
                    last.then_inc(s0["x_t"], 1)

                def project_qk(b):
                    pe.wait_ge(s0["h_t"], b + 1)
                    for j in range(4):
                        last = nc.tensor.matmul(ps[j // 2][:, (j % 2) * T:(j % 2 + 1) * T], w_qkv0[:, j, :],
                                                h_t[:, WINDOW:], start=True, stop=True)
                    last.then_inc(s0["qk_psum"], 1)

                def project_v(b):
                    pe.wait_ge(s0["rope_mul"], b + 1)
                    for qb in range(NQB):
                        last = nc.tensor.matmul(ps[qb // 4][0:WIN, (qb % 4) * C:(qb % 4 + 1) * C],
                                                h_t[:, qb * QB:qb * QB + WIN], w_qkv0[:, 4, :], start=True, stop=True)
                    last.then_inc(s0["v_psum"], 1)

                def finish(b):
                    pe.wait_ge(s0["y"], b + 1)
                    for h in range(NHALF):
                        last = nc.tensor.matmul(ps[0][:, h * P:(h + 1) * P], y_t[:, h * P:(h + 1) * P], w_proj0[:],
                                                start=True, stop=True)
                    last.then_inc(s0["proj"], 1)

                def entry(b, buf, former, has_next):
                    def scores(qb):
                        if former or qb >= 2:
                            pe.wait_ge(s0["exp"], NQB * b + qb - 1)
                        pst = ps[2 + qb % 2][:, 0:HG * WIN]
                        nc.tensor.matmul(pst, window_bf[:, min(qb, 2), :], pick_bf[:], start=True, stop=False)
                        nc.tensor.matmul(pst, q_m[:, buf, qb, :, :].rearrange("p h q -> p (h q)"),
                                         k_m[:, buf, :, qb * QB:qb * QB + WIN], start=False,
                                         stop=True).then_inc(s0["scores"], 1)

                    def attend(qb):
                        p_t_ready(pe, b, qb)
                        for g in range(HG):
                            last = nc.tensor.matmul(po[g * 32:(g + 1) * 32, qb * P:(qb + 1) * P],
                                                    v_win[:, buf, qb, g * 32:(g + 1) * 32],
                                                    p_t[:, qb % 2, g * P:(g + 1) * P], start=True, stop=True)
                        last.then_inc(s0["pv"], 1)

                    pe.wait_ge(s0["masked"], b + 1)
                    scores(0)
                    scores(1)
                    pe.wait_ge(s0["v_sb"], 2 * b + 2)
                    for qb in range(NQB):
                        if qb == 0 and former:
                            finish(b - 1)
                        if qb == 1 and has_next:
                            to_channels(b + 1)
                        if qb == 2 and has_next:
                            if former:
                                pe.wait_ge(s0["upd"], b)
                            project_qk(b + 1)
                        if qb == 5 and has_next:
                            project_v(b + 1)
                        if qb + 2 < NQB:
                            scores(qb + 2)
                        pe.wait_ge(s0["p_nrm"], NQB * b + qb + 1)
                        for g in range(HG):
                            last = nc.tensor.transpose(ps[4 + qb % 2][0:WIN, g * P:(g + 1) * P], p_nrm[:, qb % 2, g, :],
                                                       eye[:])
                        last.then_inc(s0["p_t_psum"], 1)
                        if qb >= 1:
                            attend(qb - 1)
                    attend(NQB - 1)

                pe.wait_ge(s0["pads"], 1)
                to_channels(0)
                project_qk(0)
                project_v(0)
                entries(pe, entry)
                finish(NB - 1)

            @block.scalar
            def _(act):
                def modulate(b):
                    act.wait_ge(s0["x_t"], b + 1)
                    nc.scalar.activation(h_t[:, WINDOW:], ps[1][:, 0:T], ACT.Identity, scale=mod[:, 0, 1, bass.ds(b, 1)],
                                         bias=mod[:, 0, 0, bass.ds(b, 1)]).then_inc(s0["h_t"], 1)

                def values(b, buf):
                    act.wait_ge(s0["v_psum"], b + 1)
                    for i in range(2):
                        nc.scalar.copy(v_win[:, buf, 4 * i:4 * i + 4, :].rearrange("p q c -> p (q c)"),
                                       ps[i][0:WIN, :]).then_inc(s0["v_sb"], 1)

                def entry(b, buf, former, has_next):
                    for qb in range(NQB):
                        act.wait_ge(s0["negmax"], NQB * b + qb + 1)
                        if former or qb >= 2:
                            act.wait_ge(s0["p_nrm"], NQB * b + qb - 1)
                        for g in range(HG):
                            last = nc.scalar.activation(p_exp[:, qb % 2, g, :], ps[2 + qb % 2][:, g * WIN:(g + 1) * WIN],
                                                        ACT.Exp, bias=negmax[:, qb, g:g + 1],
                                                        accum_out=esum[:, qb, g:g + 1])
                        last.then_inc(s0["exp"], 1)
                        if qb == 1 and has_next:
                            modulate(b + 1)
                        if qb == 6 and has_next:
                            values(b + 1, 1 - buf)
                        for k in (qb - 1, qb):
                            if k in ACT_QB and (k == qb - 1 or qb == NQB - 1):
                                act.wait_ge(s0["p_t_psum"], NQB * b + k + 1)
                                if former or k >= 2:
                                    act.wait_ge(s0["pv"], NQB * b + k - 1)
                                nc.scalar.copy(p_t[:, k % 2, :], ps[4 + k % 2][0:WIN, :]).then_inc(s0["p_t_act"], 1)

                modulate(0)
                values(0, 0)
                entries(act, entry)

            @block.gpsimd
            def _(pool):
                def rotate(b):
                    pool.wait_ge(s0["rope_mul"], b + 1)
                    nc.gpsimd.tensor_tensor(qk[:], rope_c[:], rope_s[:], ALU.add).then_inc(s0["rope"], 1)

                def entry(b, buf, former, has_next):
                    for qb in range(NQB):
                        pool.wait_ge(s0["rsum"], NQB * b + qb + 1)
                        if former or qb >= 2:
                            pool.wait_ge(s0["p_t_psum"], NQB * b + qb - 1)
                        nc.gpsimd.tensor_tensor(p_nrm[:, qb % 2], p_exp[:, qb % 2],
                                                rsum[:, qb, :].unsqueeze(2).to_broadcast([P, HG, WIN]),
                                                ALU.mult).then_inc(s0["p_nrm"], 1)
                        if qb == 4 and has_next:
                            rotate(b + 1)

                rotate(0)
                entries(pool, entry)
                token_scales(pool, 1)

            @block.vector
            def _(dve):
                def normalise(b):
                    for h in range(NHALF):
                        last = nc.vector.tensor_scalar(xn[:, h, :], x[:, b, h, :], mean[:, b, h:h + 1],
                                                       rstd[:, b, h:h + 1], ALU.subtract, ALU.mult)
                    last.then_inc(s0["xn"], 1)

                def rope_products(b):
                    dve.wait_ge(s0["qk_psum"], b + 1)
                    nc.vector.tensor_tensor(rope_c[:], ps[0][:], rope[:, 0:2, :].rearrange("p j t -> p (j t)"), ALU.mult)
                    nc.vector.tensor_tensor(rope_s[:], ps[1][:], rope[:, 2:4, :].rearrange("p j t -> p (j t)"),
                                            ALU.mult).then_inc(s0["rope_mul"], 1)

                def mask_queries(b, buf):
                    dve.wait_ge(s0["rope"], b + 1)
                    for i in range(HPG):
                        nc.vector.tensor_scalar(q_m[:, buf, :, i, :], qk[:, 0:T].rearrange("p (n q) -> p n q", q=QB),
                                                masks[:, i:i + 1], None, ALU.mult)

                def mask_keys(b, buf):
                    for g in range(HG):
                        last = nc.vector.tensor_scalar(k_m[:, buf, g, WINDOW:], qk[:, T:], masks[:, HG + g:HG + g + 1],
                                                       None, ALU.mult)
                    last.then_inc(s0["masked"], 1)

                def heads_out(b):
                    dve.wait_ge(s0["pv"], NQB * b + NQB)
                    o4 = po[:].rearrange("p (n h q) -> p h n q", h=HPG, q=QB)
                    yv = y_t[:].rearrange("p (n q) -> p n q", q=QB)
                    nc.vector.tensor_scalar(yv, o4[:, 0], masks[:, 0:1], None, ALU.mult).then_inc(s0["y_part"], 1)
                    for i in range(1, HPG):
                        dve.wait_ge(s0["y_part"], (HPG - 1) * b + i)
                        last = nc.vector.scalar_tensor_tensor(out=yv, in0=o4[:, i], scalar=masks[:, i:i + 1], in1=yv,
                                                              op0=ALU.mult, op1=ALU.add)
                        last.then_inc(s0["y_part" if i < HPG - 1 else "y"], 1)

                def gate_update(b):
                    dve.wait_ge(s0["proj"], b + 1)
                    nc.vector.tensor_tensor(upd[:], ps[0][:, 0:T].rearrange("p (h c) -> p h c", h=NHALF),
                                            gates[:, bass.ds(b, 1), 0, :].to_broadcast([P, NHALF, C]),
                                            ALU.mult).then_inc(s0["upd"], 1)

                def add_update(b):
                    dve.wait_ge(s0["upd"], b + 1)
                    nc.vector.tensor_tensor(x[:, b], x[:, b], upd[:], ALU.add).then_inc(s0["x1"], 1)

                def statistics(b):
                    for h in range(NHALF):
                        last = nc.vector.bn_stats(stats[:, b, h, :], x[:, b, h, :])
                    last.then_inc(s0["st"], 1)

                def entry(b, buf, former, has_next):
                    def maximum(qb):
                        dve.wait_ge(s0["scores"], NQB * b + qb + 1)
                        nc.vector.tensor_reduce(negmax[:, qb, :],
                                                ps[2 + qb % 2][:, 0:HG * WIN].rearrange("p (g k) -> p g k", g=HG),
                                                AX.X, ALU.max, negate=True).then_inc(s0["negmax"], 1)

                    def from_psum(qb):
                        dve.wait_ge(s0["p_t_psum"], NQB * b + qb + 1)
                        if former or qb >= 2:
                            dve.wait_ge(s0["pv"], NQB * b + qb - 1)
                        nc.vector.tensor_copy(p_t[:, qb % 2, :], ps[4 + qb % 2][0:WIN, :]).then_inc(s0["p_t_dve"], 1)

                    if former:
                        heads_out(b - 1)
                    maximum(0)
                    maximum(1)
                    if has_next:
                        normalise(b + 1)
                    for qb in range(NQB):
                        dve.wait_ge(s0["exp"], NQB * b + qb + 1)
                        if qb == 4 and former:
                            dve.wait_ge(s0["x1"], b)
                        nc.vector.reciprocal(rsum[:, qb, :], esum[:, qb, :]).then_inc(s0["rsum"], 1)
                        if qb == 4 and former:
                            statistics(b - 1)
                        if qb >= 1 and qb - 1 not in ACT_QB:
                            from_psum(qb - 1)
                        if qb + 2 < NQB:
                            maximum(qb + 2)
                        if qb == 1 and former:
                            gate_update(b - 1)
                        if qb == 2 and former:
                            add_update(b - 1)
                        if qb == 3 and has_next:
                            rope_products(b + 1)
                        if qb == 5 and has_next:
                            mask_queries(b + 1, 1 - buf)
                        if qb == 6 and has_next:
                            mask_keys(b + 1, 1 - buf)
                    if NQB - 1 not in ACT_QB:
                        from_psum(NQB - 1)

                nc.vector.memset(h_t[:, 0:WINDOW], 0.0)
                for buf in range(2):
                    last = nc.vector.memset(k_m[:, buf, :, 0:WINDOW], 0.0)
                last.then_inc(s0["pads"], 1)
                normalise(0)
                rope_products(0)
                mask_queries(0, 0)
                mask_keys(0, 0)
                entries(dve, entry)
                heads_out(NB - 1)
                gate_update(NB - 1)
                add_update(NB - 1)
                dve.wait_ge(s0["x1"], NB)
                statistics(NB - 1)
                dve.wait_ge(s0["st"], NB)
                token_variances(dve, 1)
        phase.close()

        phase = ExitStack()
        CH = 4
        NCH = NB * NHALF // CH
        xn4 = sb("xn4", [P, CH, C], until=phase)
        h4 = sb("h4", [P, CH * P], until=phase)
        logit_max = sb("logit_max", [P, CH], until=phase)
        prob = sb("prob", [P, CH, E0], until=phase)
        prob_sum = sb("prob_sum", [P, CH], until=phase)
        hit = sb("hit", [P, CH, E0], until=phase)
        rank = sb("rank", [P, CH, E0], until=phase)
        rank_max = sb("rank_max", [P, CH], until=phase)
        first = sb("first", [P, CH, E0], until=phase)
        second = sb("second", [P, CH, E0], until=phase)
        left = sb("left", [P, CH, E0], until=phase)
        top = sb("top", [P, 2, CH], until=phase)
        top_sum = sb("top_sum", [P, CH], until=phase)
        w_exp = sb("w_exp", [P, P], until=phase)
        w_exp_t = sb("w_exp_t", [P, P], until=phase)
        act_g = sb("act_g", [P, 2, CH * P], until=phase)
        hid = sb("hid", [P, 2, MT, CH * P], until=phase)
        acc = sb("acc", [P, CH, C], until=phase)

        ROUTE_STEPS = 4 + 5 + 6 + 7
        s1 = {n: sem("e0_" + n) for n in (
            "zero", "chain", "xn", "x_t", "h", "logits", "route", "prob", "w", "w_t_psum", "w_t", "bias", "acc0", "gate_up", "silu",
            "hid", "out", "acc", "upd", "x2", "st")}

        with nc.Block() as block:
            @block.sync
            def _(sp):
                sp.wait_ge(all_in, 16 * (6 + len(l1)))

            @block.tensor
            def _(pe):
                pe.wait_ge(all_in, 16 * (6 + len(l1)))
                with pe.Fori(0, NCH) as c:
                    pe.wait_ge(s1["xn"], c + 1)
                    for t in range(CH):
                        last = nc.tensor.transpose(ps[0][:, t * P:(t + 1) * P], xn4[:, t, :], eye[:])
                    last.then_inc(s1["x_t"], 1)
                    pe.wait_ge(s1["h"], 2 * c + 2)
                    for t in range(CH):
                        last = nc.tensor.matmul(ps[1][:, t * E0:(t + 1) * E0], h4[:, t * P:(t + 1) * P], w_router[:],
                                                start=True, stop=True)
                    last.then_inc(s1["logits"], 1)

                    def gate_up(k):
                        if k >= 2:
                            pe.wait_ge(s1["hid"], E0 * MT * c + k - 1)
                        for j, w in enumerate((w_gate, w_up)):
                            last = nc.tensor.matmul(ps[2 + 2 * j + k % 2][:], w[:, k // MT, (k % MT) * P:(k % MT + 1) * P],
                                                    h4[:], start=True, stop=True)
                        last.then_inc(s1["gate_up"], 1)

                    def down(e):
                        pe.wait_ge(s1["hid"], E0 * MT * c + MT * (e + 1))
                        if e >= 2:
                            pe.wait_ge(s1["acc"], E0 * c + e - 1)
                        for t in range(CH):
                            for m in range(MT):
                                last = nc.tensor.matmul(po[:, (e % 2) * 512 + t * C:(e % 2) * 512 + (t + 1) * C],
                                                        hid[:, e % 2, m, t * P:(t + 1) * P], w_out[:, e, m, :],
                                                        start=(m == 0), stop=(m == MT - 1))
                        last.then_inc(s1["out"], 1)

                    for e in range(E0):
                        for m in range(MT):
                            gate_up(MT * e + m)
                        if e == 1:
                            pe.wait_ge(s1["w"], c + 1)
                            nc.tensor.transpose(ps[1][:, 0:P], w_exp[:], eye[:]).then_inc(s1["w_t_psum"], 1)
                            pe.wait_ge(s1["w_t"], c + 1)
                            for t in range(CH):
                                last = nc.tensor.matmul(ps[0][:, t * C:(t + 1) * C], w_exp_t[:], b_out[:, t, :],
                                                        start=True, stop=True)
                            last.then_inc(s1["bias"], 1)
                        if e >= 1:
                            down(e - 1)
                    down(E0 - 1)

            @block.scalar
            def _(act):
                with act.Fori(0, NCH) as c:
                    act.wait_ge(s1["x_t"], c + 1)
                    for j in range(2):
                        b = 2 * c + j
                        nc.scalar.activation(h4[:, j * T:(j + 1) * T], ps[0][:, j * T:(j + 1) * T], ACT.Identity,
                                             scale=mod[:, 0, 3, bass.ds(b, 1)],
                                             bias=mod[:, 0, 2, bass.ds(b, 1)]).then_inc(s1["h"], 1)
                    act.wait_ge(s1["route"], c + 1)
                    nc.scalar.activation(prob[:], hit[:], ACT.Exp).then_inc(s1["prob"], 1)
                    for k in range(E0 * MT):
                        act.wait_ge(s1["gate_up"], E0 * MT * c + k + 1)
                        nc.scalar.activation(act_g[:, k % 2, :], ps[2 + k % 2][:], ACT.Silu,
                                             bias=b_gu[:, 0, k:k + 1]).then_inc(s1["silu"], 1)
                        if k == 3:
                            act.wait_ge(s1["bias"], c + 1)
                            nc.scalar.copy(acc[:].rearrange("p t c -> p (t c)"), ps[0][:]).then_inc(s1["acc0"], 1)

            @block.vector
            def _(dve):
                nc.vector.memset(w_exp[:], 0.0).then_inc(s1["zero"], 1)
                dve.wait_ge(s1["zero"], 1)
                with dve.Fori(0, NCH) as c:
                    for t in range(CH):
                        b = 2 * c + t // 2
                        last = nc.vector.tensor_scalar(xn4[:, t, :], x[:, b, t % 2, :], mean[:, b, t % 2:t % 2 + 1],
                                                       rstd[:, b, t % 2:t % 2 + 1], ALU.subtract, ALU.mult)
                    last.then_inc(s1["xn"], 1)
                    dve.wait_ge(s1["logits"], c + 1)
                    lg = ps[1][:, 0:CH * E0].rearrange("p (t e) -> p t e", e=E0)
                    wide = lambda v: v.unsqueeze(2).to_broadcast([P, CH, E0])
                    steps = [0]

                    def chain(ins):
                        steps[0] += 1
                        ins.then_inc(s1["chain"], 1)
                        dve.wait_ge(s1["chain"], ROUTE_STEPS * c + steps[0])

                    chain(nc.vector.tensor_reduce(logit_max[:], lg, AX.X, ALU.max))
                    nc.vector.tensor_tensor(hit[:], lg, wide(logit_max[:]), ALU.subtract).then_inc(s1["route"], 1)
                    dve.wait_ge(s1["prob"], c + 1)
                    chain(nc.vector.tensor_reduce(prob_sum[:], prob[:], AX.X, ALU.add))
                    chain(nc.vector.reciprocal(prob_sum[:], prob_sum[:]))
                    chain(nc.vector.tensor_tensor(prob[:], prob[:], wide(prob_sum[:]), ALU.mult))
                    src = prob
                    for j, mark in enumerate((first, second)):
                        chain(nc.vector.tensor_reduce(top[:, j, :], src[:], AX.X, ALU.max))
                        chain(nc.vector.tensor_tensor(hit[:], src[:], wide(top[:, j, :]), ALU.is_equal))
                        chain(nc.vector.tensor_tensor(rank[:], hit[:], order[:].unsqueeze(1).to_broadcast([P, CH, E0]),
                                                      ALU.mult))
                        chain(nc.vector.tensor_reduce(rank_max[:], rank[:], AX.X, ALU.max))
                        chain(nc.vector.tensor_tensor(mark[:], rank[:], wide(rank_max[:]), ALU.is_equal))
                        if j == 0:
                            chain(nc.vector.scalar_tensor_tensor(out=left[:], in0=mark[:], scalar=-2.0, in1=src[:],
                                                                 op0=ALU.mult, op1=ALU.add))
                            src = left
                    chain(nc.vector.tensor_tensor(top_sum[:], top[:, 0, :], top[:, 1, :], ALU.add))
                    chain(nc.vector.tensor_scalar(top_sum[:], top_sum[:], 1e-8, None, ALU.add))
                    chain(nc.vector.reciprocal(top_sum[:], top_sum[:]))
                    for j in range(2):
                        chain(nc.vector.tensor_tensor(top[:, j, :], top[:, j, :], top_sum[:], ALU.mult))
                    chain(nc.vector.tensor_tensor(first[:], first[:], wide(top[:, 0, :]), ALU.mult))
                    chain(nc.vector.tensor_tensor(second[:], second[:], wide(top[:, 1, :]), ALU.mult))
                    assert steps[0] == ROUTE_STEPS
                    nc.vector.tensor_tensor(w_exp[:, 0:CH * E0].rearrange("p (t e) -> p t e", e=E0), first[:], second[:],
                                            ALU.add).then_inc(s1["w"], 1)

                    def hidden(k):
                        dve.wait_ge(s1["silu"], E0 * MT * c + k + 1)
                        if k // MT >= 2:
                            dve.wait_ge(s1["out"], E0 * c + k // MT - 1)
                        nc.vector.scalar_tensor_tensor(out=hid[:, k // MT % 2, k % MT, :], in0=ps[4 + k % 2][:],
                                                       scalar=b_gu[:, 1, k:k + 1], in1=act_g[:, k % 2, :],
                                                       op0=ALU.add, op1=ALU.mult).then_inc(s1["hid"], 1)

                    def accumulate(e):
                        dve.wait_ge(s1["out"], E0 * c + e + 1)
                        for t in range(CH):
                            last = nc.vector.scalar_tensor_tensor(
                                out=acc[:, t, :], in0=po[:, (e % 2) * 512 + t * C:(e % 2) * 512 + (t + 1) * C],
                                scalar=w_exp[:, t * E0 + e:t * E0 + e + 1], in1=acc[:, t, :], op0=ALU.mult, op1=ALU.add)
                        last.then_inc(s1["acc"], 1)

                    for k in range(E0 * MT):
                        if k == 3:
                            dve.wait_ge(s1["w_t_psum"], c + 1)
                            nc.vector.tensor_copy(w_exp_t[:], ps[1][:, 0:P]).then_inc(s1["w_t"], 1)
                        hidden(k)
                        if k % MT == 0 and k >= 2 * MT:
                            if k == 2 * MT:
                                dve.wait_ge(s1["acc0"], c + 1)
                            else:
                                dve.wait_ge(s1["acc"], E0 * c + k // MT - 2)
                            accumulate(k // MT - 2)
                    for e in (E0 - 2, E0 - 1):
                        dve.wait_ge(s1["acc"], E0 * c + e)
                        accumulate(e)
                    dve.wait_ge(s1["acc"], E0 * (c + 1))
                    for j in range(2):
                        last = nc.vector.tensor_tensor(acc[:, 2 * j:2 * j + 2, :], acc[:, 2 * j:2 * j + 2, :],
                                                       gates[:, bass.ds(2 * c + j, 1), 1, :].to_broadcast([P, 2, C]),
                                                       ALU.mult)
                    last.then_inc(s1["upd"], 1)
                    dve.wait_ge(s1["upd"], c + 1)
                    xc = x[:, bass.ds(2 * c, 2), :, :].rearrange("p b h c -> p (b h) c")
                    nc.vector.tensor_tensor(xc, xc, acc[:], ALU.add).then_inc(s1["x2"], 1)
                    dve.wait_ge(s1["x2"], c + 1)
                    dve.wait_ge(const_done, 1)
                    for t in range(CH):
                        last = nc.vector.bn_stats(stats[:, 2 * c + t // 2, t % 2, :], x[:, 2 * c + t // 2, t % 2, :])
                    last.then_inc(s1["st"], 1)
                dve.wait_ge(s1["st"], NCH)
                token_variances(dve, 2)

            @block.gpsimd
            def _(pool):
                token_scales(pool, 2)
        phase.close()
        layer0.close()

        phase = ExitStack()
        xn1 = sb("xn1", [P, 2, C], until=phase)
        h1t = sb("h1t", [P, 2, P], until=phase)
        q1_t = sb("q1_t", [P, 2, P], until=phase)
        qkv = sb("qkv", [P, NHALF, NB, 3, C], until=phase)
        rel = sb("rel", [P, NB, H, NB], until=phase)
        prod_s = sb("prod_s", [P, 2, D, H, NB], until=phase)
        score = sb("score", [P, 2, H, NB], until=phase)
        e1 = sb("e1", [P, 2, H, NB], until=phase)
        e1_t = sb("e1_t", [P, 2 * P], until=phase)
        smax = sb("smax", [P, H], until=phase)
        ssum = sb("ssum", [P, 2, H], until=phase)
        sinv = sb("sinv", [P, 2, H], until=phase)
        prod_v = sb("prod_v", [P, 2, H, D, NB], until=phase)
        mix = sb("mix", [P, C], until=phase)
        mix_rel = sb("mix_rel", [P, C], until=phase)
        att = sb("att", [P, C], until=phase)
        att_t = sb("att_t", [P, P], until=phase)
        upd1 = sb("upd1", [P, 2, C], until=phase)
        SCALE1 = float(D) ** -0.5
        POOL_HEADS = 6

        s2 = {n: sem("a1_" + n) for n in (
            "xn", "x_t", "h", "q_psum", "qkv_psum", "q_t", "qkv", "rel_psum", "rel", "prod_s", "dots", "max", "score",
            "exp", "sum", "inv", "e_t_psum", "e_t", "rv", "prod_v_dve", "prod_v_pool", "mix", "mix_rel", "att",
            "att_t_psum", "att_t", "proj", "upd", "gated", "x3", "st")}
        rk = l1["rk"]

        def projections(eng, load, project):
            load(0, 0, 0)
            load(0, 1, 1)
            project(0, 0, 0)
            load(0, 2, 0)
            project(0, 1, 1)
            with eng.Fori(0, NB // 2 - 2) as pair:
                load(0, 2 * pair + 3, 1)
                project(0, 2 * pair + 2, 0)
                load(0, 2 * pair + 4, 0)
                project(0, 2 * pair + 3, 1)
            load(0, NB - 1, 1)
            project(0, NB - 2, 0)
            project(0, NB - 1, 1)

        def attention(eng, step):
            step(0, 0, 0, None, None)
            step(0, 1, 1, (0, 0), None)
            step(0, 2, 0, (0, 1), (0, 0))
            step(0, 3, 1, (0, 2), (0, 1))
            with eng.Fori(0, NB // 2 - 2) as pair:
                step(0, 2 * pair + 4, 0, (0, 2 * pair + 3), (0, 2 * pair + 2))
                step(0, 2 * pair + 5, 1, (0, 2 * pair + 4), (0, 2 * pair + 3))
            step(1, 0, 0, (0, NB - 1), (0, NB - 2))
            step(1, 1, 1, (1, 0), (0, NB - 1))
            with eng.Fori(0, NB // 2 - 1) as pair:
                step(1, 2 * pair + 2, 0, (1, 2 * pair + 1), (1, 2 * pair))
                step(1, 2 * pair + 3, 1, (1, 2 * pair + 2), (1, 2 * pair + 1))

        def at(half, t):
            return t + NB * half

        def former(eng, signal, n):
            if not isinstance(n, int) or n > 0:
                eng.wait_ge(s2[signal], n)

        def turned(half):
            return (ps[4] if half == 0 else po)[:, 0:P]

        with nc.Block() as block:
            @block.tensor
            def _(pe):
                def load(half, t, buf):
                    m = at(half, t)
                    former(pe, "h" if half == 0 else "rel", m)
                    pe.wait_ge(s2["xn"], m + 1)
                    nc.tensor.transpose(turned(half), xn1[:, buf, :], eye[:]).then_inc(s2["x_t"], 1)

                def project(half, t, buf):
                    m = at(half, t)
                    former(pe, "rel", m)
                    pe.wait_ge(s2["h"], m + 1)
                    nc.tensor.matmul(po[:, P:2 * P], l1["w_qkv1"][:, 0:C], h1t[:, buf, :], start=True,
                                     stop=True).then_inc(s2["q_psum"], 1)
                    former(pe, "qkv", m)
                    nc.tensor.matmul(po[:, 512:512 + 2 * C], h1t[:, buf, :], l1["w_qkv1"][:, 0:2 * C], start=True, stop=True)
                    pe.wait_ge(s2["q_t"], m + 1)
                    nc.tensor.matmul(po[:, 512 + 2 * C:512 + 3 * C], h1t[:, buf, :], l1["w_qkv1"][:, 2 * C:], start=True,
                                     stop=True).then_inc(s2["qkv_psum"], 1)
                    nc.tensor.matmul(po[:, 2 * P:2 * P + H * NB], q1_t[:, buf, :], rk[:, :, bass.ds(MAXREL - t, NB)],
                                     start=True, stop=True).then_inc(s2["rel_psum"], 1)

                def dots(half, t, buf):
                    n = at(half, t)
                    pe.wait_ge(s2["rel"], NB * (half + 1))
                    pe.wait_ge(s2["prod_s"], n + 1)
                    nc.tensor.matmul(ps[buf][:, 0:H * NB], eye[:], rel[:, t, :, :].rearrange("p h s -> p (h s)"),
                                     start=True, stop=False)
                    for d in range(D):
                        last = nc.tensor.matmul(ps[buf][:, 0:H * NB], eye[:],
                                                prod_s[:, buf, d, :, :].rearrange("p h s -> p (h s)"), start=False,
                                                stop=(d == D - 1))
                    last.then_inc(s2["dots"], 1)

                def turn_exp(half, t, buf):
                    n = at(half, t)
                    pe.wait_ge(s2["exp"], n + 1)
                    for j in range(2):
                        last = nc.tensor.transpose(ps[2][:, j * P:(j + 1) * P],
                                                   e1[:, buf, 8 * j:8 * j + 8, :].rearrange("p h s -> p (h s)"), eye[:])
                    last.then_inc(s2["e_t_psum"], 1)

                def relative_values(half, t):
                    n = at(half, t)
                    pe.wait_ge(s2["e_t"], n + 1)
                    for j in range(2):
                        last = nc.tensor.matmul(ps[3][:, j * 64:(j + 1) * 64], e1_t[:, j * P:(j + 1) * P],
                                                l1["rv"][:, bass.ds(t, 1), :, :], start=True, stop=True)
                    last.then_inc(s2["rv"], 1)

                def turn_att(half, t):
                    n = at(half, t)
                    pe.wait_ge(s2["att"], n + 1)
                    nc.tensor.transpose(ps[4][:, 0:P], att[:], eye[:]).then_inc(s2["att_t_psum"], 1)

                def out_projection(half, t):
                    n = at(half, t)
                    former(pe, "upd", n)
                    pe.wait_ge(s2["att_t"], n + 1)
                    nc.tensor.matmul(ps[5][:, 0:C], att_t[:], l1["w_o1"][:], start=True, stop=True).then_inc(s2["proj"], 1)

                def step(half, t, buf, one, two):
                    if two is not None:
                        pe.wait_ge(s2["score"], at(half, t) - 1)
                    dots(half, t, buf)
                    if half == 0:
                        load(1, t, buf)
                    if one is not None:
                        turn_exp(*one, 1 - buf)
                    if two is not None:
                        turn_att(*two)
                    if half == 0:
                        project(1, t, buf)
                    if one is not None:
                        relative_values(*one)
                    if two is not None:
                        out_projection(*two)

                gate_matmuls(pe, 1)
                projections(pe, load, project)
                attention(pe, step)
                turn_exp(1, NB - 1, 1)
                turn_att(1, NB - 2)
                relative_values(1, NB - 1)
                out_projection(1, NB - 2)
                turn_att(1, NB - 1)
                out_projection(1, NB - 1)

            @block.scalar
            def _(act):
                def load(half, t, buf):
                    m = at(half, t)
                    act.wait_ge(s2["x_t"], m + 1)
                    former(act, "qkv_psum", m - 1)
                    nc.scalar.activation(h1t[:, buf, :], turned(half), ACT.Identity, scale=mod[:, 1, 1, bass.ds(t, 1)],
                                         bias=mod[:, 1, 0, bass.ds(t, 1)]).then_inc(s2["h"], 1)

                def queries(half, t, buf):
                    m = at(half, t)
                    act.wait_ge(s2["q_psum"], m + 1)
                    nc.scalar.activation(q1_t[:, buf, :], po[:, P:2 * P], ACT.Identity,
                                         bias=l1["b_q1"][:]).then_inc(s2["q_t"], 1)

                def relative_part(half, t):
                    m = at(half, t)
                    if half == 1:
                        act.wait_ge(s2["dots"], t + 1)
                    act.wait_ge(s2["rel_psum"], m + 1)
                    nc.scalar.copy(rel[:, t, :, :].rearrange("p h s -> p (h s)"),
                                   po[:, 2 * P:2 * P + H * NB]).then_inc(s2["rel"], 1)

                def project(half, t, buf):
                    queries(half, t, buf)
                    relative_part(half, t)

                def turned_exp(half, t):
                    n = at(half, t)
                    former(act, "rv", n)
                    act.wait_ge(s2["e_t_psum"], n + 1)
                    nc.scalar.copy(e1_t[:], ps[2][:, 0:2 * P]).then_inc(s2["e_t"], 1)

                def turned_att(half, t):
                    n = at(half, t)
                    former(act, "proj", n)
                    act.wait_ge(s2["att_t_psum"], n + 1)
                    nc.scalar.copy(att_t[:], ps[4][:, 0:P]).then_inc(s2["att_t"], 1)

                def step(half, t, buf, one, two):
                    n = at(half, t)
                    if half == 0:
                        load(1, t, buf)
                    if one is not None:
                        turned_exp(*one)
                    if two is not None:
                        turned_att(*two)
                    if half == 0:
                        queries(1, t, buf)
                    if two is not None:
                        act.wait_ge(s2["mix"], n - 1)
                    act.wait_ge(s2["score"], n + 1)
                    nc.scalar.activation(e1[:, buf], score[:, buf], ACT.Exp, scale=SCALE1).then_inc(s2["exp"], 1)
                    if half == 0:
                        relative_part(1, t)

                gate_sizes(act, 1)
                projections(act, load, project)
                attention(act, step)
                turned_exp(1, NB - 1)
                turned_att(1, NB - 2)
                turned_att(1, NB - 1)

            @block.gpsimd
            def _(pool):
                def key_products(half, t, buf):
                    n = at(half, t)
                    qv = qkv[:, half, t, 0, :].rearrange("p (h d) -> p d h", d=D)
                    kv = qkv[:, half, :, 1, :].rearrange("p s (h d) -> p d h s", d=D)
                    nc.gpsimd.tensor_tensor(prod_s[:, buf], qv.unsqueeze(3).to_broadcast([P, D, H, NB]), kv,
                                            ALU.mult).then_inc(s2["prod_s"], 1)

                def value_products(half, t, buf):
                    n = at(half, t)
                    pool.wait_ge(s2["exp"], n + 1)
                    former(pool, "mix", n - 1)
                    nc.gpsimd.tensor_tensor(
                        prod_v[:, buf, 0:POOL_HEADS], e1[:, buf, 0:POOL_HEADS, :].unsqueeze(2).to_broadcast(
                            [P, POOL_HEADS, D, NB]),
                        qkv[:, half, :, 2, 0:POOL_HEADS * D].rearrange("p s (h d) -> p h d s", d=D),
                        ALU.mult).then_inc(s2["prod_v_pool"], 1)

                def step(half, t, buf, one, two):
                    if two is not None:
                        pool.wait_ge(s2["dots"], at(half, t) - 1)
                    pool.wait_ge(s2["qkv"], NB * (half + 1))
                    key_products(half, t, buf)
                    if one is not None:
                        value_products(*one, 1 - buf)

                attention(pool, step)
                value_products(1, NB - 1, 1)
                token_scales(pool, 3)

            @block.vector
            def _(dve):
                def load(half, t, buf):
                    m = at(half, t)
                    former(dve, "x_t", m - 1)
                    nc.vector.tensor_scalar(xn1[:, buf, :], x[:, t, half, :], mean[:, t, half:half + 1],
                                            rstd[:, t, half:half + 1], ALU.subtract, ALU.mult).then_inc(s2["xn"], 1)

                def project(half, t, buf):
                    m = at(half, t)
                    dve.wait_ge(s2["qkv_psum"], m + 1)
                    nc.vector.tensor_tensor(qkv[:, half, t, :, :].rearrange("p j c -> p (j c)"),
                                            po[:, 512:512 + 3 * C], l1["b_qkv1"][:], ALU.add).then_inc(s2["qkv"], 1)

                def maximum(half, t, buf):
                    n = at(half, t)
                    dve.wait_ge(s2["dots"], n + 1)
                    nc.vector.tensor_reduce(smax[:], ps[buf][:, 0:H * NB].rearrange("p (h s) -> p h s", s=NB), AX.X,
                                            ALU.max).then_inc(s2["max"], 1)

                def subtract(half, t, buf):
                    n = at(half, t)
                    dve.wait_ge(s2["max"], n + 1)
                    nc.vector.tensor_tensor(score[:, buf], ps[buf][:, 0:H * NB].rearrange("p (h s) -> p h s", s=NB),
                                            smax[:].unsqueeze(2).to_broadcast([P, H, NB]),
                                            ALU.subtract).then_inc(s2["score"], 1)

                def exp_sums(half, t, buf):
                    n = at(half, t)
                    dve.wait_ge(s2["exp"], n + 1)
                    nc.vector.tensor_reduce(ssum[:, buf], e1[:, buf], AX.X, ALU.add).then_inc(s2["sum"], 1)

                def value_products(half, t, buf):
                    n = at(half, t)
                    rest = H - POOL_HEADS
                    nc.vector.tensor_tensor(
                        prod_v[:, buf, POOL_HEADS:], e1[:, buf, POOL_HEADS:, :].unsqueeze(2).to_broadcast([P, rest, D, NB]),
                        qkv[:, half, :, 2, POOL_HEADS * D:].rearrange("p s (h d) -> p h d s", d=D),
                        ALU.mult).then_inc(s2["prod_v_dve"], 1)

                def inverse(half, t, buf):
                    n = at(half, t)
                    dve.wait_ge(s2["sum"], n + 1)
                    nc.vector.reciprocal(sinv[:, buf], ssum[:, buf]).then_inc(s2["inv"], 1)

                def mix_values(half, t, buf):
                    n = at(half, t)
                    dve.wait_ge(s2["prod_v_dve"], n + 1)
                    dve.wait_ge(s2["prod_v_pool"], n + 1)
                    nc.vector.tensor_reduce(mix[:], prod_v[:, buf].rearrange("p h d s -> p (h d) s"), AX.X,
                                            ALU.add).then_inc(s2["mix"], 1)

                def add_relative(half, t):
                    n = at(half, t)
                    dve.wait_ge(s2["mix"], n + 1)
                    dve.wait_ge(s2["rv"], n + 1)
                    nc.vector.tensor_tensor(mix_rel[:], ps[3][:, 0:C], mix[:], ALU.add).then_inc(s2["mix_rel"], 1)

                def divide(half, t, buf):
                    n = at(half, t)
                    former(dve, "att_t_psum", n)
                    dve.wait_ge(s2["inv"], n + 1)
                    dve.wait_ge(s2["mix_rel"], n + 1)
                    nc.vector.tensor_tensor(att[:].rearrange("p (h d) -> p h d", d=D),
                                            mix_rel[:].rearrange("p (h d) -> p h d", d=D),
                                            sinv[:, buf].unsqueeze(2).to_broadcast([P, H, D]), ALU.mult).then_inc(s2["att"], 1)

                def add_bias(half, t):
                    n = at(half, t)
                    dve.wait_ge(s2["proj"], n + 1)
                    nc.vector.tensor_tensor(upd1[:, 0], ps[5][:, 0:C], l1["b_o1"][:], ALU.add).then_inc(s2["upd"], 1)

                def gate(half, t):
                    n = at(half, t)
                    dve.wait_ge(s2["upd"], n + 1)
                    nc.vector.tensor_tensor(upd1[:, 1], upd1[:, 0], gates[:, t, 0, :], ALU.mult).then_inc(s2["gated"], 1)

                def add_update(half, t):
                    n = at(half, t)
                    dve.wait_ge(s2["gated"], n + 1)
                    nc.vector.tensor_tensor(x[:, t, half, :], x[:, t, half, :], upd1[:, 1], ALU.add).then_inc(s2["x3"], 1)

                def statistics(half, t):
                    n = at(half, t)
                    dve.wait_ge(s2["x3"], n + 1)
                    dve.wait_ge(const_done, 1)
                    nc.vector.bn_stats(stats[:, t, half, :], x[:, t, half, :]).then_inc(s2["st"], 1)

                def step(half, t, buf, one, two):
                    if half == 0:
                        load(1, t, buf)
                    maximum(half, t, buf)
                    subtract(half, t, buf)
                    if one is not None:
                        mix_values(*one, 1 - buf)
                    if two is not None:
                        add_bias(*two)
                    exp_sums(half, t, buf)
                    if two is not None:
                        gate(*two)
                    value_products(half, t, buf)
                    if two is not None:
                        add_update(*two)
                    inverse(half, t, buf)
                    if one is not None:
                        add_relative(*one)
                    if half == 0:
                        project(1, t, buf)
                    if two is not None:
                        statistics(*two)
                    if one is not None:
                        divide(*one, 1 - buf)

                gate_program(dve, 1)
                projections(dve, load, project)
                attention(dve, step)
                mix_values(1, NB - 1, 1)
                add_bias(1, NB - 2)
                gate(1, NB - 2)
                add_relative(1, NB - 1)
                add_update(1, NB - 2)
                divide(1, NB - 1, 1)
                statistics(1, NB - 2)
                add_bias(1, NB - 1)
                gate(1, NB - 1)
                add_update(1, NB - 1)
                statistics(1, NB - 1)
                dve.wait_ge(s2["st"], NHALF * NB)
                token_variances(dve, 3)
        phase.close()

        phase = ExitStack()
        h_b = sb("h_b", [P, T], until=phase)
        h_all = sb("h_all", [P, NB, T], until=phase)
        enc = sb("enc", [P, 2, T], until=phase)
        diff = sb("diff", [P, 2, 2, T], until=phase)
        losses = sb("losses", [P, NB, E1], until=phase)
        ones = sb("ones", [P, P], until=phase)
        least = sb("least", [P, NB], until=phase)
        is_least = sb("is_least", [P, NB, E1], until=phase)
        chosen = sb("chosen", [P, NB, E1], until=phase)
        base_u = sb("base_u", [P, NHALF, C], until=phase)
        down_m = sb("down_m", [P, R, E1], until=phase)
        down_w = sb("down_w", [P, R], until=phase)
        down_bm = sb("down_bm", [R, E1], until=phase)
        down_b = sb("down_b", [R, 1], until=phase)
        up_m = sb("up_m", [P, C, E1], until=phase)
        up_w = sb("up_w", [P, C], until=phase)
        a_t = sb("a_t", [P, T], until=phase)
        upd2 = sb("upd2", [P, NHALF, C], until=phase)
        s3 = {n: sem("e1_" + n) for n in (
            "init", "argmin", "sq", "xn", "x_t", "h", "kept", "base", "base1", "base2", "x4", "enc_psum", "enc", "rec", "diff", "loss",
            "loss_psum", "route", "down_m", "down_w", "up_m", "up_w", "code", "a_t", "up", "upd", "x5")}
        out_done = sem("out_done")
        NP = E1 // 2

        with nc.Block() as block:
            @block.tensor
            def _(pe):
                with pe.Fori(0, NB) as b:
                    pe.wait_ge(s3["xn"], b + 1)
                    for h in range(NHALF):
                        last = nc.tensor.transpose(ps[0][:, h * P:(h + 1) * P], xn[:, h, :], eye[:])
                    last.then_inc(s3["x_t"], 1)
                    pe.wait_ge(s3["h"], b + 1)
                    for j in range(2):
                        last = nc.tensor.matmul(ps[1][:, j * T:(j + 1) * T], l1["w_d1"][:, j * P:(j + 1) * P], h_b[:],
                                                start=True, stop=True)
                    last.then_inc(s3["enc_psum"], 1)
                    for h in range(NHALF):
                        last = nc.tensor.matmul(ps[0][:, h * C:(h + 1) * C], h_b[:, h * P:(h + 1) * P], l1["w_base"][:],
                                                start=True, stop=True)
                    last.then_inc(s3["base"], 1)
                    pe.wait_ge(s3["enc"], 2 * b + 2)
                    for p in range(NP):
                        if p >= 2:
                            pe.wait_ge(s3["diff"], NP * b + p - 1)
                        for j in range(2):
                            last = nc.tensor.matmul(ps[2 + p % 2][:, j * T:(j + 1) * T], l1["w_d2"][:, 2 * p + j, :],
                                                    enc[:, p // 2, :], start=True, stop=True)
                        last.then_inc(s3["rec"], 1)
                pe.wait_ge(s3["loss"], NB)
                nc.tensor.matmul(ps[4][:, 0:NB * E1], ones[:], losses[:].rearrange("p b e -> p (b e)"), start=True,
                                 stop=True).then_inc(s3["loss_psum"], 1)
                with pe.Fori(0, NB) as b:
                    pe.wait_ge(s3["down_w"], b + 1)
                    nc.tensor.matmul(ps[0][0:R, 0:T], down_w[:], h_all[:, b, :], start=True, stop=True)\
                        .then_inc(s3["code"], 1)
                    pe.wait_ge(s3["a_t"], b + 1)
                    pe.wait_ge(s3["up_w"], b + 2)
                    for h in range(NHALF):
                        last = nc.tensor.matmul(ps[1][:, h * C:(h + 1) * C], a_t[:, h * P:(h + 1) * P], up_w[:],
                                                start=True, stop=True)
                    last.then_inc(s3["up"], 1)

            @block.scalar
            def _(act):
                with act.Fori(0, NB) as b:
                    act.wait_ge(s3["x_t"], b + 1)
                    nc.scalar.activation(h_b[:], ps[0][:, 0:T], ACT.Identity, scale=mod[:, 1, 3, bass.ds(b, 1)],
                                         bias=mod[:, 1, 2, bass.ds(b, 1)]).then_inc(s3["h"], 1)
                    act.wait_ge(s3["enc_psum"], b + 1)
                    for j in range(2):
                        nc.scalar.activation(enc[:, j, :], ps[1][:, j * T:(j + 1) * T], ACT.Relu,
                                             bias=l1["b_d1"][:, j:j + 1]).then_inc(s3["enc"], 1)
                    for p in range(NP):
                        act.wait_ge(s3["diff"], NP * b + p + 1)
                        for j in range(2):
                            last = nc.scalar.activation(diff[:, p % 2, j, :], diff[:, p % 2, j, :], ACT.Square,
                                                        bias=l1["b_d2"][:, 2 * p + j:2 * p + j + 1],
                                                        accum_out=losses[:, b, 2 * p + j:2 * p + j + 1])
                        if p < NP - 1:
                            last.then_inc(s3["sq"], 1)
                        else:
                            last.then_inc(s3["loss"], 1)
                with act.Fori(0, NB) as b:
                    act.wait_ge(s3["code"], b + 1)
                    act.wait_ge(s3["down_w"], b + 1)
                    nc.scalar.activation(a_t[0:R, :], ps[0][0:R, 0:T], ACT.Relu, bias=down_b[:]).then_inc(s3["a_t"], 1)

            @block.gpsimd
            def _(pool):
                with pool.Fori(0, NB) as b:
                    pool.wait_ge(s3["h"], b + 1)
                    nc.gpsimd.tensor_copy(h_all[:, b, :], h_b[:]).then_inc(s3["kept"], 1)
                pool.wait_ge(s3["route"], 4)
                with pool.Fori(0, NB) as b:
                    pool.wait_ge(s3["up_w"], b + 1)
                    nc.gpsimd.tensor_tensor(up_m[:], l1["w_au"][:], chosen[:, b, :].unsqueeze(1).to_broadcast([P, C, E1]),
                                            ALU.mult).then_inc(s3["up_m"], 1)

            @block.vector
            def _(dve):
                nc.vector.memset(ones[:], 1.0)
                nc.vector.memset(a_t[R:P, :], 0.0).then_inc(s3["init"], 1)
                dve.wait_ge(s3["init"], 1)
                nc.vector.memset(a_t[R:R + 1, :], 1.0)
                with dve.Fori(0, NB) as b:
                    for h in range(NHALF):
                        last = nc.vector.tensor_scalar(xn[:, h, :], x[:, b, h, :], mean[:, b, h:h + 1],
                                                       rstd[:, b, h:h + 1], ALU.subtract, ALU.mult)
                    last.then_inc(s3["xn"], 1)
                    for p in range(NP):
                        dve.wait_ge(s3["rec"], NP * b + p + 1)
                        if p >= 2:
                            dve.wait_ge(s3["sq"], (NP - 1) * b + p - 1)
                        nc.vector.tensor_tensor(diff[:, p % 2], ps[2 + p % 2][:].rearrange("p (j t) -> p j t", j=2),
                                                h_b[:].unsqueeze(1).to_broadcast([P, 2, T]),
                                                ALU.subtract).then_inc(s3["diff"], 1)
                    dve.wait_ge(s3["base"], b + 1)
                    nc.vector.tensor_tensor(base_u[:], ps[0][:, 0:T].rearrange("p (h c) -> p h c", h=NHALF),
                                            l1["b_base"][:].unsqueeze(1).to_broadcast([P, NHALF, C]),
                                            ALU.add).then_inc(s3["base1"], 1)
                    dve.wait_ge(s3["base1"], b + 1)
                    nc.vector.tensor_tensor(base_u[:], base_u[:], gates[:, bass.ds(b, 1), 1, :].to_broadcast([P, NHALF, C]),
                                            ALU.mult).then_inc(s3["base2"], 1)
                    dve.wait_ge(s3["base2"], b + 1)
                    nc.vector.tensor_tensor(x[:, b], x[:, b], base_u[:], ALU.add).then_inc(s3["x4"], 1)
                    dve.wait_ge(s3["kept"], b + 1)
                    dve.wait_ge(s3["loss"], b + 1)
                dve.wait_ge(s3["loss_psum"], 1)
                ls = ps[4][:, 0:NB * E1].rearrange("p (b e) -> p b e", e=E1)
                wide = lambda v: v.unsqueeze(2).to_broadcast([P, NB, E1])
                nc.vector.tensor_reduce(least[:], ls, AX.X, ALU.min).then_inc(s3["argmin"], 1)
                dve.wait_ge(s3["argmin"], 1)
                nc.vector.tensor_tensor(is_least[:], ls, wide(least[:]), ALU.is_equal).then_inc(s3["argmin"], 1)
                dve.wait_ge(s3["argmin"], 2)
                nc.vector.tensor_tensor(is_least[:], is_least[:], order[:].unsqueeze(1).to_broadcast([P, NB, E1]),
                                        ALU.mult).then_inc(s3["argmin"], 1)
                dve.wait_ge(s3["argmin"], 3)
                nc.vector.tensor_reduce(least[:], is_least[:], AX.X, ALU.max).then_inc(s3["argmin"], 1)
                dve.wait_ge(s3["argmin"], 4)
                nc.vector.tensor_tensor(chosen[:], is_least[:], wide(least[:]), ALU.is_equal).then_inc(s3["route"], 4)
                dve.wait_ge(s3["route"], 4)
                nc.vector.memset(up_w[:], 0.0).then_inc(s3["up_w"], 1)
                dve.wait_ge(s3["up_w"], 1)
                with dve.Fori(0, NB) as b:
                    pick = lambda rows, n: chosen[0:rows, b, :].unsqueeze(1).to_broadcast([rows, n, E1])
                    nc.vector.tensor_tensor(down_m[:], l1["w_ad"][:], pick(P, R), ALU.mult)
                    nc.vector.tensor_tensor(down_bm[:], l1["b_ad"][:], chosen[0:R, b, :], ALU.mult).then_inc(s3["down_m"], 1)
                    dve.wait_ge(s3["down_m"], b + 1)
                    nc.vector.tensor_reduce(down_b[:], down_bm[:], AX.X, ALU.add)
                    nc.vector.tensor_reduce(down_w[:], down_m[:], AX.X, ALU.add).then_inc(s3["down_w"], 1)
                    dve.wait_ge(s3["up_m"], b + 1)
                    nc.vector.tensor_reduce(up_w[:], up_m[:], AX.X, ALU.add).then_inc(s3["up_w"], 1)
                    dve.wait_ge(s3["up"], b + 1)
                    nc.vector.tensor_tensor(upd2[:], ps[1][:, 0:T].rearrange("p (h c) -> p h c", h=NHALF),
                                            gates[:, bass.ds(b, 1), 1, :].to_broadcast([P, NHALF, C]),
                                            ALU.mult).then_inc(s3["upd"], 1)
                    dve.wait_ge(s3["upd"], b + 1)
                    nc.vector.tensor_tensor(x[:, b], x[:, b], upd2[:], ALU.add).then_inc(s3["x5"], 1)

            @block.sync
            def _(sp):
                ov = out.rearrange("b (h p) c -> b p h c", p=P)
                with sp.Fori(0, NB) as b:
                    sp.wait_ge(s3["x5"], b + 1)
                    sp.dma_start(ov[b], x[:, b]).then_inc(out_done, 16)
                sp.wait_ge(out_done, 16 * NB)
        phase.close()


def lay_out(d):
    g = {k: np.asarray(v) for k, v in d.items()}
    half = D // 2
    ch = np.arange(C)
    partner = (ch // D) * D + (ch % D + half) % D
    wa = g["L0_attn_w_attn"]
    q, k, v = wa[:C], wa[C:2 * C], wa[2 * C:]
    r = {"x": g["L0_attn_x"]}
    r["wqkv0"] = np.stack([q.T, k.T, q[partner].T, k[partner].T, v.T], 1)
    r["wproj0"] = g["L0_attn_w_proj"].T
    r["cT"] = np.stack([g["L0_c"].T, g["L1_c"].T], 1)
    r["wmod"] = np.stack([g[n].reshape(C, 6, C)[:, [0, 1, 3, 4, 2, 5]] for n in ("L0_wmod", "L1_wmod")], 1)
    r["wgate"] = g["L0_ffn_W_gate"].transpose(1, 0, 2)
    r["wup"] = g["L0_ffn_W_up"].transpose(1, 0, 2)
    r["wout"] = g["L0_ffn_W_out"].reshape(E0, MT, P, C).transpose(2, 0, 1, 3)
    r["bgu"] = np.stack([g["L0_ffn_b_gate"].reshape(E0 * MT, P).T, g["L0_ffn_b_up"].reshape(E0 * MT, P).T], 1)
    bo = np.zeros((P, 4, C), np.float32)
    for i in range(4):
        bo[i * E0:(i + 1) * E0, i] = g["L0_ffn_b_out"]
    r["bout"] = bo
    r["wrouter"] = g["L0_ffn_W_router"]
    row = lambda n: np.broadcast_to(g[n].reshape(1, -1), (P, g[n].size))
    r["w_qkv1"] = np.concatenate([g["L1_attn_W" + n].T for n in "qkv"], 1)
    r["b_qkv1"] = np.concatenate([row("L1_attn_b" + n) for n in "qkv"], 1)
    r["b_q1"] = g["L1_attn_bq"].reshape(C, 1)
    rk = np.zeros((C, H, 2 * MAXREL + 1), np.float32)
    rv = np.zeros((P, 16, 8, D), np.float32)
    for h in range(H):
        rk[h * D:(h + 1) * D, h] = g["L1_attn_rk_table"].T
    for h in range(8):
        for t in range(16):
            rv[h * 16:(h + 1) * 16, t, h] = g["L1_attn_rv_table"][MAXREL - t:2 * MAXREL - t]
    r["rk"], r["rv"] = rk, rv
    r["w_o1"] = g["L1_attn_Wo"].T
    r["b_o1"] = row("L1_attn_bo")
    r["w_base"] = g["L1_ffn_W_base"]
    r["b_base"] = row("L1_ffn_b_base")
    r["w_d1"] = g["L1_ffn_Wd1"].transpose(1, 0, 2).reshape(C, E1 * HD1)
    r["b_d1"] = g["L1_ffn_bd1"].reshape(2, P).T
    wd2 = np.zeros((P, E1, C), np.float32)
    for e in range(E1):
        wd2[(e % 4) * HD1:(e % 4 + 1) * HD1, e] = g["L1_ffn_Wd2"][e]
    r["w_d2"] = wd2
    r["b_d2"] = g["L1_ffn_bd2"].T
    r["w_ad"] = g["L1_ffn_Wa_down"].transpose(1, 2, 0)
    r["b_ad"] = g["L1_ffn_ba_down"].T
    au = np.zeros((P, C, E1), np.float32)
    au[:R] = g["L1_ffn_Wa_up"].transpose(1, 2, 0)
    au[R] = g["L1_ffn_ba_up"].T
    r["w_au"] = au
    return r


def kernel(**inputs):
    import concourse.bacc as bacc
    from concourse.bass_utils import run_bass_kernel_spmd

    arrays = {**lay_out(inputs), **shape_constants()}
    arrays = {"in_" + k: np.ascontiguousarray(v) for k, v in arrays.items()}
    nc = bacc.Bacc("TRN2", target_bir_lowering=False, num_devices=1)
    aps = {k[3:]: nc.dram_tensor(k, v.shape, mybir.dt.from_np(v.dtype), kind="ExternalInput").ap() for k, v in arrays.items()}
    out = nc.dram_tensor("x_out", (NB, T, C), F32, kind="ExternalOutput").ap()
    build(nc, aps, out)
    r = run_bass_kernel_spmd(nc, [arrays], core_ids=[0])
    return r.results[0]["x_out"]
```

```python
from contextlib import ExitStack

import numpy as np

import concourse.bass as bass
from concourse import mybir

F32 = mybir.dt.float32
F32R = mybir.dt.float32r
BF16 = mybir.dt.bfloat16
ALU = mybir.AluOpType
ACT = mybir.ActivationFunctionType
AX = mybir.AxisListType

NB, T, C = 16, 256, 128
P = 128
NHALF = T // P
H, D = 16, 8
WINDOW = 64
QB = 32
NQB = T // QB
WIN = WINDOW + QB
HG = 4
HPG = H // HG
E0, M = 8, 256
MT = M // P
MAXREL = 16
E1, HD1, R = 8, 32, 64
EPS = 1e-5
NEG = -1e30


def shape_constants():
    f = np.float32
    half = D // 2
    inv = (1.0 / (f(10000.0) ** (np.arange(0, D, 2, dtype=f) / f(D)))).astype(f)
    ang = np.outer(np.arange(T, dtype=f), inv).astype(f)
    cos, sin = np.cos(ang).astype(f), np.sin(ang).astype(f)
    ch = np.arange(C)
    rc = cos[:, ch % half].T
    rs = sin[:, ch % half].T * np.where(ch % D < half, 1, -1)[:, None]
    scale = 1.0 / np.sqrt(f(D))
    rope = np.stack([rc * scale, rc, rs * scale, rs], 1).astype(f)
    masks = np.zeros((P, 2 * HG), f)
    masks[ch, (ch // D) % HPG] = 1
    masks[ch, HG + ch // (C // HG)] = 1
    key, q = np.arange(P)[:, None], np.arange(QB)[None, :]
    win = np.zeros((P, 3, HPG, QB), f)
    for v, first in enumerate((WINDOW, WINDOW - QB, 0)):
        ok = (key >= q) & (key <= q + WINDOW) & (key >= first)
        win[:, v] = np.where(ok | (key >= WIN), 0.0, NEG)[:, None, :]
    eye = np.eye(P, dtype=f)
    pick = np.zeros((P, HG, WIN), f)
    pick[np.arange(WIN), :, np.arange(WIN)] = 1
    return {
        "const_rope": rope, "const_masks": masks, "const_window": win.reshape(P, -1),
        "const_eye": eye, "const_pick": pick.reshape(P, -1),
        "const_order": np.tile((E0 - np.arange(E0, dtype=f))[None], (P, 1)),
    }


def build(nc, a, out):
    with ExitStack() as ctx:
        def sb(name, shape, dt=F32, until=ctx):
            return until.enter_context(nc.sbuf_tensor(name, shape, dt))

        def sem(name):
            return ctx.enter_context(nc.semaphore(name))

        x = sb("x", [P, NB, NHALF, C])
        eye = sb("eye", [P, P])
        masks = sb("masks", [P, 2 * HG])
        order = sb("order", [P, E0])
        c_t = sb("c_t", [P, 2, NB])
        silu_c = sb("silu_c", [P, 2, NB])
        w_mod = sb("w_mod", [P, 2, 6, C])
        mod = sb("mod", [P, 2, 4, NB])
        gates = sb("gates", [P, NB, 2, C])
        gate_sign = sb("gate_sign", [NB, 2, 2 * C])
        gate_size = sb("gate_size", [NB, 2, 2 * C])
        gate_rows = sb("gate_rows", [P, 2, 2 * C])
        stats = sb("stats", [P, NB, NHALF, 6])
        ln_sum = sb("ln_sum", [P, NB, NHALF])
        ln_dif = sb("ln_dif", [P, NB, NHALF])
        ln_dev = sb("ln_dev", [P, NB, NHALF])
        var_eps = sb("var_eps", [P, NB, NHALF])
        mean = sb("mean", [P, NB, NHALF])
        minus_half = sb("minus_half", [P, NB, NHALF])
        rstd = sb("rstd", [P, NB, NHALF])
        xn = sb("xn", [P, NHALF, C])

        po = ctx.enter_context(nc.psum_tensor("po", [P, 1024], F32))
        ps = [ctx.enter_context(nc.psum_tensor(f"ps{i}", [P, 512], F32)) for i in range(6)]

        x_in = sem("x_in")
        small_in = sem("small_in")
        eye_in = sem("eye_in")
        l0_in = sem("l0_in")
        gu_in = sem("gu_in")
        all_in = sem("all_in")
        silu_done = sem("silu_done")
        mod_psum = sem("mod_psum")
        mod_done = sem("mod_done")
        rows_zero = sem("rows_zero")
        rows_psum = sem("rows_psum")
        row_sizes = sem("row_sizes")
        row_signs = sem("row_signs")
        rows_done = sem("rows_done")
        gates_psum = sem("gates_psum")
        gates_kept = sem("gates_kept")
        const_done = sem("const_done")
        st_done = sem("st_done")
        ln_steps = sem("ln_steps")
        ln_var = sem("ln_var")
        ln_rstd = sem("ln_rstd")

        def token_variances(dve, n):
            nc.vector.tensor_tensor(ln_sum[:], stats[:, :, :, 1], stats[:, :, :, 4], ALU.add)
            nc.vector.tensor_tensor(ln_dif[:], stats[:, :, :, 1], stats[:, :, :, 4], ALU.subtract)
            nc.vector.tensor_tensor(ln_dev[:], stats[:, :, :, 2], stats[:, :, :, 5], ALU.add).then_inc(ln_steps, 1)
            dve.wait_ge(ln_steps, 3 * n + 1)
            nc.vector.tensor_scalar(mean[:], ln_sum[:], 0.5, None, ALU.mult)
            nc.vector.tensor_tensor(ln_dif[:], ln_dif[:], ln_dif[:], ALU.mult).then_inc(ln_steps, 1)
            dve.wait_ge(ln_steps, 3 * n + 2)
            nc.vector.tensor_scalar(ln_dif[:], ln_dif[:], 0.25, EPS, ALU.mult, ALU.add).then_inc(ln_steps, 1)
            dve.wait_ge(ln_steps, 3 * n + 3)
            nc.vector.scalar_tensor_tensor(out=var_eps[:], in0=ln_dev[:], scalar=1.0 / C, in1=ln_dif[:], op0=ALU.mult,
                                           op1=ALU.add).then_inc(ln_var, 1)

        def token_scales(pool, n):
            pool.wait_ge(ln_var, n + 1)
            nc.gpsimd.tensor_tensor(rstd[:, 0:2], var_eps[:, 0:2], minus_half[:, 0:2], ALU.pow).then_inc(ln_rstd, 1)
            nc.gpsimd.tensor_tensor(rstd[:, 2:], var_eps[:, 2:], minus_half[:, 2:], ALU.pow).then_inc(ln_rstd, 1)


        l1 = {}
        for name, shape in (("w_qkv1", [P, 3 * C]), ("b_qkv1", [P, 3 * C]), ("b_q1", [P, 1]), ("rk", [P, H, 2 * MAXREL + 1]),
                            ("rv", [P, 16, 8, D]), ("w_o1", [P, C]), ("b_o1", [P, C]),
                            ("w_base", [P, C]), ("w_d1", [P, 2 * P]), ("b_d1", [P, 2]),
                            ("w_d2", [P, E1, C]), ("b_d2", [P, E1]), ("w_ad", [P, R, E1]), ("b_ad", [R, E1]),
                            ("w_au", [P, C, E1])):
            l1[name] = sb(name, shape)

        layer0 = ExitStack()
        rope = sb("rope", [P, 4, T], until=layer0)
        window_f = sb("window_f", [P, 3 * P], until=layer0)
        window_bf = sb("window_bf", [P, 3, P], BF16, until=layer0)
        pick_f = sb("pick_f", [P, HG * WIN], until=layer0)
        pick_bf = sb("pick_bf", [P, HG * WIN], BF16, until=layer0)
        w_qkv0 = sb("w_qkv0", [P, 5, C], until=layer0)
        w_proj0 = sb("w_proj0", [P, C], until=layer0)
        w_gu = sb("w_gu", [P, 2, E0 * M], until=layer0)
        w_gu_hi = sb("w_gu_hi", [P, 2, E0 * M], F32R, until=layer0)
        w_gu_lo = sb("w_gu_lo", [P, 2, E0 * M], F32R, until=layer0)
        w_out = sb("w_out", [P, E0, MT, C], until=layer0)
        b_gu = sb("b_gu", [P, 2, E0 * MT], until=layer0)
        b_out = sb("b_out", [P, 4, C], until=layer0)
        w_router = sb("w_router", [P, E0], until=layer0)

        def spread_gates(pe, layer):
            for pair in range(NB // 2):
                n = layer * (NB // 2) + pair
                if pair >= 2:
                    pe.wait_ge(gates_kept, n - 1)
                for j in range(2):
                    b = 2 * pair + j
                    last = nc.tensor.matmul(ps[pair % 2][:, j * 2 * C:(j + 1) * 2 * C],
                                            eye[:, b:b + 1].to_broadcast([P, P]),
                                            gate_rows[:, layer, :], start=True, stop=True)
                last.then_inc(gates_psum, 1)

        def keep_gates(act, layer):
            for pair in range(NB // 2):
                n = layer * (NB // 2) + pair
                act.wait_ge(gates_psum, n + 1)
                nc.scalar.copy(gates[:, 2 * pair:2 * pair + 2, :, :].rearrange("p b g c -> p (b g c)"),
                               ps[pair % 2][:]).then_inc(gates_kept, 1)

        with nc.Block() as block:
            @block.sync
            def _(sp):
                for name, t in (("cT", c_t), ("wmod", w_mod)):
                    sp.dma_start(t[:], a[name]).then_inc(small_in, 16)
                xv = a["x"].rearrange("b (h p) c -> p b h c", p=P)
                for q in range(4):
                    sp.dma_start(x[:, 4 * q:4 * q + 4], xv[:, 4 * q:4 * q + 4]).then_inc(x_in, 16)
                sp.wait_ge(x_in, 64)
                sp.wait_ge(l0_in, 16 * 7)
                sp.dma_start(w_gu[:], a["wgu"]).then_inc(gu_in, 16)
                for name, t in (("wout", w_out), ("bgu", b_gu), ("bout", b_out),
                                ("wrouter", w_router)) + tuple(l1.items()):
                    sp.dma_start(t[:], a[name]).then_inc(all_in, 16)

            @block.gpsimd
            def _(pool):
                pool.dma_start(eye[:], a["const_eye"]).then_inc(eye_in, 16)
                for name, t in (("const_rope", rope), ("const_masks", masks),
                                ("const_window", window_f), ("const_pick", pick_f), ("const_order", order),
                                ("wqkv0", w_qkv0), ("wproj0", w_proj0)):
                    pool.dma_start(t[:], a[name]).then_inc(l0_in, 16)

            @block.scalar
            def _(act):
                act.wait_ge(small_in, 32)
                nc.scalar.activation(silu_c[:], c_t[:], ACT.Silu).then_inc(silu_done, 1)
                act.wait_ge(rows_psum, 1)
                nc.scalar.activation(gate_size[:].rearrange("b l c -> b (l c)"), ps[3][0:NB, :], ACT.Abs,
                                     scale=2.0).then_inc(row_sizes, 1)
                keep_gates(act, 0)

            @block.tensor
            def _(pe):
                pe.wait_ge(silu_done, 1)
                for layer in range(2):
                    for j in range(4):
                        last = nc.tensor.matmul(ps[2][:, (layer * 4 + j) * NB:(layer * 4 + j + 1) * NB],
                                                w_mod[:, layer, j, :], silu_c[:, layer, :], start=True, stop=True)
                last.then_inc(mod_psum, 1)
                for layer in range(2):
                    last = nc.tensor.matmul(ps[3][0:NB, layer * 2 * C:(layer + 1) * 2 * C], silu_c[:, layer, :],
                                            w_mod[:, layer, 4:6, :].rearrange("p j c -> p (j c)"), start=True, stop=True)
                last.then_inc(rows_psum, 1)
                pe.wait_ge(eye_in, 16)
                pe.wait_ge(rows_done, 1)
                spread_gates(pe, 0)

            @block.vector
            def _(dve):
                nc.vector.memset(minus_half[:], -0.5)
                nc.vector.memset(gate_rows[:], 0.0).then_inc(rows_zero, 1)
                dve.wait_ge(mod_psum, 1)
                pm = ps[2][:, 0:8 * NB].rearrange("p (l j b) -> p l j b", l=2, j=4)
                nc.vector.tensor_copy(mod[:, :, 0, :], pm[:, :, 0, :])
                nc.vector.tensor_scalar(mod[:, :, 1, :], pm[:, :, 1, :], 1.0, None, ALU.add)
                nc.vector.tensor_copy(mod[:, :, 2, :], pm[:, :, 2, :])
                nc.vector.tensor_scalar(mod[:, :, 3, :], pm[:, :, 3, :], 1.0, None, ALU.add).then_inc(mod_done, 1)
                dve.wait_ge(row_sizes, 1)
                nc.vector.tensor_scalar(gate_sign[:].rearrange("b l c -> b (l c)"), ps[3][0:NB, :], 0.0, 0.5, ALU.is_ge,
                                        ALU.subtract).then_inc(row_signs, 1)
                dve.wait_ge(rows_zero, 1)
                dve.wait_ge(row_signs, 1)
                nc.vector.scalar_tensor_tensor(out=gate_rows[0:NB], in0=gate_size[:], scalar=0.5, in1=gate_sign[:],
                                               op0=ALU.max, op1=ALU.mult).then_inc(rows_done, 1)
                dve.wait_ge(l0_in, 16 * 7)
                nc.vector.tensor_copy(window_bf[:].rearrange("p v q -> p (v q)"), window_f[:])
                nc.vector.tensor_copy(pick_bf[:], pick_f[:]).then_inc(const_done, 1)
                dve.wait_ge(x_in, 64)
                for b in range(NB):
                    for h in range(NHALF):
                        last = nc.vector.bn_stats(stats[:, b, h, :], x[:, b, h, :])
                last.then_inc(st_done, 1)
                dve.wait_ge(st_done, 1)
                token_variances(dve, 0)

        phase = ExitStack()
        h_t = sb("h_t", [P, WINDOW + T], until=phase)
        rope_c = sb("rope_c", [P, 512], until=phase)
        rope_s = sb("rope_s", [P, 512], until=phase)
        qk = sb("qk", [P, 512], until=phase)
        q_m = sb("q_m", [P, 2, NQB, HPG, QB], until=phase)
        k_m = sb("k_m", [P, 2, HG, WINDOW + T], until=phase)
        v_win = sb("v_win", [WIN, 2, NQB, C], until=phase)
        negmax = sb("negmax", [P, NQB, HG], until=phase)
        esum = sb("esum", [P, NQB, HG], until=phase)
        rsum = sb("rsum", [P, NQB, HG], until=phase)
        p_exp = sb("p_exp", [P, 2, HG, WIN], until=phase)
        p_nrm = sb("p_nrm", [P, 2, HG, WIN], until=phase)
        p_t = sb("p_t", [WIN, 2, HG * P], until=phase)
        y_t = sb("y_t", [P, 2, T], until=phase)
        upd = sb("upd", [P, NHALF, C], until=phase)
        ACT_QB = (0, 2, 5, 7)
        s0 = {n: sem("a0_" + n) for n in (
            "pads", "w_hi", "w_lo", "xn", "x_t", "h_t", "qk_psum", "v_psum", "v_sb", "rope_mul", "rope", "masked", "scores",
            "negmax",
            "exp", "rsum", "p_nrm", "p_t_psum", "p_t_dve", "p_t_act", "pv", "y_part", "y", "proj", "upd", "x1", "st")}

        def p_t_ready(eng, b, qb):
            if qb in ACT_QB:
                eng.wait_ge(s0["p_t_act"], len(ACT_QB) * b + ACT_QB.index(qb) + 1)
            else:
                before = sum(q in ACT_QB for q in range(qb))
                eng.wait_ge(s0["p_t_dve"], (NQB - len(ACT_QB)) * b + qb - before + 1)

        def entries(eng, entry):
            entry(0, 0, False, True)
            with eng.Fori(0, NB // 2 - 1) as pair:
                entry(2 * pair + 1, 1, True, True)
                entry(2 * pair + 2, 0, True, True)
            entry(NB - 1, 1, True, False)

        def near(b, buf, qb):
            if qb < 0:
                return b - 1, qb + NQB, 1 - buf
            if qb >= NQB:
                return b + 1, qb - NQB, 1 - buf
            return b, qb, buf

        with nc.Block() as block:
            @block.tensor
            def _(pe):
                def to_channels(b, first=False):
                    if not first:
                        pe.wait_ge(s0["v_sb"], 2 * b)
                    pe.wait_ge(s0["xn"], b + 1)
                    for h in range(NHALF):
                        last = nc.tensor.transpose(ps[1][:, h * P:(h + 1) * P], xn[:, h, :], eye[:])
                    last.then_inc(s0["x_t"], 1)

                def project_qk(b):
                    pe.wait_ge(s0["h_t"], b + 1)
                    for j in range(4):
                        last = nc.tensor.matmul(ps[j // 2][:, (j % 2) * T:(j % 2 + 1) * T], w_qkv0[:, j, :],
                                                h_t[:, WINDOW:], start=True, stop=True)
                    last.then_inc(s0["qk_psum"], 1)

                def project_v(b):
                    pe.wait_ge(s0["rope_mul"], b + 1)
                    for qb in range(NQB):
                        last = nc.tensor.matmul(ps[qb // 4][0:WIN, (qb % 4) * C:(qb % 4 + 1) * C],
                                                h_t[:, qb * QB:qb * QB + WIN], w_qkv0[:, 4, :], start=True, stop=True)
                    last.then_inc(s0["v_psum"], 1)

                def scores(b, qb, buf, free=False):
                    if not free:
                        pe.wait_ge(s0["exp"], NQB * b + qb - 1)
                    if qb == 0:
                        pe.wait_ge(s0["masked"], b + 1)
                    pst = ps[2 + qb % 2][:, 0:HG * WIN]
                    nc.tensor.matmul(pst, window_bf[:, min(qb, 2), :], pick_bf[:], start=True, stop=False)
                    nc.tensor.matmul(pst, q_m[:, buf, qb, :, :].rearrange("p h q -> p (h q)"),
                                     k_m[:, buf, :, qb * QB:qb * QB + WIN], start=False,
                                     stop=True).then_inc(s0["scores"], 1)

                def turn(b, qb, buf):
                    pe.wait_ge(s0["p_nrm"], NQB * b + qb + 1)
                    for g in range(HG):
                        last = nc.tensor.transpose(ps[4 + qb % 2][0:WIN, g * P:(g + 1) * P], p_nrm[:, qb % 2, g, :],
                                                   eye[:])
                    last.then_inc(s0["p_t_psum"], 1)

                def attend(b, qb, buf, first=False):
                    if qb == 0:
                        pe.wait_ge(s0["v_sb"], 2 * b + 2)
                    if qb % (NQB // 2) == 0 and not first:
                        pe.wait_ge(s0["y"], 2 * b - 1 + qb // (NQB // 2))
                    p_t_ready(pe, b, qb)
                    for g in range(HG):
                        last = nc.tensor.matmul(po[g * 32:(g + 1) * 32, qb * P:(qb + 1) * P],
                                                v_win[:, buf, qb, g * 32:(g + 1) * 32],
                                                p_t[:, qb % 2, g * P:(g + 1) * P], start=True, stop=True)
                    last.then_inc(s0["pv"], 1)

                def finish(b, buf):
                    pe.wait_ge(s0["y"], 2 * b + 2)
                    for h in range(NHALF):
                        last = nc.tensor.matmul(ps[0][:, h * P:(h + 1) * P], y_t[:, buf, h * P:(h + 1) * P], w_proj0[:],
                                                start=True, stop=True)
                    last.then_inc(s0["proj"], 1)

                def entry(b, buf, former, has_next):
                    for qb in range(NQB):
                        if qb >= 1 or former:
                            turn(*near(b, buf, qb - 1))
                        if qb >= 2 or former:
                            attend(*near(b, buf, qb - 2), first=not former)
                        if qb + 2 < NQB or has_next:
                            scores(*near(b, buf, qb + 2))
                        if qb == 1 and has_next:
                            to_channels(b + 1)
                        if qb == 2 and has_next:
                            if former:
                                pe.wait_ge(s0["upd"], b)
                            project_qk(b + 1)
                        if qb == 4 and has_next:
                            project_v(b + 1)
                        if qb == 6 and former:
                            if has_next:
                                pe.wait_ge(s0["v_sb"], 2 * b + 4)
                            finish(b - 1, 1 - buf)

                pe.wait_ge(s0["pads"], 1)
                to_channels(0, first=True)
                project_qk(0)
                project_v(0)
                scores(0, 0, 0, free=True)
                scores(0, 1, 0, free=True)
                entries(pe, entry)
                turn(NB - 1, NQB - 1, 1)
                attend(NB - 1, NQB - 2, 1)
                attend(NB - 1, NQB - 1, 1)
                finish(NB - 1, 1)

            @block.scalar
            def _(act):
                def modulate(b):
                    act.wait_ge(s0["x_t"], b + 1)
                    nc.scalar.activation(h_t[:, WINDOW:], ps[1][:, 0:T], ACT.Identity, scale=mod[:, 0, 1, bass.ds(b, 1)],
                                         bias=mod[:, 0, 0, bass.ds(b, 1)]).then_inc(s0["h_t"], 1)

                def values(b, buf):
                    act.wait_ge(s0["v_psum"], b + 1)
                    for i in range(2):
                        nc.scalar.copy(v_win[:, buf, 4 * i:4 * i + 4, :].rearrange("p q c -> p (q c)"),
                                       ps[i][0:WIN, :]).then_inc(s0["v_sb"], 1)

                def from_psum(b, qb, buf, free=False):
                    act.wait_ge(s0["p_t_psum"], NQB * b + qb + 1)
                    if not free:
                        act.wait_ge(s0["pv"], NQB * b + qb - 1)
                    nc.scalar.copy(p_t[:, qb % 2, :], ps[4 + qb % 2][0:WIN, :]).then_inc(s0["p_t_act"], 1)

                def entry(b, buf, former, has_next):
                    for qb in range(NQB):
                        act.wait_ge(s0["negmax"], NQB * b + qb + 1)
                        if former or qb >= 2:
                            act.wait_ge(s0["p_nrm"], NQB * b + qb - 1)
                        for g in range(HG):
                            last = nc.scalar.activation(p_exp[:, qb % 2, g, :], ps[2 + qb % 2][:, g * WIN:(g + 1) * WIN],
                                                        ACT.Exp, bias=negmax[:, qb, g:g + 1],
                                                        accum_out=esum[:, qb, g:g + 1])
                        last.then_inc(s0["exp"], 1)
                        if (qb - 1) % NQB in ACT_QB and (former or qb >= 1):
                            from_psum(*near(b, buf, qb - 1), free=not former and qb < 3)
                        if qb == 2 and has_next:
                            modulate(b + 1)
                        if qb == 5 and has_next:
                            values(b + 1, 1 - buf)

                modulate(0)
                values(0, 0)
                entries(act, entry)
                from_psum(NB - 1, NQB - 1, 1)

            @block.gpsimd
            def _(pool):
                def rotate(b):
                    pool.wait_ge(s0["rope_mul"], b + 1)
                    nc.gpsimd.tensor_tensor(qk[:], rope_c[:], rope_s[:], ALU.add).then_inc(s0["rope"], 1)

                def entry(b, buf, former, has_next):
                    for qb in range(NQB):
                        pool.wait_ge(s0["rsum"], NQB * b + qb + 1)
                        if former or qb >= 2:
                            pool.wait_ge(s0["p_t_psum"], NQB * b + qb - 1)
                        nc.gpsimd.tensor_tensor(p_nrm[:, qb % 2], p_exp[:, qb % 2],
                                                rsum[:, qb, :].unsqueeze(2).to_broadcast([P, HG, WIN]),
                                                ALU.mult).then_inc(s0["p_nrm"], 1)
                        if qb == 3 and has_next:
                            rotate(b + 1)

                token_scales(pool, 0)
                rotate(0)
                entries(pool, entry)

            @block.vector
            def _(dve):
                def normalise(b):
                    for h in range(NHALF):
                        last = nc.vector.tensor_scalar(xn[:, h, :], x[:, b, h, :], mean[:, b, h:h + 1],
                                                       rstd[:, b, h:h + 1], ALU.subtract, ALU.mult)
                    last.then_inc(s0["xn"], 1)

                def rope_products(b):
                    dve.wait_ge(s0["qk_psum"], b + 1)
                    nc.vector.tensor_tensor(rope_c[:], ps[0][:], rope[:, 0:2, :].rearrange("p j t -> p (j t)"), ALU.mult)
                    nc.vector.tensor_tensor(rope_s[:], ps[1][:], rope[:, 2:4, :].rearrange("p j t -> p (j t)"),
                                            ALU.mult).then_inc(s0["rope_mul"], 1)

                def mask_queries(b, buf):
                    dve.wait_ge(s0["rope"], b + 1)
                    for i in range(HPG):
                        nc.vector.tensor_scalar(q_m[:, buf, :, i, :], qk[:, 0:T].rearrange("p (n q) -> p n q", q=QB),
                                                masks[:, i:i + 1], None, ALU.mult)

                def mask_keys(b, buf):
                    for g in range(HG):
                        last = nc.vector.tensor_scalar(k_m[:, buf, g, WINDOW:], qk[:, T:], masks[:, HG + g:HG + g + 1],
                                                       None, ALU.mult)
                    last.then_inc(s0["masked"], 1)

                def heads_out(b, buf, half):
                    n = NQB // 2
                    dve.wait_ge(s0["pv"], NQB * b + n * (half + 1))
                    o4 = po[:, half * 512:(half + 1) * 512].rearrange("p (n h q) -> p h n q", h=HPG, q=QB)
                    yv = y_t[:, buf, half * P:(half + 1) * P].rearrange("p (n q) -> p n q", q=QB)
                    nc.vector.tensor_scalar(yv, o4[:, 0], masks[:, 0:1], None, ALU.mult).then_inc(s0["y_part"], 1)
                    for i in range(1, HPG):
                        dve.wait_ge(s0["y_part"], (HPG - 1) * (2 * b + half) + i)
                        last = nc.vector.scalar_tensor_tensor(out=yv, in0=o4[:, i], scalar=masks[:, i:i + 1], in1=yv,
                                                              op0=ALU.mult, op1=ALU.add)
                        last.then_inc(s0["y_part" if i < HPG - 1 else "y"], 1)

                def gate_update(b):
                    dve.wait_ge(s0["proj"], b + 1)
                    nc.vector.tensor_tensor(upd[:], ps[0][:, 0:T].rearrange("p (h c) -> p h c", h=NHALF),
                                            gates[:, bass.ds(b, 1), 0, :].to_broadcast([P, NHALF, C]),
                                            ALU.mult).then_inc(s0["upd"], 1)

                def add_update(b):
                    dve.wait_ge(s0["upd"], b + 2)
                    nc.vector.tensor_tensor(x[:, b], x[:, b], upd[:], ALU.add).then_inc(s0["x1"], 1)

                def statistics(b):
                    for h in range(NHALF):
                        last = nc.vector.bn_stats(stats[:, b, h, :], x[:, b, h, :])
                    last.then_inc(s0["st"], 1)

                def upper_weights(b):
                    dve.wait_ge(gu_in, 16)
                    nc.vector.tensor_copy(w_gu_hi[:, :, bass.ds(P * b, P)],
                                          w_gu[:, :, bass.ds(P * b, P)]).then_inc(s0["w_hi"], 1)

                def lower_weights(b):
                    dve.wait_ge(s0["w_hi"], b + 1)
                    nc.vector.tensor_tensor(w_gu_lo[:, :, bass.ds(P * b, P)], w_gu[:, :, bass.ds(P * b, P)],
                                            w_gu_hi[:, :, bass.ds(P * b, P)].bitcast(F32),
                                            ALU.subtract).then_inc(s0["w_lo"], 1)

                def maximum(b, qb, buf):
                    dve.wait_ge(s0["scores"], NQB * b + qb + 1)
                    nc.vector.tensor_reduce(negmax[:, qb, :],
                                            ps[2 + qb % 2][:, 0:HG * WIN].rearrange("p (g k) -> p g k", g=HG),
                                            AX.X, ALU.max, negate=True).then_inc(s0["negmax"], 1)

                def from_psum(b, qb, buf, free=False):
                    dve.wait_ge(s0["p_t_psum"], NQB * b + qb + 1)
                    if not free:
                        dve.wait_ge(s0["pv"], NQB * b + qb - 1)
                    nc.vector.tensor_copy(p_t[:, qb % 2, :], ps[4 + qb % 2][0:WIN, :]).then_inc(s0["p_t_dve"], 1)

                def entry(b, buf, former, has_next):
                    for qb in range(NQB):
                        dve.wait_ge(s0["exp"], NQB * b + qb + 1)
                        nc.vector.reciprocal(rsum[:, qb, :], esum[:, qb, :]).then_inc(s0["rsum"], 1)
                        if (qb - 1) % NQB not in ACT_QB and (former or qb >= 1):
                            from_psum(*near(b, buf, qb - 1), free=not former and qb < 3)
                        if qb == 7 and former:
                            add_update(b - 1)
                        if qb + 2 < NQB or has_next:
                            maximum(*near(b, buf, qb + 2))
                        if qb == 5 and has_next:
                            mask_keys(b + 1, 1 - buf)
                        if qb == 0 and has_next:
                            if former:
                                dve.wait_ge(ln_rstd, 2)
                            normalise(b + 1)
                        if qb == 0:
                            upper_weights(b)
                        if qb == 1:
                            lower_weights(b)
                        if qb == 2 and former:
                            heads_out(b - 1, 1 - buf, 1)
                        if qb == 3 and has_next:
                            rope_products(b + 1)
                        if qb == 4 and has_next:
                            mask_queries(b + 1, 1 - buf)
                        if qb == 6:
                            heads_out(b, buf, 0)
                            if former:
                                gate_update(b - 1)
                        if qb == 7 and former:
                            dve.wait_ge(s0["x1"], b)
                            statistics(b - 1)

                nc.vector.memset(h_t[:, 0:WINDOW], 0.0).then_inc(s0["upd"], 1)
                for buf in range(2):
                    last = nc.vector.memset(k_m[:, buf, :, 0:WINDOW], 0.0)
                last.then_inc(s0["pads"], 1)
                dve.wait_ge(ln_rstd, 1)
                normalise(0)
                rope_products(0)
                mask_queries(0, 0)
                mask_keys(0, 0)
                maximum(0, 0, 0)
                maximum(0, 1, 0)
                entries(dve, entry)
                heads_out(NB - 1, 1, 1)
                gate_update(NB - 1)
                add_update(NB - 1)
                dve.wait_ge(s0["x1"], NB)
                statistics(NB - 1)
                dve.wait_ge(s0["st"], NB)
                token_variances(dve, 1)
        phase.close()

        phase = ExitStack()
        CH = 4
        NCH = NB * NHALF // CH
        xn4 = sb("xn4", [P, CH, C], until=phase)
        h4 = sb("h4", [P, 2, CH * P], until=phase)
        h_hi = sb("h_hi", [P, 2, CH * P], F32R, until=phase)
        h_lo = sb("h_lo", [P, 2, CH * P], F32R, until=phase)
        logit_max = sb("logit_max", [P, CH], until=phase)
        prob = sb("prob", [P, CH, E0], until=phase)
        prob_sum = sb("prob_sum", [P, CH], until=phase)
        hit = sb("hit", [P, CH, E0], until=phase)
        rank = sb("rank", [P, CH, E0], until=phase)
        rank_max = sb("rank_max", [P, CH], until=phase)
        first = sb("first", [P, CH, E0], until=phase)
        second = sb("second", [P, CH, E0], until=phase)
        left = sb("left", [P, CH, E0], until=phase)
        top = sb("top", [P, 2, CH], until=phase)
        top_sum = sb("top_sum", [P, CH], until=phase)
        w_exp = sb("w_exp", [P, 2, P], until=phase)
        w_exp_t = sb("w_exp_t", [P, P], until=phase)
        act_g = sb("act_g", [P, 2, CH * P], until=phase)
        hid = sb("hid", [P, 2, MT, CH * P], until=phase)
        acc = sb("acc", [P, 2, CH, C], until=phase)

        ROUTE_LINKS = 21
        NK = E0 * MT
        s1 = {n: sem("e0_" + n) for n in (
            "zero", "chain", "xn", "x_t", "h", "h_hi", "h_lo", "logits", "route", "prob", "w", "w_t_psum", "w_t", "bias",
            "acc0", "gate_up", "silu", "hid", "out", "acc", "upd", "x2", "st")}

        def chunks(eng, chunk):
            chunk(0, 0, False, True)
            with eng.Fori(0, NCH // 2 - 1) as pair:
                chunk(2 * pair + 1, 1, True, True)
                chunk(2 * pair + 2, 0, True, True)
            chunk(NCH - 1, 1, True, False)

        with nc.Block() as block:
            @block.sync
            def _(sp):
                sp.wait_ge(all_in, 16 * (4 + len(l1)))

            @block.tensor
            def _(pe):
                def turn(c):
                    pe.wait_ge(s1["xn"], c + 1)
                    for t in range(CH):
                        last = nc.tensor.transpose(ps[0][:, t * P:(t + 1) * P], xn4[:, t, :], eye[:])
                    last.then_inc(s1["x_t"], 1)

                def logits(c, buf):
                    pe.wait_ge(s1["h"], 2 * c + 2)
                    for t in range(CH):
                        last = nc.tensor.matmul(ps[1][:, t * E0:(t + 1) * E0], h4[:, buf, t * P:(t + 1) * P], w_router[:],
                                                start=True, stop=True)
                    last.then_inc(s1["logits"], 1)

                def down(c, e, former):
                    pe.wait_ge(s1["hid"], NK * c + MT * (e + 1))
                    if former or e >= 2:
                        pe.wait_ge(s1["acc"], E0 * c + e - 1)
                    for t in range(CH):
                        for m in range(MT):
                            last = nc.tensor.matmul(po[:, (e % 2) * 512 + t * C:(e % 2) * 512 + (t + 1) * C],
                                                    hid[:, e % 2, m, t * P:(t + 1) * P], w_out[:, e, m, :],
                                                    start=(m == 0), stop=(m == MT - 1))
                    last.then_inc(s1["out"], 1)

                def chunk(c, buf, former, has_next):
                    def gate_up(k):
                        if former or k >= 2:
                            pe.wait_ge(s1["hid"], NK * c + k - 1)
                        if k == 0:
                            pe.wait_ge(s1["h_lo"], c + 1)
                        for j in range(2):
                            bank, w = ps[2 + 2 * j + k % 2], slice(k * P, (k + 1) * P)
                            nc.tensor.matmul(bank[:], w_gu_hi[:, j, w], h_hi[:, buf, :], start=True, stop=False)
                            nc.tensor.matmul(bank[:], w_gu_lo[:, j, w], h_hi[:, buf, :], start=False, stop=False)
                            last = nc.tensor.matmul(bank[:], w_gu_hi[:, j, w], h_lo[:, buf, :], start=False, stop=True)
                        last.then_inc(s1["gate_up"], 1)

                    for e in range(E0):
                        for m in range(MT):
                            gate_up(MT * e + m)
                        if e == (0 if former else 1):
                            pe.wait_ge(s1["w"], c + 1)
                            nc.tensor.transpose(ps[1][:, 0:P], w_exp[:, buf, :], eye[:]).then_inc(s1["w_t_psum"], 1)
                        if e == 1:
                            pe.wait_ge(s1["w_t"], c + 1)
                            for t in range(CH):
                                last = nc.tensor.matmul(ps[0][:, t * C:(t + 1) * C], w_exp_t[:], b_out[:, t, :],
                                                        start=True, stop=True)
                            last.then_inc(s1["bias"], 1)
                        if e == 3 and has_next:
                            pe.wait_ge(s1["acc0"], c + 1)
                            turn(c + 1)
                        if e == 5 and has_next:
                            logits(c + 1, 1 - buf)
                        if e >= 1:
                            down(c, e - 1, former)
                        elif former:
                            down(c - 1, E0 - 1, True)

                pe.wait_ge(all_in, 16 * (4 + len(l1)))
                pe.wait_ge(s0["w_lo"], NB)
                turn(0)
                logits(0, 0)
                chunks(pe, chunk)
                down(NCH - 1, E0 - 1, True)

            @block.scalar
            def _(act):
                def modulate(c, buf):
                    act.wait_ge(s1["x_t"], c + 1)
                    for j in range(2):
                        b = 2 * c + j
                        nc.scalar.activation(h4[:, buf, j * T:(j + 1) * T], ps[0][:, j * T:(j + 1) * T], ACT.Identity,
                                             scale=mod[:, 0, 3, bass.ds(b, 1)],
                                             bias=mod[:, 0, 2, bass.ds(b, 1)]).then_inc(s1["h"], 1)

                def exponentials(c):
                    act.wait_ge(s1["route"], c + 1)
                    nc.scalar.activation(prob[:], hit[:], ACT.Exp).then_inc(s1["prob"], 1)

                def chunk(c, buf, former, has_next):
                    for k in range(NK):
                        act.wait_ge(s1["gate_up"], NK * c + k + 1)
                        nc.scalar.activation(act_g[:, k % 2, :], ps[2 + k % 2][:], ACT.Silu,
                                             bias=b_gu[:, 0, k:k + 1]).then_inc(s1["silu"], 1)
                        if k == 3:
                            act.wait_ge(s1["bias"], c + 1)
                            nc.scalar.copy(acc[:, buf].rearrange("p t c -> p (t c)"), ps[0][:]).then_inc(s1["acc0"], 1)
                        if k == 7 and has_next:
                            modulate(c + 1, 1 - buf)
                        if k == 12 and has_next:
                            exponentials(c + 1)

                modulate(0, 0)
                exponentials(0)
                chunks(act, chunk)

            @block.vector
            def _(dve):
                wide = lambda v: v.unsqueeze(2).to_broadcast([P, CH, E0])

                def normalise(c):
                    for t in range(CH):
                        b = 2 * c + t // 2
                        last = nc.vector.tensor_scalar(xn4[:, t, :], x[:, b, t % 2, :], mean[:, b, t % 2:t % 2 + 1],
                                                       rstd[:, b, t % 2:t % 2 + 1], ALU.subtract, ALU.mult)
                    last.then_inc(s1["xn"], 1)

                def upper_tokens(c, buf):
                    dve.wait_ge(s1["h"], 2 * c + 2)
                    nc.vector.tensor_copy(h_hi[:, buf, :], h4[:, buf, :]).then_inc(s1["h_hi"], 1)

                def logits_below_maximum(c):
                    link = ROUTE_LINKS * c
                    dve.wait_ge(s1["logits"], c + 1)
                    lg = ps[1][:, 0:CH * E0].rearrange("p (t e) -> p t e", e=E0)
                    nc.vector.tensor_reduce(logit_max[:], lg, AX.X, ALU.max).then_inc(s1["chain"], 1)
                    dve.wait_ge(s1["chain"], link + 1)
                    nc.vector.tensor_tensor(hit[:], lg, wide(logit_max[:]), ALU.subtract).then_inc(s1["route"], 1)

                def probabilities(c):
                    link = ROUTE_LINKS * c
                    dve.wait_ge(s1["prob"], c + 1)
                    nc.vector.tensor_reduce(prob_sum[:], prob[:], AX.X, ALU.add).then_inc(s1["chain"], 1)
                    dve.wait_ge(s1["chain"], link + 2)
                    nc.vector.reciprocal(prob_sum[:], prob_sum[:]).then_inc(s1["chain"], 1)
                    dve.wait_ge(s1["chain"], link + 3)
                    nc.vector.tensor_tensor(prob[:], prob[:], wide(prob_sum[:]), ALU.mult).then_inc(s1["chain"], 1)

                def largest(c, j, src, mark):
                    link = ROUTE_LINKS * c + 4 + 6 * j
                    dve.wait_ge(s1["chain"], link)
                    nc.vector.tensor_reduce(top[:, j, :], src[:], AX.X, ALU.max).then_inc(s1["chain"], 1)
                    dve.wait_ge(s1["chain"], link + 1)
                    nc.vector.tensor_tensor(hit[:], src[:], wide(top[:, j, :]), ALU.is_equal).then_inc(s1["chain"], 1)
                    dve.wait_ge(s1["chain"], link + 2)
                    nc.vector.tensor_tensor(rank[:], hit[:], order[:].unsqueeze(1).to_broadcast([P, CH, E0]),
                                            ALU.mult).then_inc(s1["chain"], 1)
                    dve.wait_ge(s1["chain"], link + 3)
                    nc.vector.tensor_reduce(rank_max[:], rank[:], AX.X, ALU.max).then_inc(s1["chain"], 1)
                    dve.wait_ge(s1["chain"], link + 4)
                    nc.vector.tensor_tensor(mark[:], rank[:], wide(rank_max[:]), ALU.is_equal).then_inc(s1["chain"], 1)

                def without_first(c):
                    dve.wait_ge(s1["chain"], ROUTE_LINKS * c + 9)
                    nc.vector.scalar_tensor_tensor(out=left[:], in0=first[:], scalar=-2.0, in1=prob[:], op0=ALU.mult,
                                                   op1=ALU.add).then_inc(s1["chain"], 1)

                def expert_weights(c, buf):
                    link = ROUTE_LINKS * c + 15
                    dve.wait_ge(s1["chain"], link)
                    nc.vector.tensor_tensor(top_sum[:], top[:, 0, :], top[:, 1, :], ALU.add).then_inc(s1["chain"], 1)
                    dve.wait_ge(s1["chain"], link + 1)
                    nc.vector.tensor_scalar(top_sum[:], top_sum[:], 1e-8, None, ALU.add).then_inc(s1["chain"], 1)
                    dve.wait_ge(s1["chain"], link + 2)
                    nc.vector.reciprocal(top_sum[:], top_sum[:]).then_inc(s1["chain"], 1)
                    dve.wait_ge(s1["chain"], link + 3)
                    nc.vector.tensor_tensor(top[:, 0, :], top[:, 0, :], top_sum[:], ALU.mult)
                    nc.vector.tensor_tensor(top[:, 1, :], top[:, 1, :], top_sum[:], ALU.mult).then_inc(s1["chain"], 1)
                    dve.wait_ge(s1["chain"], link + 4)
                    nc.vector.tensor_tensor(first[:], first[:], wide(top[:, 0, :]), ALU.mult).then_inc(s1["chain"], 1)
                    nc.vector.tensor_tensor(second[:], second[:], wide(top[:, 1, :]), ALU.mult).then_inc(s1["chain"], 1)
                    dve.wait_ge(s1["chain"], link + 6)
                    nc.vector.tensor_tensor(w_exp[:, buf, 0:CH * E0].rearrange("p (t e) -> p t e", e=E0), first[:],
                                            second[:], ALU.add).then_inc(s1["w"], 1)

                def accumulate(c, buf, e):
                    if e == 0:
                        dve.wait_ge(s1["acc0"], c + 1)
                    else:
                        dve.wait_ge(s1["acc"], E0 * c + e)
                    dve.wait_ge(s1["out"], E0 * c + e + 1)
                    for t in range(CH):
                        last = nc.vector.scalar_tensor_tensor(
                            out=acc[:, buf, t, :], in0=po[:, (e % 2) * 512 + t * C:(e % 2) * 512 + (t + 1) * C],
                            scalar=w_exp[:, buf, t * E0 + e:t * E0 + e + 1], in1=acc[:, buf, t, :], op0=ALU.mult,
                            op1=ALU.add)
                    last.then_inc(s1["acc"], 1)

                def gate(c, buf):
                    dve.wait_ge(s1["acc"], E0 * (c + 1))
                    for j in range(2):
                        last = nc.vector.tensor_tensor(acc[:, buf, 2 * j:2 * j + 2, :], acc[:, buf, 2 * j:2 * j + 2, :],
                                                       gates[:, bass.ds(2 * c + j, 1), 1, :].to_broadcast([P, 2, C]),
                                                       ALU.mult)
                    last.then_inc(s1["upd"], 1)

                def add_update(c, buf):
                    dve.wait_ge(s1["upd"], c + 1)
                    xc = x[:, bass.ds(2 * c, 2), :, :].rearrange("p b h c -> p (b h) c")
                    nc.vector.tensor_tensor(xc, xc, acc[:, buf], ALU.add).then_inc(s1["x2"], 1)

                def statistics(c):
                    dve.wait_ge(s1["x2"], c + 1)
                    dve.wait_ge(const_done, 1)
                    for t in range(CH):
                        last = nc.vector.bn_stats(stats[:, 2 * c + t // 2, t % 2, :], x[:, 2 * c + t // 2, t % 2, :])
                    last.then_inc(s1["st"], 1)

                def chunk(c, buf, former, has_next):
                    def hidden(k):
                        if former or k // MT >= 2:
                            dve.wait_ge(s1["out"], E0 * c + k // MT - 1)
                        dve.wait_ge(s1["silu"], NK * c + k + 1)
                        nc.vector.scalar_tensor_tensor(out=hid[:, k // MT % 2, k % MT, :], in0=ps[4 + k % 2][:],
                                                       scalar=b_gu[:, 1, k:k + 1], in1=act_g[:, k % 2, :],
                                                       op0=ALU.add, op1=ALU.mult).then_inc(s1["hid"], 1)

                    for k in range(NK):
                        hidden(k)
                        if k % MT == 0 and k >= 2 * MT:
                            accumulate(c, buf, k // MT - 2)
                        elif k % MT == 0 and former:
                            accumulate(c - 1, 1 - buf, E0 - 2 + k // MT)
                        if k == 1:
                            dve.wait_ge(s1["w_t_psum"], c + 1)
                            nc.vector.tensor_copy(w_exp_t[:], ps[1][:, 0:P]).then_inc(s1["w_t"], 1)
                        if k == 5 and former:
                            gate(c - 1, 1 - buf)
                        if k == 7 and former:
                            add_update(c - 1, 1 - buf)
                        if k == 8 and former:
                            statistics(c - 1)
                        if has_next:
                            if k == 5:
                                dve.wait_ge(ln_rstd, 4)
                                normalise(c + 1)
                            if k == 9:
                                upper_tokens(c + 1, 1 - buf)
                            if k == 11:
                                logits_below_maximum(c + 1)
                            if k == 13:
                                probabilities(c + 1)
                                largest(c + 1, 0, prob, first)
                            if k == 14:
                                without_first(c + 1)
                                largest(c + 1, 1, left, second)
                            if k == 15:
                                expert_weights(c + 1, 1 - buf)

                nc.vector.memset(w_exp[:], 0.0).then_inc(s1["zero"], 1)
                dve.wait_ge(s1["zero"], 1)
                dve.wait_ge(ln_rstd, 3)
                normalise(0)
                upper_tokens(0, 0)
                logits_below_maximum(0)
                probabilities(0)
                largest(0, 0, prob, first)
                without_first(0)
                largest(0, 1, left, second)
                expert_weights(0, 0)
                chunks(dve, chunk)
                for e in range(E0 - 2, E0):
                    accumulate(NCH - 1, 1, e)
                gate(NCH - 1, 1)
                add_update(NCH - 1, 1)
                statistics(NCH - 1)
                dve.wait_ge(s1["st"], NCH)
                token_variances(dve, 2)

            @block.gpsimd
            def _(pool):
                def lower_tokens(c, buf, former, has_next):
                    pool.wait_ge(s1["h_hi"], c + 1)
                    nc.gpsimd.tensor_tensor(h_lo[:, buf, :], h4[:, buf, :], h_hi[:, buf, :].bitcast(F32),
                                            ALU.subtract).then_inc(s1["h_lo"], 1)

                token_scales(pool, 1)
                chunks(pool, lower_tokens)
        phase.close()
        layer0.close()

        phase = ExitStack()
        xn1 = sb("xn1", [P, 2, C], until=phase)
        h1t = sb("h1t", [P, 2, P], until=phase)
        q1_t = sb("q1_t", [P, 2, P], until=phase)
        qkv = sb("qkv", [P, NHALF, NB, 3, C], until=phase)
        AHEAD = 2
        q_all = sb("q_all", [P, NB + AHEAD, P], until=phase)
        prod_s = sb("prod_s", [P, 2, D, H, NB], until=phase)
        score = sb("score", [P, 2, H, NB], until=phase)
        e1 = sb("e1", [P, 2, H, NB], until=phase)
        e1_t = sb("e1_t", [P, 2 * P], until=phase)
        smax = sb("smax", [P, H], until=phase)
        ssum = sb("ssum", [P, 2, H], until=phase)
        sinv = sb("sinv", [P, 2, H], until=phase)
        prod_v = sb("prod_v", [P, 2, H, D, NB], until=phase)
        mix = sb("mix", [P, C], until=phase)
        mix_rel = sb("mix_rel", [P, C], until=phase)
        att = sb("att", [P, C], until=phase)
        att_t = sb("att_t", [P, P], until=phase)
        upd1 = sb("upd1", [P, C], until=phase)
        SCALE1 = float(D) ** -0.5
        POOL_HEADS = 5

        s2 = {n: sem("a1_" + n) for n in (
            "xn", "x_t", "h", "q_psum", "qkv_psum", "q_t", "qkv", "q_one", "prod_s", "dots", "max", "score",
            "exp", "sum", "inv", "e_t_psum", "e_t", "rv", "prod_v_dve", "prod_v_pool", "mix", "mix_rel", "att",
            "att_t_psum", "att_t", "proj", "gated", "x3", "st")}
        rk = l1["rk"]

        def projections(eng, load, project):
            load(0, 0, 0)
            project(0, 0, 0, (0, 1, 1))
            project(0, 1, 1, (0, 2, 0))
            with eng.Fori(0, NB // 2 - 2) as pair:
                project(0, 2 * pair + 2, 0, (0, 2 * pair + 3, 1))
                project(0, 2 * pair + 3, 1, (0, 2 * pair + 4, 0))
            project(0, NB - 2, 0, (0, NB - 1, 1))
            project(0, NB - 1, 1)
            for t in range(AHEAD):
                load(1, t, t)
                project(1, t, t)

        def attention(eng, step):
            step(0, 0, 0, None, None, 2)
            step(0, 1, 1, (0, 0), None, 3)
            step(0, 2, 0, (0, 1), (0, 0), 4)
            step(0, 3, 1, (0, 2), (0, 1), 5)
            with eng.Fori(0, NB // 2 - 4) as pair:
                step(0, 2 * pair + 4, 0, (0, 2 * pair + 3), (0, 2 * pair + 2), 2 * pair + 6)
                step(0, 2 * pair + 5, 1, (0, 2 * pair + 4), (0, 2 * pair + 3), 2 * pair + 7)
            step(0, NB - 4, 0, (0, NB - 5), (0, NB - 6), NB - 2)
            step(0, NB - 3, 1, (0, NB - 4), (0, NB - 5), NB - 1)
            step(0, NB - 2, 0, (0, NB - 3), (0, NB - 4), None)
            step(0, NB - 1, 1, (0, NB - 2), (0, NB - 3), None)
            step(1, 0, 0, (0, NB - 1), (0, NB - 2), None)
            step(1, 1, 1, (1, 0), (0, NB - 1), None)
            with eng.Fori(0, NB // 2 - 1) as pair:
                step(1, 2 * pair + 2, 0, (1, 2 * pair + 1), (1, 2 * pair), None)
                step(1, 2 * pair + 3, 1, (1, 2 * pair + 2), (1, 2 * pair + 1), None)

        def at(half, t):
            return t + NB * half

        def query_slot(half, t):
            return t if half == 0 else NB + t if isinstance(t, int) and t < AHEAD else t - AHEAD

        def former(eng, signal, n):
            if not isinstance(n, int) or n > 0:
                eng.wait_ge(s2[signal], n)

        def turned(half):
            return (ps[4] if half == 0 else po)[:, 0:P]

        def query_bank(half):
            return (ps[2] if half == 0 else po)[:, P:2 * P]

        def qkv_bank(half, buf):
            return ps[5][:, 0:3 * C] if half == 0 and buf == 1 else po[:, 512:512 + 3 * C]

        with nc.Block() as block:
            @block.tensor
            def _(pe):
                def load(half, t, buf):
                    m = at(half, t)
                    former(pe, "h" if half == 0 else "q_t", m)
                    pe.wait_ge(s2["xn"], m + 1)
                    nc.tensor.transpose(turned(half), xn1[:, buf, :], eye[:]).then_inc(s2["x_t"], 1)

                def project(half, t, buf, meanwhile=None):
                    m = at(half, t)
                    banks = 2 if half == 0 else 1
                    former(pe, "q_t", m)
                    pe.wait_ge(s2["h"], m + 1)
                    nc.tensor.matmul(query_bank(half), l1["w_qkv1"][:, 0:C], h1t[:, buf, :], start=True,
                                     stop=True).then_inc(s2["q_psum"], 1)
                    former(pe, "qkv", m + 1 - banks)
                    bank = qkv_bank(half, buf)
                    nc.tensor.matmul(bank, h1t[:, buf, :], l1["w_qkv1"][:], start=True,
                                     stop=True).then_inc(s2["qkv_psum"], 1)
                    if meanwhile is not None:
                        load(*meanwhile)

                def dots(half, t, buf):
                    n = at(half, t)
                    pe.wait_ge(s2["prod_s"], n + 1)
                    for d in range(D):
                        if d == D - 1:
                            pe.wait_ge(s2["q_one"], n + 1)
                        nc.tensor.matmul(ps[buf][:, 0:H * NB], eye[:], prod_s[:, buf, d, :, :].rearrange("p h s -> p (h s)"),
                                         start=(d == 0), stop=False)
                    last = nc.tensor.matmul(ps[buf][:, 0:H * NB], q1_t[:, buf, :], rk[:, :, bass.ds(MAXREL - t, NB)],
                                            start=False, stop=True)
                    last.then_inc(s2["dots"], 1)

                def turn_exp(half, t, buf):
                    n = at(half, t)
                    pe.wait_ge(s2["exp"], n + 1)
                    for j in range(2):
                        last = nc.tensor.transpose(ps[2][:, j * P:(j + 1) * P],
                                                   e1[:, buf, 8 * j:8 * j + 8, :].rearrange("p h s -> p (h s)"), eye[:])
                    last.then_inc(s2["e_t_psum"], 1)

                def relative_values(half, t):
                    n = at(half, t)
                    pe.wait_ge(s2["e_t"], n + 1)
                    for j in range(2):
                        last = nc.tensor.matmul(ps[3][:, j * 64:(j + 1) * 64], e1_t[:, j * P:(j + 1) * P],
                                                l1["rv"][:, bass.ds(t, 1), :, :], start=True, stop=True)
                    last.then_inc(s2["rv"], 1)

                def turn_att(half, t):
                    n = at(half, t)
                    pe.wait_ge(s2["att"], n + 1)
                    nc.tensor.transpose(ps[4][:, 0:P], att[:], eye[:]).then_inc(s2["att_t_psum"], 1)

                def out_projection(half, t):
                    n = at(half, t)
                    former(pe, "gated", n)
                    pe.wait_ge(s2["att_t"], n + 1)
                    nc.tensor.matmul(ps[5][:, 0:C], eye[:], l1["b_o1"][:], start=True, stop=False)
                    nc.tensor.matmul(ps[5][:, 0:C], att_t[:], l1["w_o1"][:], start=False, stop=True).then_inc(s2["proj"], 1)

                def step(half, t, buf, one, two, ahead):
                    if ahead is not None:
                        load(1, ahead, buf)
                    if one is not None:
                        turn_exp(*one, 1 - buf)
                    if two is not None:
                        pe.wait_ge(s2["score"], at(half, t) - 1)
                    dots(half, t, buf)
                    if two is not None:
                        turn_att(*two)
                    if ahead is not None:
                        project(1, ahead, buf)
                    if one is not None:
                        relative_values(*one)
                    if two is not None:
                        out_projection(*two)

                spread_gates(pe, 1)
                pe.wait_ge(gates_kept, NB)
                projections(pe, load, project)
                attention(pe, step)
                turn_exp(1, NB - 1, 1)
                turn_att(1, NB - 2)
                relative_values(1, NB - 1)
                out_projection(1, NB - 2)
                turn_att(1, NB - 1)
                out_projection(1, NB - 1)

            @block.scalar
            def _(act):
                def load(half, t, buf):
                    m = at(half, t)
                    act.wait_ge(s2["x_t"], m + 1)
                    former(act, "qkv_psum", m - 1)
                    nc.scalar.activation(h1t[:, buf, :], turned(half), ACT.Identity, scale=mod[:, 1, 1, bass.ds(t, 1)],
                                         bias=mod[:, 1, 0, bass.ds(t, 1)]).then_inc(s2["h"], 1)

                def queries(half, t, buf):
                    nc.scalar.activation(q_all[:, query_slot(half, t), :], query_bank(half), ACT.Identity,
                                         bias=l1["b_q1"][:]).then_inc(s2["q_t"], 1)

                def keep_query(half, t, buf):
                    n = at(half, t)
                    former(act, "dots", n - 1)
                    act.wait_ge(s2["q_t"], n + 1)
                    nc.scalar.copy(q1_t[:, buf, :], q_all[:, query_slot(half, t), :]).then_inc(s2["q_one"], 1)

                def project(half, t, buf, meanwhile=None):
                    act.wait_ge(s2["q_psum"], at(half, t) + 1)
                    queries(half, t, buf)
                    if meanwhile is not None:
                        load(*meanwhile)

                def turned_exp(half, t):
                    n = at(half, t)
                    former(act, "rv", n)
                    act.wait_ge(s2["e_t_psum"], n + 1)
                    nc.scalar.copy(e1_t[:], ps[2][:, 0:2 * P]).then_inc(s2["e_t"], 1)

                def turned_att(half, t):
                    n = at(half, t)
                    former(act, "proj", n)
                    act.wait_ge(s2["att_t_psum"], n + 1)
                    nc.scalar.copy(att_t[:], ps[4][:, 0:P]).then_inc(s2["att_t"], 1)

                def step(half, t, buf, one, two, ahead):
                    n = at(half, t)
                    keep_query(half, t, buf)
                    if ahead is not None:
                        load(1, ahead, buf)
                    if one is not None:
                        turned_exp(*one)
                    if ahead is not None:
                        act.wait_ge(s2["q_psum"], at(1, ahead) + 1)
                    if two is not None:
                        turned_att(*two)
                    if ahead is not None:
                        queries(1, ahead, buf)
                    if two is not None:
                        act.wait_ge(s2["mix"], n - 1)
                    act.wait_ge(s2["score"], n + 1)
                    nc.scalar.activation(e1[:, buf], score[:, buf], ACT.Exp, scale=SCALE1).then_inc(s2["exp"], 1)

                keep_gates(act, 1)
                projections(act, load, project)
                attention(act, step)
                turned_exp(1, NB - 1)
                turned_att(1, NB - 2)
                turned_att(1, NB - 1)

            @block.gpsimd
            def _(pool):
                def key_products(half, t, buf):
                    n = at(half, t)
                    qv = qkv[:, half, t, 0, :].rearrange("p (h d) -> p d h", d=D)
                    kv = qkv[:, half, :, 1, :].rearrange("p s (h d) -> p d h s", d=D)
                    nc.gpsimd.tensor_tensor(prod_s[:, buf], qv.unsqueeze(3).to_broadcast([P, D, H, NB]), kv,
                                            ALU.mult).then_inc(s2["prod_s"], 1)

                def value_products(half, t, buf):
                    n = at(half, t)
                    pool.wait_ge(s2["exp"], n + 1)
                    former(pool, "mix", n - 1)
                    nc.gpsimd.tensor_tensor(
                        prod_v[:, buf, 0:POOL_HEADS], e1[:, buf, 0:POOL_HEADS, :].unsqueeze(2).to_broadcast(
                            [P, POOL_HEADS, D, NB]),
                        qkv[:, half, :, 2, 0:POOL_HEADS * D].rearrange("p s (h d) -> p h d s", d=D),
                        ALU.mult).then_inc(s2["prod_v_pool"], 1)

                def step(half, t, buf, one, two, ahead):
                    if two is not None:
                        pool.wait_ge(s2["dots"], at(half, t) - 1)
                    pool.wait_ge(s2["qkv"], NB * (half + 1))
                    key_products(half, t, buf)
                    if one is not None:
                        value_products(*one, 1 - buf)

                token_scales(pool, 2)
                attention(pool, step)
                value_products(1, NB - 1, 1)

            @block.vector
            def _(dve):
                def load(half, t, buf):
                    m = at(half, t)
                    if not isinstance(t, int) or t <= 2:
                        dve.wait_ge(ln_rstd, 5 if isinstance(t, int) and t < 2 else 6)
                    former(dve, "x_t", m - 1)
                    nc.vector.tensor_scalar(xn1[:, buf, :], x[:, t, half, :], mean[:, t, half:half + 1],
                                            rstd[:, t, half:half + 1], ALU.subtract, ALU.mult).then_inc(s2["xn"], 1)

                def project(half, t, buf):
                    m = at(half, t)
                    dve.wait_ge(s2["qkv_psum"], m + 1)
                    nc.vector.tensor_tensor(qkv[:, half, t, :, :].rearrange("p j c -> p (j c)"),
                                            qkv_bank(half, buf), l1["b_qkv1"][:], ALU.add).then_inc(s2["qkv"], 1)

                def maximum(half, t, buf):
                    n = at(half, t)
                    dve.wait_ge(s2["dots"], n + 1)
                    nc.vector.tensor_reduce(smax[:], ps[buf][:, 0:H * NB].rearrange("p (h s) -> p h s", s=NB), AX.X,
                                            ALU.max).then_inc(s2["max"], 1)

                def subtract(half, t, buf):
                    n = at(half, t)
                    dve.wait_ge(s2["max"], n + 1)
                    nc.vector.tensor_tensor(score[:, buf], ps[buf][:, 0:H * NB].rearrange("p (h s) -> p h s", s=NB),
                                            smax[:].unsqueeze(2).to_broadcast([P, H, NB]),
                                            ALU.subtract).then_inc(s2["score"], 1)

                def exp_sums(half, t, buf):
                    n = at(half, t)
                    dve.wait_ge(s2["exp"], n + 1)
                    nc.vector.tensor_reduce(ssum[:, buf], e1[:, buf], AX.X, ALU.add).then_inc(s2["sum"], 1)

                def value_products(half, t, buf):
                    n = at(half, t)
                    rest = H - POOL_HEADS
                    nc.vector.tensor_tensor(
                        prod_v[:, buf, POOL_HEADS:], e1[:, buf, POOL_HEADS:, :].unsqueeze(2).to_broadcast([P, rest, D, NB]),
                        qkv[:, half, :, 2, POOL_HEADS * D:].rearrange("p s (h d) -> p h d s", d=D),
                        ALU.mult).then_inc(s2["prod_v_dve"], 1)

                def inverse(half, t, buf):
                    n = at(half, t)
                    dve.wait_ge(s2["sum"], n + 1)
                    nc.vector.reciprocal(sinv[:, buf], ssum[:, buf]).then_inc(s2["inv"], 1)

                def mix_values(half, t, buf):
                    n = at(half, t)
                    dve.wait_ge(s2["prod_v_dve"], n + 1)
                    dve.wait_ge(s2["prod_v_pool"], n + 1)
                    nc.vector.tensor_reduce(mix[:], prod_v[:, buf].rearrange("p h d s -> p (h d) s"), AX.X,
                                            ALU.add).then_inc(s2["mix"], 1)

                def add_relative(half, t):
                    n = at(half, t)
                    dve.wait_ge(s2["mix"], n + 1)
                    dve.wait_ge(s2["rv"], n + 1)
                    nc.vector.tensor_tensor(mix_rel[:], ps[3][:, 0:C], mix[:], ALU.add).then_inc(s2["mix_rel"], 1)

                def divide(half, t, buf):
                    n = at(half, t)
                    former(dve, "att_t_psum", n)
                    dve.wait_ge(s2["inv"], n + 1)
                    dve.wait_ge(s2["mix_rel"], n + 1)
                    nc.vector.tensor_tensor(att[:].rearrange("p (h d) -> p h d", d=D),
                                            mix_rel[:].rearrange("p (h d) -> p h d", d=D),
                                            sinv[:, buf].unsqueeze(2).to_broadcast([P, H, D]), ALU.mult).then_inc(s2["att"], 1)

                def gate(half, t):
                    n = at(half, t)
                    dve.wait_ge(s2["proj"], n + 1)
                    nc.vector.tensor_tensor(upd1[:], ps[5][:, 0:C], gates[:, t, 0, :], ALU.mult).then_inc(s2["gated"], 1)

                def add_update(half, t):
                    n = at(half, t)
                    dve.wait_ge(s2["gated"], n + 1)
                    nc.vector.tensor_tensor(x[:, t, half, :], x[:, t, half, :], upd1[:], ALU.add).then_inc(s2["x3"], 1)

                def statistics(half, t):
                    n = at(half, t)
                    dve.wait_ge(s2["x3"], n + 1)
                    dve.wait_ge(const_done, 1)
                    nc.vector.bn_stats(stats[:, t, half, :], x[:, t, half, :]).then_inc(s2["st"], 1)

                def step(half, t, buf, one, two, ahead):
                    maximum(half, t, buf)
                    subtract(half, t, buf)
                    if ahead is not None and not (isinstance(ahead, int) and ahead == NB - 1):
                        load(1, ahead + 1, 1 - buf)
                    if one is not None:
                        mix_values(*one, 1 - buf)
                    if two is not None:
                        gate(*two)
                    exp_sums(half, t, buf)
                    value_products(half, t, buf)
                    if two is not None:
                        add_update(*two)
                    inverse(half, t, buf)
                    if one is not None:
                        add_relative(*one)
                    if ahead is not None:
                        project(1, ahead, buf)
                    if one is not None:
                        divide(*one, 1 - buf)
                    if two is not None:
                        statistics(*two)

                load(0, 0, 0)
                load(0, 1, 1)
                load(0, 2, 0)
                project(0, 0, 0)
                load(0, 3, 1)
                project(0, 1, 1)
                with dve.Fori(0, NB // 2 - 2) as pair:
                    load(0, 2 * pair + 4, 0)
                    project(0, 2 * pair + 2, 0)
                    load(0, 2 * pair + 5, 1)
                    project(0, 2 * pair + 3, 1)
                for t in range(AHEAD):
                    load(1, t, t)
                    project(0, NB - AHEAD + t, t)
                for t in range(AHEAD):
                    project(1, t, t)
                load(1, AHEAD, 0)
                attention(dve, step)
                mix_values(1, NB - 1, 1)
                gate(1, NB - 2)
                add_relative(1, NB - 1)
                add_update(1, NB - 2)
                divide(1, NB - 1, 1)
                statistics(1, NB - 2)
                gate(1, NB - 1)
                add_update(1, NB - 1)
                statistics(1, NB - 1)
                dve.wait_ge(s2["st"], NHALF * NB)
                token_variances(dve, 3)
        phase.close()

        phase = ExitStack()
        h_all = sb("h_all", [P, NB, T], until=phase)
        enc = sb("enc", [P, 2, 2, T], until=phase)
        NP = E1 // 2
        diff = sb("diff", [P, NP, 2, T], until=phase)
        WIDE = (0, 2)
        POOL_R = 24
        losses = sb("losses", [P, NB, E1], until=phase)
        ones = sb("ones", [P, P], until=phase)
        least = sb("least", [P, NB], until=phase)
        is_least = sb("is_least", [P, NB, E1], until=phase)
        chosen = sb("chosen", [P, NB, E1], until=phase)
        down_m = sb("down_m", [P, R, E1], until=phase)
        down_w = sb("down_w", [P, 2, R], until=phase)
        down_bm = sb("down_bm", [R, E1], until=phase)
        down_b = sb("down_b", [R, 2], until=phase)
        up_m = sb("up_m", [P, 2, C, E1], until=phase)
        up_w = sb("up_w", [P, 2, C], until=phase)
        a_t = sb("a_t", [P, 2, T], until=phase)
        h_one = sb("h_one", [P, 2, T], until=phase)
        upd2 = sb("upd2", [P, 2, NHALF, C], until=phase)
        s3 = {n: sem("e1_" + n) for n in (
            "init", "xn", "x_t", "h", "enc_psum", "enc", "rec", "diff", "sq", "loss", "loss_psum", "argmin", "route",
            "down_m", "down_m_pool", "down_w", "up_m", "up_w", "code", "h_one", "a_t", "up", "upd", "x4")}
        out_done = sem("out_done")

        def sweep(eng, step):
            step(0, 0, True, 2)
            with eng.Fori(0, NB // 2 - 2) as pair:
                step(2 * pair + 1, 1, False, 2)
                step(2 * pair + 2, 0, False, 2)
            step(NB - 3, 1, False, 2)
            step(NB - 2, 0, False, 1)
            step(NB - 1, 1, False, 0)

        with nc.Block() as block:
            @block.tensor
            def _(pe):
                def turn(b):
                    pe.wait_ge(s3["xn"], b + 1)
                    for h in range(NHALF):
                        last = nc.tensor.transpose(ps[0][:, h * P:(h + 1) * P], xn[:, h, :], eye[:])
                    last.then_inc(s3["x_t"], 1)

                def encode(b):
                    pe.wait_ge(s3["h"], b + 1)
                    for j in range(2):
                        last = nc.tensor.matmul(ps[1][:, j * T:(j + 1) * T], l1["w_d1"][:, j * P:(j + 1) * P],
                                                h_all[:, b, :], start=True, stop=True)
                    last.then_inc(s3["enc_psum"], 1)

                def reconstruct(b, buf, first, p):
                    if not first:
                        pe.wait_ge(s3["diff"], NP * b + p + 1 - NP)
                    pe.wait_ge(s3["enc"], 2 * b + p // 2 + 1)
                    for j in range(2):
                        last = nc.tensor.matmul(ps[2 + p][:, j * T:(j + 1) * T], l1["w_d2"][:, 2 * p + j, :],
                                                enc[:, buf, p // 2, :], start=True, stop=True)
                    last.then_inc(s3["rec"], 1)

                def step(b, buf, first, to_come):
                    reconstruct(b, buf, first, 0)
                    reconstruct(b, buf, first, 1)
                    if to_come:
                        turn(b + 1)
                    reconstruct(b, buf, first, 2)
                    if to_come:
                        encode(b + 1)
                    reconstruct(b, buf, first, 3)

                def adapt(b, buf, first, to_come):
                    if not first:
                        pe.wait_ge(s3["a_t"], b)
                    pe.wait_ge(s3["down_w"], b + 1)
                    nc.tensor.matmul(ps[0][0:R, 0:T], down_w[:, buf, :], h_all[:, b, :], start=True,
                                     stop=True).then_inc(s3["code"], 1)
                    pe.wait_ge(s3["h_one"], b + 1)
                    for h in range(NHALF):
                        nc.tensor.matmul(ps[4 + buf][:, h * C:(h + 1) * C], h_one[:, buf, h * P:(h + 1) * P],
                                         l1["w_base"][:], start=True, stop=False)
                        if h == 0:
                            pe.wait_ge(s3["up_w"], b + 1)
                            pe.wait_ge(s3["a_t"], b + 1)
                        last = nc.tensor.matmul(ps[4 + buf][:, h * C:(h + 1) * C], a_t[:, buf, h * P:(h + 1) * P],
                                                up_w[:, buf, :], start=False, stop=True)
                    last.then_inc(s3["up"], 1)

                turn(0)
                encode(0)
                sweep(pe, step)
                pe.wait_ge(s3["sq"], NP * NB)
                pe.wait_ge(s3["loss"], len(WIDE) * NB)
                nc.tensor.matmul(po[:, 0:NB * E1], ones[:], losses[:].rearrange("p b e -> p (b e)"), start=True,
                                 stop=True).then_inc(s3["loss_psum"], 1)
                sweep(pe, adapt)

            @block.scalar
            def _(act):
                def modulate(b):
                    act.wait_ge(s3["x_t"], b + 1)
                    nc.scalar.activation(h_all[:, b, :], ps[0][:, 0:T], ACT.Identity, scale=mod[:, 1, 3, bass.ds(b, 1)],
                                         bias=mod[:, 1, 2, bass.ds(b, 1)]).then_inc(s3["h"], 1)

                def codes(b, buf):
                    act.wait_ge(s3["enc_psum"], b + 1)
                    for j in range(2):
                        nc.scalar.activation(enc[:, buf, j, :], ps[1][:, j * T:(j + 1) * T], ACT.Relu,
                                             bias=l1["b_d1"][:, j:j + 1]).then_inc(s3["enc"], 1)

                def squares(b, p):
                    act.wait_ge(s3["diff"], NP * b + p + 1)
                    if p in WIDE:
                        last = nc.scalar.activation(diff[:, p], diff[:, p], ACT.Square)
                    else:
                        for j in range(2):
                            last = nc.scalar.activation(diff[:, p, j, :], diff[:, p, j, :], ACT.Square,
                                                        accum_out=losses[:, b, 2 * p + j:2 * p + j + 1])
                    last.then_inc(s3["sq"], 1)

                def step(b, buf, first, to_come):
                    squares(b, 0)
                    if to_come:
                        modulate(b + 1)
                    squares(b, 1)
                    squares(b, 2)
                    if to_come:
                        codes(b + 1, 1 - buf)
                    squares(b, 3)

                def adapt(b, buf, first, to_come):
                    if not first:
                        act.wait_ge(s3["up"], b)
                    nc.scalar.copy(h_one[:, buf, :], h_all[:, b, :]).then_inc(s3["h_one"], 1)
                    act.wait_ge(s3["down_w"], b + 1)
                    act.wait_ge(s3["code"], b + 1)
                    nc.scalar.activation(a_t[0:R, buf, :], ps[0][0:R, 0:T], ACT.Relu,
                                         bias=down_b[:, buf:buf + 1]).then_inc(s3["a_t"], 1)

                modulate(0)
                codes(0, 0)
                sweep(act, step)
                act.wait_ge(s3["init"], 2)
                sweep(act, adapt)

            @block.gpsimd
            def _(pool):
                token_scales(pool, 3)

                def adapt(b, buf, first, to_come):
                    if not first:
                        pool.wait_ge(s3["down_w"], b)
                    nc.gpsimd.tensor_tensor(down_m[:, 0:POOL_R], l1["w_ad"][:, 0:POOL_R],
                                            chosen[:, b, :].unsqueeze(1).to_broadcast([P, POOL_R, E1]),
                                            ALU.mult).then_inc(s3["down_m_pool"], 1)
                    nc.gpsimd.tensor_tensor(up_m[:, buf], l1["w_au"][:], chosen[:, b, :].unsqueeze(1).to_broadcast([P, C, E1]),
                                            ALU.mult).then_inc(s3["up_m"], 1)

                pool.wait_ge(s3["route"], 1)
                sweep(pool, adapt)

            @block.vector
            def _(dve):
                def normalise(b):
                    for h in range(NHALF):
                        last = nc.vector.tensor_scalar(xn[:, h, :], x[:, b, h, :], mean[:, b, h:h + 1],
                                                       rstd[:, b, h:h + 1], ALU.subtract, ALU.mult)
                    last.then_inc(s3["xn"], 1)

                def differences(b, first, p):
                    if not first:
                        dve.wait_ge(s3["sq"], NP * b + p + 1 - NP)
                        if p in WIDE:
                            dve.wait_ge(s3["loss"], len(WIDE) * (b - 1) + WIDE.index(p) + 1)
                    dve.wait_ge(s3["rec"], NP * b + p + 1)
                    for j in range(2):
                        last = nc.vector.scalar_tensor_tensor(
                            out=diff[:, p, j, :], in0=ps[2 + p][:, j * T:(j + 1) * T],
                            scalar=l1["b_d2"][:, 2 * p + j:2 * p + j + 1], in1=h_all[:, b, :], op0=ALU.add,
                            op1=ALU.subtract)
                    last.then_inc(s3["diff"], 1)

                def sums(b, p):
                    dve.wait_ge(s3["sq"], NP * b + p + 1)
                    nc.vector.tensor_reduce(losses[:, b, 2 * p:2 * p + 2], diff[:, p], AX.X, ALU.add).then_inc(s3["loss"], 1)

                def step(b, buf, first, to_come):
                    differences(b, first, 0)
                    differences(b, first, 1)
                    sums(b, 0)
                    differences(b, first, 2)
                    if to_come == 2:
                        dve.wait_ge(ln_rstd, 8)
                        dve.wait_ge(s3["x_t"], b + 2)
                        normalise(b + 2)
                    differences(b, first, 3)
                    sums(b, 2)

                def chosen_down(b, buf, first):
                    pick = lambda rows, n: chosen[0:rows, b, :].unsqueeze(1).to_broadcast([rows, n, E1])
                    if not first:
                        dve.wait_ge(s3["down_w"], b)
                    nc.vector.tensor_tensor(down_bm[:], l1["b_ad"][:], chosen[0:R, b, :], ALU.mult)
                    nc.vector.tensor_tensor(down_m[:, POOL_R:], l1["w_ad"][:, POOL_R:], pick(P, R - POOL_R),
                                            ALU.mult).then_inc(s3["down_m"], 1)
                    dve.wait_ge(s3["down_m"], b + 1)
                    dve.wait_ge(s3["down_m_pool"], b + 1)
                    nc.vector.tensor_reduce(down_b[:, buf:buf + 1], down_bm[:], AX.X, ALU.add)
                    nc.vector.tensor_reduce(down_w[:, buf, :], down_m[:], AX.X, ALU.add).then_inc(s3["down_w"], 1)

                def chosen_up(b, buf):
                    dve.wait_ge(s3["up_m"], b + 1)
                    nc.vector.tensor_reduce(up_w[:, buf, :], up_m[:, buf], AX.X, ALU.add).then_inc(s3["up_w"], 1)

                def gate(b, buf):
                    dve.wait_ge(s3["up"], b + 1)
                    nc.vector.tensor_tensor(upd2[:, buf], ps[4 + buf][:, 0:T].rearrange("p (h c) -> p h c", h=NHALF),
                                            gates[:, bass.ds(b, 1), 1, :].to_broadcast([P, NHALF, C]),
                                            ALU.mult).then_inc(s3["upd"], 1)

                def add_update(b, buf):
                    dve.wait_ge(s3["upd"], b + 1)
                    nc.vector.tensor_tensor(x[:, b], x[:, b], upd2[:, buf], ALU.add).then_inc(s3["x4"], 1)

                def adapt(b, buf, first, to_come):
                    chosen_down(b, buf, first)
                    chosen_up(b, buf)
                    if not first:
                        gate(b - 1, 1 - buf)
                    if not first:
                        add_update(b - 1, 1 - buf)

                nc.vector.memset(ones[:], 1.0)
                nc.vector.memset(a_t[R:P], 0.0).then_inc(s3["init"], 1)
                dve.wait_ge(s3["init"], 1)
                nc.vector.memset(a_t[R:R + 2], 1.0).then_inc(s3["init"], 1)
                dve.wait_ge(ln_rstd, 7)
                normalise(0)
                dve.wait_ge(s3["x_t"], 1)
                normalise(1)
                sweep(dve, step)
                dve.wait_ge(s3["loss_psum"], 1)
                ls = po[:, 0:NB * E1].rearrange("p (b e) -> p b e", e=E1)
                wide = lambda v: v.unsqueeze(2).to_broadcast([P, NB, E1])
                nc.vector.tensor_reduce(least[:], ls, AX.X, ALU.min).then_inc(s3["argmin"], 1)
                dve.wait_ge(s3["argmin"], 1)
                nc.vector.tensor_tensor(is_least[:], ls, wide(least[:]), ALU.is_equal).then_inc(s3["argmin"], 1)
                dve.wait_ge(s3["argmin"], 2)
                nc.vector.tensor_tensor(is_least[:], is_least[:], order[:].unsqueeze(1).to_broadcast([P, NB, E1]),
                                        ALU.mult).then_inc(s3["argmin"], 1)
                dve.wait_ge(s3["argmin"], 3)
                nc.vector.tensor_reduce(least[:], is_least[:], AX.X, ALU.max).then_inc(s3["argmin"], 1)
                dve.wait_ge(s3["argmin"], 4)
                nc.vector.tensor_tensor(chosen[:], is_least[:], wide(least[:]), ALU.is_equal).then_inc(s3["route"], 1)
                dve.wait_ge(s3["route"], 1)
                sweep(dve, adapt)
                gate(NB - 1, 1)
                add_update(NB - 1, 1)

            @block.sync
            def _(sp):
                ov = out.rearrange("b (h p) c -> b p h c", p=P)
                with sp.Fori(0, NB) as b:
                    sp.wait_ge(s3["x4"], b + 1)
                    sp.dma_start(ov[b], x[:, b]).then_inc(out_done, 16)
                sp.wait_ge(out_done, 16 * NB)
        phase.close()


def lay_out(d):
    g = {k: np.asarray(v) for k, v in d.items()}
    half = D // 2
    ch = np.arange(C)
    partner = (ch // D) * D + (ch % D + half) % D
    wa = g["L0_attn_w_attn"]
    q, k, v = wa[:C], wa[C:2 * C], wa[2 * C:]
    r = {"x": g["L0_attn_x"]}
    r["wqkv0"] = np.stack([q.T, k.T, q[partner].T, k[partner].T, v.T], 1)
    r["wproj0"] = g["L0_attn_w_proj"].T
    r["cT"] = np.stack([g["L0_c"].T, g["L1_c"].T], 1)
    r["wmod"] = np.stack([g[n].reshape(C, 6, C)[:, [0, 1, 3, 4, 2, 5]] for n in ("L0_wmod", "L1_wmod")], 1)
    r["wgu"] = np.stack([g["L0_ffn_W_" + n].transpose(1, 0, 2).reshape(C, E0 * M) for n in ("gate", "up")], 1)
    r["wout"] = g["L0_ffn_W_out"].reshape(E0, MT, P, C).transpose(2, 0, 1, 3)
    r["bgu"] = np.stack([g["L0_ffn_b_gate"].reshape(E0 * MT, P).T, g["L0_ffn_b_up"].reshape(E0 * MT, P).T], 1)
    bo = np.zeros((P, 4, C), np.float32)
    for i in range(4):
        bo[i * E0:(i + 1) * E0, i] = g["L0_ffn_b_out"]
    r["bout"] = bo
    r["wrouter"] = g["L0_ffn_W_router"]
    row = lambda n: np.broadcast_to(g[n].reshape(1, -1), (P, g[n].size))
    r["w_qkv1"] = np.concatenate([g["L1_attn_W" + n].T for n in "qkv"], 1)
    r["b_qkv1"] = np.concatenate([row("L1_attn_b" + n) for n in "qkv"], 1)
    r["b_q1"] = g["L1_attn_bq"].reshape(C, 1)
    rk = np.zeros((C, H, 2 * MAXREL + 1), np.float32)
    rv = np.zeros((P, 16, 8, D), np.float32)
    for h in range(H):
        rk[h * D:(h + 1) * D, h] = g["L1_attn_rk_table"].T
    for h in range(8):
        for t in range(16):
            rv[h * 16:(h + 1) * 16, t, h] = g["L1_attn_rv_table"][MAXREL - t:2 * MAXREL - t]
    r["rk"], r["rv"] = rk, rv
    r["w_o1"] = g["L1_attn_Wo"].T
    r["b_o1"] = row("L1_attn_bo")
    r["w_base"] = g["L1_ffn_W_base"]
    r["w_d1"] = g["L1_ffn_Wd1"].transpose(1, 0, 2).reshape(C, E1 * HD1)
    r["b_d1"] = g["L1_ffn_bd1"].reshape(2, P).T
    wd2 = np.zeros((P, E1, C), np.float32)
    for e in range(E1):
        wd2[(e % 4) * HD1:(e % 4 + 1) * HD1, e] = g["L1_ffn_Wd2"][e]
    r["w_d2"] = wd2
    r["b_d2"] = g["L1_ffn_bd2"].T
    r["w_ad"] = g["L1_ffn_Wa_down"].transpose(1, 2, 0)
    r["b_ad"] = g["L1_ffn_ba_down"].T
    au = np.zeros((P, C, E1), np.float32)
    au[:R] = g["L1_ffn_Wa_up"].transpose(1, 2, 0)
    au[R] = g["L1_ffn_ba_up"].T
    au[R + 1] = g["L1_ffn_b_base"][:, None]
    r["w_au"] = au
    return r


def kernel(**inputs):
    import concourse.bacc as bacc
    from concourse.bass_utils import run_bass_kernel_spmd

    arrays = {**lay_out(inputs), **shape_constants()}
    arrays = {"in_" + k: np.ascontiguousarray(v) for k, v in arrays.items()}
    nc = bacc.Bacc("TRN2", target_bir_lowering=False, num_devices=1)
    aps = {k[3:]: nc.dram_tensor(k, v.shape, mybir.dt.from_np(v.dtype), kind="ExternalInput").ap() for k, v in arrays.items()}
    out = nc.dram_tensor("x_out", (NB, T, C), F32, kind="ExternalOutput").ap()
    build(nc, aps, out)
    r = run_bass_kernel_spmd(nc, [arrays], core_ids=[0])
    return r.results[0]["x_out"]
```
